# Optimizing a Trainium2 kernel written in Bass

```python
import numpy as np
import jax
import jax.numpy as jnp

def _softmax(x, axis=-1):
    return jax.nn.softmax(x, axis=axis)

def _gelu(x):
    return jax.nn.gelu(x, approximate=True)

def _silu(x):
    return jax.nn.silu(x)

def _sigmoid(x):
    return jax.nn.sigmoid(x)

def _layernorm(x, axis=-1, eps=1e-05):
    m = jnp.mean(x, axis=axis, keepdims=True)
    v = jnp.var(x, axis=axis, keepdims=True)
    return (x - m) / jnp.sqrt(v + eps)

def _scatter_add(tgt, idx, src, axis=0):
    return tgt.at[idx].add(src)

def _segment_sum(src, seg, n):
    return jax.ops.segment_sum(src, seg, n)
kernel_name = 'mk_gps_d2_gnn_r16_a26f34'

def setup_inputs(seed: int=0):
    np.random.seed(seed)
    _w = jnp.asarray

    def _rec_inputs():
        import jax
        import jax.numpy as jnp
        _gk = jax.random.key(seed)
        x = -0.0003713 + 1 * jax.random.normal(jax.random.fold_in(_gk, 1), (3125, 256), jnp.float32)
        src = jax.random.randint(jax.random.fold_in(_gk, 2), (100000,), 0, 3125, jnp.int32)
        dst = jax.random.randint(jax.random.fold_in(_gk, 3), (100000,), 0, 3125, jnp.int32)
        _o = jnp.argsort(dst, stable=True)
        src = src[_o]
        dst = dst[_o]
        edge_weight = jax.random.uniform(jax.random.fold_in(_gk, 12), (100000,), jnp.float32, 0.0, 0.999999)
        return (x, src, dst, edge_weight)
    x, src, dst, edge_weight = _rec_inputs()

    def _L0_gnn_setup():
        import jax, jax.numpy as jnp
        import numpy as np
        N_NODES = 3125
        N_EDGES = 50000
        D_IN = 256
        D_OUT = 256
        key = jax.random.key(seed)
        ks = jax.random.split(key, 7)
        stdv = 1.0 / np.sqrt(D_OUT)
        x = jax.random.normal(ks[0], (N_NODES, D_IN), dtype=jnp.float32)
        edge_src = jax.random.randint(ks[1], (N_EDGES,), 0, N_NODES, dtype=jnp.int32)
        edge_dst = jax.random.randint(ks[2], (N_EDGES,), 0, N_NODES, dtype=jnp.int32)
        edge_weight = jax.random.uniform(ks[3], (N_EDGES,), dtype=jnp.float32)
        W_self = jax.random.uniform(ks[4], (D_IN, D_OUT), minval=-stdv, maxval=stdv, dtype=jnp.float32)
        W_neighbor = jax.random.uniform(ks[5], (D_IN, D_OUT), minval=-stdv, maxval=stdv, dtype=jnp.float32)
        bias = jax.random.uniform(ks[6], (D_OUT,), minval=-stdv, maxval=stdv, dtype=jnp.float32)
        return {'x': x, 'edge_src': edge_src, 'edge_dst': edge_dst, 'edge_weight': edge_weight, 'W_self': W_self, 'W_neighbor': W_neighbor, 'bias': bias}
    _L0_gnn_all = _L0_gnn_setup()
    _L0_gnn_in = {k: v for k, v in _L0_gnn_all.items() if k in ('W_self', 'W_neighbor', 'bias')}
    del _L0_gnn_all

    def _L0_mix_setup():
        import math
        import jax, jax.numpy as jnp
        import numpy as np
        EPS_DIV = 1e-07
        EPS_NORM = 1e-12

        def _l2_normalize(x, axis):
            n = jnp.sqrt(jnp.sum(x * x, axis=axis, keepdims=True))
            return x / jnp.maximum(n, EPS_NORM)
        key = jax.random.key(seed)
        ks = jax.random.split(key, 5)
        b, N, C = (8, 256, 256)
        x = jax.random.normal(ks[0], (b, N, C), dtype=jnp.float32)
        W_qkv = jax.random.normal(ks[1], (C, 3 * C), dtype=jnp.float32) * (1.0 / math.sqrt(C))
        b_qkv = jax.random.normal(ks[2], (3 * C,), dtype=jnp.float32) * 0.02
        W_out = jax.random.normal(ks[3], (C, C), dtype=jnp.float32) * (1.0 / math.sqrt(C))
        b_out = jax.random.normal(ks[4], (C,), dtype=jnp.float32) * 0.02
        return {'x': x, 'W_qkv': W_qkv, 'b_qkv': b_qkv, 'W_out': W_out, 'b_out': b_out}
    _L0_mix_all = _L0_mix_setup()
    _L0_mix_in = {k: v for k, v in _L0_mix_all.items() if k in ('W_qkv', 'b_qkv', 'W_out', 'b_out')}
    del _L0_mix_all

    def _L0_ffn_setup():
        import jax, jax.numpy as jnp
        import numpy as np
        C = 256
        HID = 1024
        E = 8
        TEMP = 1.0
        key = jax.random.key(seed)
        ks = jax.random.split(key, 7)
        x = jax.random.normal(ks[0], (8, 1024, C), dtype=jnp.float32)
        W1 = jax.random.normal(ks[1], (C, HID), dtype=jnp.float32) * 0.02
        b1 = jnp.zeros((HID,), dtype=jnp.float32)
        Wg = jax.random.normal(ks[2], (HID, E), dtype=jnp.float32) * 0.02
        bg = jnp.zeros((E,), dtype=jnp.float32)
        Wd = jax.random.normal(ks[3], (E, HID, C), dtype=jnp.float32) * 0.02
        bd = jnp.zeros((E, C), dtype=jnp.float32)
        return {'x': x, 'W1': W1, 'b1': b1, 'Wg': Wg, 'bg': bg, 'Wd': Wd, 'bd': bd}
    _L0_ffn_all = _L0_ffn_setup()
    _L0_ffn_in = {k: v for k, v in _L0_ffn_all.items() if k in ('W1', 'b1', 'Wg', 'bg', 'Wd', 'bd')}
    del _L0_ffn_all

    def _L1_gnn_setup():
        import jax, jax.numpy as jnp
        import numpy as np
        N_NODES = 6250
        N_EDGES = 100000
        IN_DIM = 256
        HID_DIM = 256
        key = jax.random.key(seed)
        k1, k2, k3, k4 = jax.random.split(key, 4)
        h = jax.random.normal(k1, (N_NODES, IN_DIM), dtype=jnp.float32)
        weight = jax.random.normal(k2, (IN_DIM, HID_DIM), dtype=jnp.float32) * (1.0 / np.sqrt(IN_DIM))
        bias = jnp.zeros((HID_DIM,), dtype=jnp.float32)
        src = jax.random.randint(k3, (N_EDGES,), 0, N_NODES, dtype=jnp.int32)
        dst = jax.random.randint(k4, (N_EDGES,), 0, N_NODES, dtype=jnp.int32)
        return {'h': h, 'weight': weight, 'bias': bias, 'src': src, 'dst': dst}
    _L1_gnn_all = _L1_gnn_setup()
    _L1_gnn_in = {k: v for k, v in _L1_gnn_all.items() if k in ('weight', 'bias')}
    del _L1_gnn_all

    def _L1_mix_setup():
        import jax, jax.numpy as jnp
        import numpy as np
        D_MODEL = 256
        NHEAD = 8
        D_HEAD = D_MODEL // NHEAD
        DIM_FF = 1024
        B, L = (4, 1024)
        LN_EPS = 1e-05

        def _layernorm(x, g, b):
            mu = jnp.mean(x, axis=-1, keepdims=True)
            var = jnp.mean((x - mu) ** 2, axis=-1, keepdims=True)
            return (x - mu) * jax.lax.rsqrt(var + LN_EPS) * g + b

        def _phi(x):
            return jnp.where(x > 0, x + 1.0, jnp.exp(x))
        key = jax.random.key(seed)
        ks = jax.random.split(key, 16)
        s_in = 1.0 / np.sqrt(D_MODEL)
        s_ff = 1.0 / np.sqrt(DIM_FF)
        inp = {'x': jax.random.normal(ks[0], (B, L, D_MODEL), dtype=jnp.float32), 'Wq': jax.random.normal(ks[1], (D_MODEL, D_MODEL), dtype=jnp.float32) * s_in, 'bq': jnp.zeros((D_MODEL,), jnp.float32), 'Wk': jax.random.normal(ks[2], (D_MODEL, D_MODEL), dtype=jnp.float32) * s_in, 'bk': jnp.zeros((D_MODEL,), jnp.float32), 'Wv': jax.random.normal(ks[3], (D_MODEL, D_MODEL), dtype=jnp.float32) * s_in, 'bv': jnp.zeros((D_MODEL,), jnp.float32), 'Wo': jax.random.normal(ks[4], (D_MODEL, D_MODEL), dtype=jnp.float32) * s_in, 'bo': jnp.zeros((D_MODEL,), jnp.float32), 'W1': jax.random.normal(ks[5], (D_MODEL, DIM_FF), dtype=jnp.float32) * s_in, 'b1': jnp.zeros((DIM_FF,), jnp.float32), 'W2': jax.random.normal(ks[6], (DIM_FF, D_MODEL), dtype=jnp.float32) * s_ff, 'b2': jnp.zeros((D_MODEL,), jnp.float32), 'ln1_g': jnp.ones((D_MODEL,), jnp.float32), 'ln1_b': jnp.zeros((D_MODEL,), jnp.float32), 'ln2_g': jnp.ones((D_MODEL,), jnp.float32), 'ln2_b': jnp.zeros((D_MODEL,), jnp.float32)}
        return inp
    _L1_mix_all = _L1_mix_setup()
    _L1_mix_in = {k: v for k, v in _L1_mix_all.items() if k in ('Wq', 'bq', 'Wk', 'bk', 'Wv', 'bv', 'Wo', 'bo', 'W1', 'b1', 'W2', 'b2', 'ln1_g', 'ln1_b', 'ln2_g', 'ln2_b')}
    del _L1_mix_all

    def _L1_ffn_setup():
        import jax, jax.numpy as jnp
        import numpy as np
        B, S, D, E, H, K = (4, 256, 256, 8, 512, 2)
        key = jax.random.key(seed)
        ks = jax.random.split(key, 6)
        x = jax.random.normal(ks[0], (B, S, D), jnp.float32)
        Wg = jax.random.normal(ks[1], (D, E), jnp.float32) * 0.02
        bg = jnp.zeros((E,), jnp.float32)
        W1 = jax.random.normal(ks[2], (E, D, H), jnp.float32) * 0.02
        b1 = jnp.zeros((E, H), jnp.float32)
        W2 = jax.random.normal(ks[3], (E, H, D), jnp.float32) * 0.02
        b2 = jnp.zeros((E, D), jnp.float32)
        return {'x': x, 'Wg': Wg, 'bg': bg, 'W1': W1, 'b1': b1, 'W2': W2, 'b2': b2}
    _L1_ffn_all = _L1_ffn_setup()
    _L1_ffn_in = {k: v for k, v in _L1_ffn_all.items() if k in ('Wg', 'bg', 'W1', 'b1', 'W2', 'b2')}
    del _L1_ffn_all
    return {'x': x, 'src': src, 'dst': dst, 'edge_weight': edge_weight, 'L0_gnn_W_self': _L0_gnn_in['W_self'], 'L0_gnn_W_neighbor': _L0_gnn_in['W_neighbor'], 'L0_gnn_bias': _L0_gnn_in['bias'], 'L0_mix_W_qkv': _L0_mix_in['W_qkv'], 'L0_mix_b_qkv': _L0_mix_in['b_qkv'], 'L0_mix_W_out': _L0_mix_in['W_out'], 'L0_mix_b_out': _L0_mix_in['b_out'], 'L0_ffn_W1': _L0_ffn_in['W1'], 'L0_ffn_b1': _L0_ffn_in['b1'], 'L0_ffn_Wg': _L0_ffn_in['Wg'], 'L0_ffn_bg': _L0_ffn_in['bg'], 'L0_ffn_Wd': _L0_ffn_in['Wd'], 'L0_ffn_bd': _L0_ffn_in['bd'], 'L1_gnn_weight': _L1_gnn_in['weight'], 'L1_gnn_bias': _L1_gnn_in['bias'], 'L1_mix_Wq': _L1_mix_in['Wq'], 'L1_mix_bq': _L1_mix_in['bq'], 'L1_mix_Wk': _L1_mix_in['Wk'], 'L1_mix_bk': _L1_mix_in['bk'], 'L1_mix_Wv': _L1_mix_in['Wv'], 'L1_mix_bv': _L1_mix_in['bv'], 'L1_mix_Wo': _L1_mix_in['Wo'], 'L1_mix_bo': _L1_mix_in['bo'], 'L1_mix_W1': _L1_mix_in['W1'], 'L1_mix_b1': _L1_mix_in['b1'], 'L1_mix_W2': _L1_mix_in['W2'], 'L1_mix_b2': _L1_mix_in['b2'], 'L1_mix_ln1_g': _L1_mix_in['ln1_g'], 'L1_mix_ln1_b': _L1_mix_in['ln1_b'], 'L1_mix_ln2_g': _L1_mix_in['ln2_g'], 'L1_mix_ln2_b': _L1_mix_in['ln2_b'], 'L1_ffn_Wg': _L1_ffn_in['Wg'], 'L1_ffn_bg': _L1_ffn_in['bg'], 'L1_ffn_W1': _L1_ffn_in['W1'], 'L1_ffn_b1': _L1_ffn_in['b1'], 'L1_ffn_W2': _L1_ffn_in['W2'], 'L1_ffn_b2': _L1_ffn_in['b2']}

def reference(x, src, dst, edge_weight, L0_gnn_W_self, L0_gnn_W_neighbor, L0_gnn_bias, L0_mix_W_qkv, L0_mix_b_qkv, L0_mix_W_out, L0_mix_b_out, L0_ffn_W1, L0_ffn_b1, L0_ffn_Wg, L0_ffn_bg, L0_ffn_Wd, L0_ffn_bd, L1_gnn_weight, L1_gnn_bias, L1_mix_Wq, L1_mix_bq, L1_mix_Wk, L1_mix_bk, L1_mix_Wv, L1_mix_bv, L1_mix_Wo, L1_mix_bo, L1_mix_W1, L1_mix_b1, L1_mix_W2, L1_mix_b2, L1_mix_ln1_g, L1_mix_ln1_b, L1_mix_ln2_g, L1_mix_ln2_b, L1_ffn_Wg, L1_ffn_bg, L1_ffn_W1, L1_ffn_b1, L1_ffn_W2, L1_ffn_b2):
    import jax
    import jax.numpy as jnp

    def _L0_gnn_ref(x, edge_src, edge_dst, edge_weight, W_self, W_neighbor, bias):
        import jax, jax.numpy as jnp
        import numpy as np
        N_NODES = 3125
        N_EDGES = 50000
        D_IN = 256
        D_OUT = 256
        act_self = x @ W_self
        support = x @ W_neighbor
        gathered = support[edge_src] * edge_weight[:, None]
        act_neighbor = jax.ops.segment_sum(gathered, edge_dst, num_segments=N_NODES)
        return act_self + act_neighbor + bias

    def _L0_mix_ref(x, W_qkv, b_qkv, W_out, b_out):
        import math
        import jax, jax.numpy as jnp
        import numpy as np
        EPS_DIV = 1e-07
        EPS_NORM = 1e-12

        def _l2_normalize(x, axis):
            n = jnp.sqrt(jnp.sum(x * x, axis=axis, keepdims=True))
            return x / jnp.maximum(n, EPS_NORM)
        b, N, C = x.shape
        qkv = x @ W_qkv + b_qkv
        q, k, v = jnp.split(qkv, 3, axis=2)
        q = q - jnp.mean(q, axis=2, keepdims=True)
        k = k - jnp.mean(k, axis=2, keepdims=True)
        q2 = q * q
        k2 = k * k
        q2s = jnp.sum(q2, axis=2, keepdims=True)
        k2s = jnp.sum(k2, axis=2, keepdims=True)
        k2 = _l2_normalize(k2 / (k2s + EPS_DIV), axis=-2)
        q2 = _l2_normalize(q2 / (q2s + EPS_DIV), axis=-1)
        kv = jnp.einsum('bnc,bnd->bcd', k2, v)
        t2 = jnp.einsum('bnc,bcd->bnd', q2, kv) / math.sqrt(N)
        attn = v + t2
        return attn @ W_out + b_out

    def _L0_ffn_ref(x, W1, b1, Wg, bg, Wd, bd):
        import jax, jax.numpy as jnp
        import numpy as np
        C = 256
        HID = 1024
        E = 8
        TEMP = 1.0
        orig_shape = x.shape
        xf = x.reshape(-1, orig_shape[-1])
        H = jax.nn.gelu(xf @ W1 + b1, approximate=False)
        probs = jax.nn.softmax((H @ Wg + bg) / TEMP, axis=-1)
        assign = jnp.argmax(probs, axis=-1)
        out = jnp.zeros_like(xf)
        for e in range(Wd.shape[0]):
            y = H @ Wd[e] + bd[e]
            sel = (assign == e)[:, None]
            out = out + jnp.where(sel, probs[:, e:e + 1] * y, 0.0)
        return out.reshape(orig_shape)

    def _L1_gnn_ref(h, weight, bias, src, dst):
        import jax, jax.numpy as jnp
        import numpy as np
        N_NODES = 6250
        N_EDGES = 100000
        IN_DIM = 256
        HID_DIM = 256
        n = h.shape[0]
        ones = jnp.ones_like(src, dtype=h.dtype)
        out_deg = jax.ops.segment_sum(ones, src, num_segments=n)
        in_deg = jax.ops.segment_sum(ones, dst, num_segments=n)
        norm_src = jax.lax.rsqrt(jnp.clip(out_deg, 1.0))
        norm_dst = jax.lax.rsqrt(jnp.clip(in_deg, 1.0))
        h_src = h * norm_src[:, None]
        msg = h_src[src]
        agg = jax.ops.segment_sum(msg, dst, num_segments=n)
        agg = agg * norm_dst[:, None]
        out = agg @ weight + bias
        return jax.nn.elu(out)

    def _L1_mix_ref(x, Wq, bq, Wk, bk, Wv, bv, Wo, bo, W1, b1, W2, b2, ln1_g, ln1_b, ln2_g, ln2_b):
        import jax, jax.numpy as jnp
        import numpy as np
        D_MODEL = 256
        NHEAD = 8
        D_HEAD = D_MODEL // NHEAD
        DIM_FF = 1024
        B, L = (4, 1024)
        LN_EPS = 1e-05

        def _layernorm(x, g, b):
            mu = jnp.mean(x, axis=-1, keepdims=True)
            var = jnp.mean((x - mu) ** 2, axis=-1, keepdims=True)
            return (x - mu) * jax.lax.rsqrt(var + LN_EPS) * g + b

        def _phi(x):
            return jnp.where(x > 0, x + 1.0, jnp.exp(x))
        Bq, Lq, _ = x.shape
        q = (x @ Wq + bq).reshape(Bq, Lq, NHEAD, D_HEAD)
        k = (x @ Wk + bk).reshape(Bq, Lq, NHEAD, D_HEAD)
        v = (x @ Wv + bv).reshape(Bq, Lq, NHEAD, D_HEAD)
        q_phi = _phi(q)
        k_phi = _phi(k)
        kv = jnp.einsum('blhd,blhe->bhde', k_phi, v)
        k_sum = k_phi.sum(axis=1)
        z = 1.0 / (jnp.einsum('blhd,bhd->blh', q_phi, k_sum) + 1e-06)
        out = jnp.einsum('blhd,bhde,blh->blhe', q_phi, kv, z)
        out = out.reshape(Bq, Lq, D_MODEL) @ Wo + bo
        x = _layernorm(x + out, ln1_g, ln1_b)
        ff = jax.nn.relu(x @ W1 + b1) @ W2 + b2
        x = _layernorm(x + ff, ln2_g, ln2_b)
        return x

    def _L1_ffn_ref(x, Wg, bg, W1, b1, W2, b2):
        import jax, jax.numpy as jnp
        import numpy as np
        B, S, D, E, H, K = (4, 256, 256, 8, 512, 2)
        Bv, Sv, Dv = x.shape
        gate_scores = x @ Wg + bg
        _, idx = jax.lax.top_k(gate_scores, K)
        mask = jax.nn.one_hot(idx, E, dtype=x.dtype).sum(axis=-2)
        xf = x.reshape(-1, Dv)
        mf = mask.reshape(-1, E)
        h = jax.nn.gelu(jnp.einsum('td,edh->teh', xf, W1) + b1[None], approximate=False)
        y = jnp.einsum('teh,ehd->ted', h, W2) + b2[None]
        out = jnp.einsum('ted,te->td', y, mf)
        return out.reshape(Bv, Sv, Dv)
    xn = _layernorm(x, axis=-1)
    x = x + _L0_gnn_ref(xn, src, dst, edge_weight, L0_gnn_W_self, L0_gnn_W_neighbor, L0_gnn_bias) + _L0_mix_ref(xn[None], L0_mix_W_qkv, L0_mix_b_qkv, L0_mix_W_out, L0_mix_b_out)[0]
    x = x + _L0_ffn_ref(_layernorm(x, axis=-1)[None], L0_ffn_W1, L0_ffn_b1, L0_ffn_Wg, L0_ffn_bg, L0_ffn_Wd, L0_ffn_bd)[0]
    xn = _layernorm(x, axis=-1)
    x = x + _L1_gnn_ref(xn, L1_gnn_weight, L1_gnn_bias, src, dst) + _L1_mix_ref(xn[None], L1_mix_Wq, L1_mix_bq, L1_mix_Wk, L1_mix_bk, L1_mix_Wv, L1_mix_bv, L1_mix_Wo, L1_mix_bo, L1_mix_W1, L1_mix_b1, L1_mix_W2, L1_mix_b2, L1_mix_ln1_g, L1_mix_ln1_b, L1_mix_ln2_g, L1_mix_ln2_b)[0]
    x = x + _L1_ffn_ref(_layernorm(x, axis=-1)[None], L1_ffn_Wg, L1_ffn_bg, L1_ffn_W1, L1_ffn_b1, L1_ffn_W2, L1_ffn_b2)[0]
    return x

_drawn_inputs = setup_inputs


def setup_inputs(seed=0):
    import zlib

    import numpy as np

    out = dict(_drawn_inputs(seed))
    spreads = {'L0_ffn_b1': (0.0, 0.8),
     'L0_ffn_bg': (0.0, 0.8),
     'L0_ffn_bd': (0.0, 0.8),
     'L1_gnn_bias': (0.0, 0.462),
     'L1_mix_bq': (0.0, 2.0),
     'L1_mix_bk': (0.0, 2.0),
     'L1_mix_bv': (0.0, 0.445),
     'L1_mix_bo': (0.0, 0.497),
     'L1_mix_b1': (0.0, 0.425),
     'L1_mix_b2': (0.0, 0.291),
     'L1_mix_ln1_g': (1.0, 0.2),
     'L1_mix_ln1_b': (0.0, 0.416),
     'L1_mix_ln2_g': (1.0, 0.2),
     'L1_mix_ln2_b': (0.0, 0.453),
     'L1_ffn_bg': (0.0, 0.1),
     'L1_ffn_b1': (0.0, 0.727),
     'L1_ffn_b2': (0.0, 0.347)}
    factors = {'L0_gnn_bias': 3.243,
     'L0_mix_b_out': 5.765,
     'L0_ffn_W1': 5.614,
     'L0_ffn_Wg': 6.128,
     'L0_ffn_Wd': 6.817,
     'L1_mix_Wq': 64.0,
     'L1_mix_Wk': 61.1}
    for name, (base, spread) in spreads.items():
        noise = np.random.default_rng([zlib.crc32(name.encode()), seed]).standard_normal(out[name].shape)
        drawn = base * np.exp(spread * noise) if base else spread * noise
        out[name] = jnp.asarray(drawn.astype(out[name].dtype))
    for name, factor in factors.items():
        out[name] = (out[name] * factor).astype(out[name].dtype)
    return out
```

```python
import math
from contextlib import ExitStack

import concourse.bass as bass
from concourse import mybir

F32 = mybir.dt.float32
BF16 = mybir.dt.bfloat16
I32 = mybir.dt.int32
ALU = mybir.AluOpType
ACT = mybir.ActivationFunctionType
AX = mybir.AxisListType

N, E, D = 3125, 100000, 256
B = 125
NB = N // B
NT = E // B
KC = D // 128
GS, GR = 6, 6
CH = GS * GR
NTP = NT + CH
MAXCH = -(-NT // CH)
TR, TC = 100, NT // 100
H0, E0 = 1024, 8
H1, E1 = 512, 8
J0, J1 = H0 // 128, H1 // 128
FF = 1024
JF = FF // 128
HEADS, DH = 8, 32
LN_EPS = 1e-5
ds = bass.ds


def take(eng, sem, n=1):
    eng.wait_ge(sem, n)
    eng.sem_clear(sem)


class Chain:

    def __init__(self, eng, sem):
        self.eng, self.sem, self.n = eng, sem, 0

    def __call__(self, ins):
        ins.then_inc(self.sem, 1)
        self.n += 1
        self.eng.wait_ge(self.sem, self.n)

    def restart(self):
        if self.n:
            self.eng.sem_clear(self.sem)
        self.n = 0


def program(nc, a, out, dbg=None):
    ctx = ExitStack()
    with ctx:
        def sb(name, shape, dt=F32):
            return ctx.enter_context(nc.sbuf_tensor(name, shape, dt))

        def sem(name):
            return ctx.enter_context(nc.semaphore(name))

        banks = [ctx.enter_context(nc.psum_tensor(f"bank{i}", [128, 512], F32)) for i in range(8)]
        ps_agg, ps_t, ps_o, ps_h0, ps_h1, ps_y0, ps_y1, ps_kv = banks
        ps_h, ps_y = [ps_h0, ps_h1], [ps_y0, ps_y1]

        feat0 = nc.dram_tensor("feat0", (N, D), F32).ap()
        feat1 = nc.dram_tensor("feat1", (N, D), F32).ap()
        rows_a = nc.dram_tensor("rows_a", (N, 2 * D), F32).ap()
        rows_b = nc.dram_tensor("rows_b", (N, 3 * D), F32).ap()
        tile_min = nc.dram_tensor("tile_min", (TR, TC), F32).ap()
        tile_max = nc.dram_tensor("tile_max", (TR, TC), F32).ap()
        block_lo = nc.dram_tensor("block_lo", (NB, 1), I32).ap()
        block_n = nc.dram_tensor("block_n", (NB, 1), I32).ap()

        ident = sb("ident", [128, 128])
        iota = sb("iota", [B, B])
        base = sb("base", [B, NB])
        base_col = sb("base_col", [NB, 1])
        ones = sb("ones", [128, B])
        zero_w = sb("zero_w", [1, 128], BF16)
        zero_r = sb("zero_r", [1, 512], BF16)

        dst_f = sb("dst_f", [B, NTP])
        w_f = sb("w_f", [B, NTP])
        src_i = sb("src_i", [B, NTP], I32)
        lo_tab = sb("lo_tab", [1, NB], I32)
        n_tab = sb("n_tab", [1, NB], I32)
        cum_tab = sb("cum_tab", [1, NB + 1], I32)
        cum_f = sb("cum_f", [1, NB + 1])
        n_f = sb("n_f", [1, NB])
        idx_cur = sb("idx_cur", [B, CH], I32)
        dst_cur = sb("dst_cur", [B, CH])
        w_cur = sb("w_cur", [B, CH])
        xg = sb("xg", [B, CH, D + 1])
        oh = sb("oh", [B, CH, B])
        inv_out = sb("inv_out", [B, NB])

        moe = sb("moe", [128, J0 * E0 * D])
        x_big = moe[0:B, 0:NB * D].rearrange("p (b d) -> p b d", b=NB)
        xn_big = moe[0:B, NB * D:2 * NB * D].rearrange("p (b d) -> p b d", b=NB)
        wd_sb = moe[:, :].rearrange("p (j e d) -> p j e d", j=J0, e=E0)
        w1e_sb = moe[:, 0:E1 * KC * H1].rearrange("p (e c h) -> p e c h", e=E1, c=KC)
        w2e_sb = moe[:, E1 * KC * H1:].rearrange("p (e j d) -> p e j d", e=E1, j=J1)
        w_h = sb("w_h", [128, KC, H0])
        w_x = sb("w_x", [128, 8 * D])
        wqkvs = w_x[:, :].rearrange("p (c n) -> p c n", c=KC)
        w2m = w_x[:, :].rearrange("p (j n) -> p j n", j=JF)
        wqkv1 = sb("wqkv1", [128, KC, 3 * D])
        wn = sb("wn", [128, KC, D])
        wo = sb("wo", [128, KC, D])
        kvo = sb("kvo", [128, KC, D])
        kvd = sb("kvd", [128, KC, 132])
        wg = sb("wg", [128, J0, E0])
        bd_sb = sb("bd_sb", [E0, D])
        b1_col = sb("b1_col", [128, J0])
        b1e_col = sb("b1e_col", [128, E1, J1])
        bias0 = sb("bias0", [B, 4 * D])
        bias1 = sb("bias1", [B, 3 * D])
        bc = sb("bc", [B, 7, D])
        bg_bc = sb("bg_bc", [B, E0])
        b_tmp = sb("b_tmp", [B, D])

        row_a = sb("row_a", [B, 2 * D])
        row_b = sb("row_b", [B, 3 * D])
        agg_s = sb("agg_s", [B, D])
        t4 = sb("t4", [128, 4, B])
        t2 = sb("t2", [128, 2, B])
        x1 = sb("x1", [B, D])
        y = sb("y", [B, D])
        acc = sb("acc", [B, D])
        ht = sb("ht", [128, 8, B])
        qk = sb("qk", [B, 2 * D])
        ek = sb("ek", [B, 2 * D])
        v1 = sb("v1", [B, 2, 129])
        f_out = sb("f_out", [B, D])
        st = sb("st", [B, 16])
        bn6 = sb("bn6", [B, 6])
        mv = sb("mv", [B, 2])
        sd = sb("sd", [B, 2])
        rs = sb("rs", [B, 1])
        lg = sb("lg", [B, 8])
        lt = sb("lt", [B, 8])
        lu = sb("lu", [B, 8])
        gate = sb("gate", [B, 8])
        gt = sb("gt", [8, B])
        mv_all = sb("mv_all", [B, NB, 2])
        rs_all = sb("rs_all", [B, NB])

        st_min, st_max = sb("st_min", [TR, TC]), sb("st_max", [TR, TC])
        blk, blk_i = sb("blk", [NB, 3]), sb("blk_i", [NB, 2], I32)
        st4 = sb("st4", [128, KC, 2])[:, :, :]
        st2 = sb("st2", [128, 2])
        kvf = sb("kvf", [128, 2 * D])
        t4f = ht[:, :, :].rearrange("p a b -> p (a b)")[:, 0:2 * D]

        e_i32 = [xg[0:TR, 4 * i:4 * i + 4, :].rearrange("p a b -> p (a b)")[:, 0:TC * B].bitcast(I32)
                 for i in range(2)]
        e_f32 = [xg[0:TR, 8 + 4 * i:12 + 4 * i, :].rearrange("p a b -> p (a b)")[:, 0:TC * B]
                 for i in range(3)]
        src_f = xg[:, 20:24, :].rearrange("p a b -> p (a b)")[:, 0:NT]
        src_hi = xg[:, 24:28, :].rearrange("p a b -> p (a b)")[:, 0:NT]
        src_lo = xg[:, 28:32, :].rearrange("p a b -> p (a b)")[:, 0:NT]
        HT_ = 20
        oh_lo = [oh[:, :, :].rearrange("p a b -> p (a b)")[:, 2000 * i:2000 * i + HT_ * B // 2].bitcast(BF16)
                 .rearrange("p (t l) -> p t l", t=HT_) for i in range(2)]
        oh_hi = [oh[:, :, :].rearrange("p a b -> p (a b)")[:, 2000 * i + 1250:2000 * i + 1250 + HT_ * NB // 2]
                 .bitcast(BF16).rearrange("p (t l) -> p t l", t=HT_) for i in range(2)]
        range_t = xg[0:NB, 0:16, :].rearrange("p a b -> p (a b)")
        t_min, t_max, t_msk, t_val, t_iot = (range_t[:, NT * i:NT * i + NT] for i in range(5))

        l_x, l_edge, l_w0, l_wh, l_bias0, l_wn, l_ffn0, l_moe0, l_l1, l_c = (
            sem(n) for n in ("x_loaded", "edges_loaded", "w_mix0_loaded", "w_hid0_loaded", "bias0_loaded",
                             "w_nbr_loaded", "ffn0_loaded", "experts0_loaded", "w_layer1_loaded", "w_c_loaded"))
        l_moe1 = sem("experts1_loaded")
        const_full, edge_f_full, edge_t_full, minmax_full, minmax_stored, minmax_loaded = (
            sem(n) for n in ("consts_made", "edges_as_float", "edges_turned", "tile_range_made",
                             "tile_range_stored", "tile_range_loaded"))
        cum_full = sem("chunk_sums_made")
        iota_full, blk_full, blk_stored, blk_loaded, tabs_full = (
            sem(n) for n in ("tile_iota_made", "block_range_made", "block_range_stored",
                             "block_range_loaded", "edge_tables_made"))
        tile_iota, dbg_stored = sem("tile_numbers_made"), sem("dbg_stored")
        edge_ps_full, edge_ps_free = sem("edge_turn_full"), sem("edge_turn_free")
        var_full, std_full = sem("variance_full"), sem("deviation_full")
        feat0_full, feat0_stored = sem("feat0_made"), sem("feat0_stored")
        deg_full = [sem(f"degree_onehot_full{i}") for i in range(2)]
        deg_free = [sem(f"degree_onehot_free{i}") for i in range(2)]
        deg_ps_full = sem("degree_counted")
        xg_clear = sem("gather_buffer_clear")
        w_prep, w_prep_ps, w_prep2 = sem("w_prep"), sem("w_prep_ps"), sem("w_prep2")
        xg_full = [sem(f"rows_full{k}") for k in range(GR)]
        xg_free = [sem(f"rows_free{k}") for k in range(GR)]
        oh_full, oh_free, idx_full = sem("onehot_full"), sem("onehot_free"), sem("indices_full")
        agg_full, agg_free = sem("agg_full"), sem("agg_free")
        ps_full = sem("ps_stage_full")
        ps_t_full = sem("ps_turned_full")
        t_full = sem("turned_full")
        v_full = sem("vector_stage_full")
        act_in, act_out = sem("act_in"), sem("act_out")
        xa_full = sem("block_rows_full")
        pa_full, pa_free = sem("proj_qk_full"), sem("proj_qk_free")
        pb_full, pb_free = sem("proj_vs_full"), sem("proj_vs_free")
        k4_full, kn_full, kn_free = sem("key4_full"), sem("key_full"), sem("key_free")
        h_full = [sem(f"hidden_ps_full{i}") for i in range(2)]
        h_free = [sem(f"hidden_ps_free{i}") for i in range(2)]
        ht_full = [sem(f"hidden_full{i}") for i in range(2)]
        ht_free = [sem(f"hidden_free{i}") for i in range(2)]
        y_full = [sem(f"expert_full{i}") for i in range(2)]
        y_free = [sem(f"expert_free{i}") for i in range(2)]
        rowa_full, rowa_free, rowa_in = sem("row_a_full"), sem("row_a_stored"), sem("row_a_loaded")
        rowa_used = sem("row_a_used")
        rowb_full, rowb_free, rowb_in = sem("row_b_full"), sem("row_b_stored"), sem("row_b_loaded")
        rowb_used = sem("row_b_used")
        fout_full, fout_free = sem("f_out_full"), sem("f_out_stored")
        loop_a_done, loop_b_done, stored = sem("loop_a_done"), sem("loop_b_done"), sem("loop_a_stored")
        dve_s, act_s = sem("vector_steps"), sem("scalar_steps")

        nb_rows = lambda ap, b: ap[ds(b * B, B), :]

        def wview(w):
            return w.rearrange("(c p) n -> p c n", p=128)

        def row(v, p=B):
            return v.partition_broadcast(p)

        ctx.enter_context(nc.allow_non_contiguous_dma(reason="bias columns and block tables, a few KB"))
        block = ctx.enter_context(nc.Block())

        @block.sync
        def _(sp):
            sp.sem_inc(rowa_free, 16)
            sp.sem_inc(rowb_free, 16)
            sp.sem_inc(fout_free, 16)
            xv = a["x"].rearrange("(b p) d -> p b d", p=B)
            for i in range(5):
                sp.dma_start(x_big[:, 5 * i:5 * i + 5, :], xv[:, 5 * i:5 * i + 5, :]).then_inc(l_x, 16)
            sp.dma_start(wqkvs[:, :, 0:3 * D], wview(a["L0_mix_W_qkv"])).then_inc(l_w0, 16)
            sp.dma_start(wqkvs[:, :, 3 * D:4 * D], wview(a["L0_gnn_W_self"])).then_inc(l_w0, 16)
            sp.dma_start(wo[:, :, :], wview(a["L0_mix_W_out"])).then_inc(l_w0, 16)
            sp.dma_start(b1_col[:, 0:KC], a["L0_mix_b_qkv"][2 * D:3 * D].rearrange("(c p) -> p c", p=128)).then_inc(l_w0, 16)
            sp.dma_start(bias0[:, 0:3 * D], row(a["L0_mix_b_qkv"])).then_inc(l_w0, 16)
            sp.dma_start(bias0[:, 3 * D:], row(a["L0_gnn_bias"])).then_inc(l_w0, 16)
            sp.dma_start(b_tmp[:, :], row(a["L0_mix_b_out"])).then_inc(l_w0, 16)
            fv = feat0.rearrange("(b p) d -> p b d", p=B)
            take(sp, feat0_full)
            for i in range(5):
                sp.dma_start(fv[:, 5 * i:5 * i + 5, :], xn_big[:, 5 * i:5 * i + 5, :]).then_inc(feat0_stored, 16)
            take(sp, minmax_full)
            sp.dma_start(tile_min, st_min[:, :]).then_inc(minmax_stored, 16)
            sp.dma_start(tile_max, st_max[:, :]).then_inc(minmax_stored, 16)
            sp.wait_ge(minmax_stored, 32)
            take(sp, tabs_full)
            sp.dma_start(t_min, tile_min.rearrange("q c -> (q c)").partition_broadcast(NB)).then_inc(minmax_loaded, 16)
            sp.dma_start(t_max, tile_max.rearrange("q c -> (q c)").partition_broadcast(NB)).then_inc(minmax_loaded, 16)
            take(sp, blk_full)
            sp.dma_start(block_lo, blk_i[:, 0:1]).then_inc(blk_stored, 16)
            sp.dma_start(block_n, blk_i[:, 1:2]).then_inc(blk_stored, 16)
            sp.wait_ge(blk_stored, 32)
            sp.dma_start(lo_tab[:, :], block_lo.rearrange("b o -> o b")).then_inc(blk_loaded, 16)
            sp.dma_start(n_tab[:, :], block_n.rearrange("b o -> o b")).then_inc(blk_loaded, 16)
            sp.dma_start(w_h[:, :, :], wview(a["L0_ffn_W1"])).then_inc(l_wh, 16)
            sp.dma_start(wn[:, :, :], wview(a["L0_gnn_W_neighbor"])).then_inc(l_wh, 16)
            sp.dma_start(wg[:, :, :], a["L0_ffn_Wg"].rearrange("(j p) e -> p j e", p=128)).then_inc(l_wh, 16)
            sp.dma_start(bg_bc[:, :], row(a["L0_ffn_bg"])).then_inc(l_wh, 16)
            sp.dma_start(bd_sb[:, :], a["L0_ffn_bd"]).then_inc(l_wh, 16)
            for i, n in enumerate("qkv"):
                sp.dma_start(wqkv1[:, :, D * i:D * i + D], wview(a["L1_mix_W" + n])).then_inc(l_l1, 16)
                sp.dma_start(bias1[:, D * i:D * i + D], row(a["L1_mix_b" + n])).then_inc(l_l1, 16)
            for i, n in enumerate(("L1_gnn_bias", "L1_mix_bo", "L1_mix_b2", "L1_mix_ln1_g", "L1_mix_ln1_b",
                                   "L1_mix_ln2_g", "L1_mix_ln2_b")):
                sp.dma_start(bc[:, i, :], row(a[n])).then_inc(l_l1, 16)
            sp.dma_start(b1e_col[:, :, :], a["L1_ffn_b1"].rearrange("e (j p) -> p e j", p=128)).then_inc(l_l1, 16)
            with sp.Fori(0, NB) as b:
                take(sp, rowa_full)
                sp.dma_start(nb_rows(rows_a, b), row_a[:, :]).then_inc(rowa_free, 16)
            take(sp, loop_a_done)
            sp.wait_ge(feat0_stored, 80)
            sp.dma_start(b1_col[:, :], a["L0_ffn_b1"].rearrange("(j p) -> p j", p=128)).then_inc(l_moe0, 16)
            for e in range(E0):
                sp.dma_start(wd_sb[:, :, e, :], a["L0_ffn_Wd"][e].rearrange("(j p) d -> p j d", p=128)).then_inc(l_moe0, 16)
            with sp.Fori(0, NB) as b:
                take(sp, rowa_used)
                sp.dma_start(row_a[:, :], nb_rows(rows_a, b)).then_inc(rowa_in, 16)
                take(sp, rowb_full)
                sp.dma_start(nb_rows(rows_b, b), row_b[:, :]).then_inc(rowb_free, 16)
                take(sp, fout_full)
                sp.dma_start(nb_rows(feat1, b), f_out[:, :]).then_inc(fout_free, 16)
            take(sp, loop_b_done)
            sp.sem_inc(fout_free, 16)
            if dbg is not None:
                sp.dma_start(dbg, rows_b).then_inc(dbg_stored, 16)
                sp.wait_ge(dbg_stored, 16)
            sp.dma_start(w_h[:, :, :], wview(a["L1_mix_W1"])).then_inc(l_c, 16)
            sp.dma_start(w2m, a["L1_mix_W2"].rearrange("(j p) n -> p j n", p=128)).then_inc(l_c, 16)
            sp.dma_start(wn[:, :, :], wview(a["L1_gnn_weight"])).then_inc(l_c, 16)
            sp.dma_start(wo[:, :, :], wview(a["L1_mix_Wo"])).then_inc(l_c, 16)
            sp.dma_start(wg[:, 0:KC, :], wview(a["L1_ffn_Wg"])).then_inc(l_c, 16)
            sp.dma_start(bg_bc[:, :], row(a["L1_ffn_bg"])).then_inc(l_c, 16)
            sp.dma_start(bd_sb[:, :], a["L1_ffn_b2"]).then_inc(l_c, 16)
            sp.dma_start(b1_col[:, :], a["L1_mix_b1"].rearrange("(j p) -> p j", p=128)).then_inc(l_c, 16)
            for e in range(E1):
                sp.dma_start(w1e_sb[:, e, :, :], wview(a["L1_ffn_W1"][e])).then_inc(l_moe1, 16)
                sp.dma_start(w2e_sb[:, e, :, :], a["L1_ffn_W2"][e].rearrange("(j p) d -> p j d", p=128)).then_inc(l_moe1, 16)
            with sp.Fori(0, NB) as b:
                take(sp, rowb_used)
                sp.dma_start(row_b[:, :], nb_rows(rows_b, b)).then_inc(rowb_in, 16)
                take(sp, fout_full)
                sp.dma_start(nb_rows(out, b), f_out[:, :]).then_inc(fout_free, 16)
            sp.wait_ge(fout_free, 16)

        @block.gpsimd
        def _(pool):
            chain = Chain(pool, idx_full)
            chain(pool.memset(ident[:, :], 0.0))
            pool.memset(zero_w[:, :], 0.0)
            pool.memset(zero_r[:, :], 0.0)
            pool.memset(ones[:, :], 1.0)
            chain(pool.affine_select(out=ident[:, :], in_=ident[:, :], compare_op=ALU.not_equal, fill=1.0,
                                     base=0, pattern=[[-1, 128]], channel_multiplier=1))
            pool.iota(iota[:, :], [[1, B]], base=0, channel_multiplier=0, allow_small_or_imprecise_dtypes=True)
            pool.iota(base[:, :], [[B, NB]], base=0, channel_multiplier=0, allow_small_or_imprecise_dtypes=True)
            chain(pool.iota(base_col[:, :], [[1, 1]], base=0, channel_multiplier=B, allow_small_or_imprecise_dtypes=True))
            pool.memset(v1[:, :, 128:129], 1.0)
            pool.memset(dst_f[:, NT:], -1.0)
            pool.memset(w_f[:, NT:], 0.0)
            chain(pool.memset(src_i[:, NT:], 0))
            chain.restart()
            pool.sem_inc(const_full, 3)
            for i, n in enumerate(("dst", "src")):
                pool.dma_start(e_i32[i], a[n].rearrange("(q n) -> q n", q=TR)).then_inc(l_edge, 16)
            pool.dma_start(e_f32[2], a["edge_weight"].rearrange("(q n) -> q n", q=TR)).then_inc(l_edge, 16)
            take(pool, iota_full)
            pool.iota(t_iot, [[1, NT]], base=0, channel_multiplier=0,
                      allow_small_or_imprecise_dtypes=True).then_inc(tile_iota, 1)
            take(pool, xg_clear)
            chain(pool.memset(xg[:, :, D:D + 1], 1.0))
            chain.restart()
            pool.wait_ge(feat0_stored, 80)
            pool.wait_ge(blk_loaded, 32)

            def gather(b, feat):
                n = pool.value_load(n_tab[0:1, ds(b, 1)], min_val=1, max_val=MAXCH)
                lo = pool.value_load(lo_tab[0:1, ds(b, 1)], min_val=0, max_val=NT - 1)
                with pool.Fori(0, n) as c:
                    t0 = nc.s_assert_within(pool.snap(lo + c * CH), 0, NT - 1,
                                            skip_runtime_bounds_check_because="a block's chunks start inside its span")
                    for k in range(GR):
                        take(pool, xg_free[k])
                        pool.tensor_copy(idx_cur[:, GS * k:GS * k + GS],
                                         src_i[:, ds(t0 + GS * k, GS)]).then_inc(idx_full, 1)
                        take(pool, idx_full)
                        for s in range(GS * k, GS * k + GS):
                            pool.indirect_dma_start(
                                xg[:, s, 0:D], None, feat,
                                bass.IndirectOffsetOnAxis(ap=idx_cur[:, s:s + 1], axis=0)).then_inc(xg_full[k], 16)

            with pool.Fori(0, NB) as b:
                gather(b, feat0)
            take(pool, stored)
            with pool.Fori(0, NB) as b:
                gather(b, feat1)

        @block.tensor
        def _(pe):
            mm = pe.matmul

            def zero(ps, cols, start, stop):
                return mm(ps[:, 0:cols], zero_w[:, :], zero_r[:, 0:cols], start=start, stop=stop,
                          skip_group_check=True)

            def turn(ps, at, src, n=B):
                return pe.transpose(ps[:, at:at + n], src, ident[0:n, 0:n])

            def turn2(src, at=0):
                for c in range(2):
                    last = turn(ps_t, at + B * c, src[:, 128 * c:128 * c + 128])
                return last

            pe.wait_ge(const_full, 1)
            for k in range(GR):
                pe.sem_inc(xg_free[k], 1)
            pe.sem_inc(oh_free, 1)
            take(pe, edge_f_full)
            for g in range(6):
                if g >= 2:
                    pe.wait_ge(edge_ps_free, g - 1)
                ps = ps_h[g % 2]
                for c in range(4):
                    last = pe.transpose(ps[0:B, TR * c:TR * c + TR],
                                        e_f32[g // 2][:, B * (4 * (g % 2) + c):B * (4 * (g % 2) + c + 1)],
                                        ident[0:TR, 0:TR])
                last.then_inc(edge_ps_full, 1)
            pe.wait_ge(l_w0, 112)
            take(pe, w_prep)
            for r in range(KC):
                for c in range(KC):
                    last = turn(ps_y0, 128 * (KC * r + c), wqkvs[:, r, 2 * D + 128 * c:2 * D + 128 * c + 128], 128)
            last.then_inc(w_prep_ps, 1)
            take(pe, w_prep2)
            for r in range(KC):
                for c in range(KC):
                    mm(ps_y1[:, D * r:D * r + D], t4f[:, 128 * (KC * r + c):128 * (KC * r + c) + 128],
                       wo[:, c, :], start=(c == 0), stop=(c == KC - 1))
            for c in range(KC):
                last = mm(ps_o[0:B, 0:D], ht[:, 5 + c, :], wo[:, c, :], start=(c == 0), stop=(c == KC - 1))
            last.then_inc(w_prep_ps, 1)
            zero(ps_kv, NB, True, False)
            with pe.Fori(0, NT // HT_ // 2) as i:
                for j in range(2):
                    take(pe, deg_full[j])
                    for t in range(HT_):
                        last = mm(ps_kv[0:B, 0:NB], oh_lo[j][:, t, :], oh_hi[j][:, t, :], start=False, stop=False,
                                  skip_group_check=True)
                    last.then_inc(deg_free[j], 1)
            zero(ps_kv, NB, False, True).then_inc(deg_ps_full, 1)
            take(pe, w_prep)

            zero(ps_kv, 512, True, False)
            zero(ps_y1, 2, True, False)
            with pe.Fori(0, NB) as b:
                take(pe, xa_full)
                turn2(y).then_inc(ps_t_full, 1)
                take(pe, t_full)
                take(pe, pa_free)
                for c in range(KC):
                    last = mm(ps_h0[0:B, :], t2[:, c, :], wqkvs[:, c, 0:512], start=(c == 0), stop=(c == 1))
                last.then_inc(pa_full, 1)
                take(pe, pb_free)
                for c in range(KC):
                    last = mm(ps_h1[0:B, :], t2[:, c, :], wqkvs[:, c, 512:1024], start=(c == 0), stop=(c == 1))
                last.then_inc(pb_full, 1)
                take(pe, k4_full)
                take(pe, v_full)
                for c in range(KC):
                    mm(ps_y1[:, c:c + 1], ek[:, D + 128 * c:D + 128 * c + 128], ones[0:B, 0:1], start=False, stop=False,
                       skip_group_check=True)
                for c in range(KC):
                    mm(ps_kv[:, D * c:D * c + D], ek[:, 128 * c:128 * c + 128], agg_s[:, :], start=False,
                       stop=False, skip_group_check=True)
            zero(ps_y1, 2, False, True)
            zero(ps_kv, 512, False, True).then_inc(ps_full, 1)
            take(pe, v_full)
            for r in range(KC):
                for c in range(KC):
                    last = turn(ps_y0, 128 * (KC * r + c), kvf[:, D * r + 128 * c:D * r + 128 * c + 128], 128)
            last.then_inc(ps_full, 1)
            take(pe, v_full)
            for r in range(KC):
                for c in range(KC):
                    last = mm(ps_y1[:, D * r:D * r + D], t4f[:, 128 * (KC * r + c):128 * (KC * r + c) + 128],
                              wo[:, c, :], start=(c == 0), stop=(c == KC - 1))
            last.then_inc(ps_full, 1)
            take(pe, v_full)

            def aggregate(b, cols, before):
                first = pe.value_load(cum_tab[0:1, ds(b, 1)], min_val=0, max_val=MAXCH * NB)
                n = pe.value_load(n_tab[0:1, ds(b, 1)], min_val=1, max_val=MAXCH)
                take(pe, agg_free)
                zero(ps_agg, cols, True, False)
                with pe.Fori(0, n) as c:
                    take(pe, oh_full)
                    landed = pe.snap((before + first + c + 1) * (16 * GS))
                    for k in range(GR):
                        pe.wait_ge(xg_full[k], landed)
                        for s in range(GS * k, GS * k + GS):
                            last = mm(ps_agg[0:B, 0:cols], oh[:, s, :], xg[:, s, 0:cols], start=False, stop=False,
                                      skip_group_check=True)
                        last.then_inc(xg_free[k], 1)
                    zero(ps_agg, cols, False, False).then_inc(oh_free, 1)
                zero(ps_agg, cols, False, True).then_inc(agg_full, 1)

            take(pe, cum_full)
            pe.wait_ge(l_wh, 80)
            pe.wait_ge(l_moe0, 16 * (E0 + 1))
            pe.wait_ge(l_l1, 16 * 14)
            zero(ps_kv, 258, True, False)
            with pe.Fori(0, NB) as b:
                aggregate(b, D, 0)
                take(pe, v_full)
                turn2(agg_s[:, :])
                turn2(row_a[:, D:2 * D], 2 * B).then_inc(ps_t_full, 1)
                take(pe, t_full)
                for c in range(KC):
                    mm(ps_o[0:B, 0:D], t4[:, c, :], wn[:, c, :], start=(c == 0), stop=False)
                for c in range(KC):
                    last = mm(ps_o[0:B, 0:D], t4[:, 2 + c, :], kvo[:, c, :], start=False, stop=(c == 1))
                last.then_inc(ps_full, 1)
                take(pe, v_full)
                turn2(y).then_inc(ps_t_full, 1)
                take(pe, t_full)
                for i in range(2):
                    for j in range(4):
                        for c in range(KC):
                            last = mm(ps_h[i][:, B * j:B * j + B], w_h[:, c, 128 * (4 * i + j):128 * (4 * i + j) + 128],
                                      t2[:, c, :], start=(c == 0), stop=(c == 1))
                    last.then_inc(h_full[i], 1)
                take(pe, ht_full[0])
                take(pe, ht_full[1])
                for j in range(J0):
                    last = mm(ps_t[0:B, 0:E0], ht[:, j, :], wg[:, j, :], start=(j == 0), stop=(j == J0 - 1))
                last.then_inc(ps_full, 1)
                take(pe, v_full)
                pe.transpose(ps_t[0:E0, 0:B], gate[:, :], ident[0:B, 0:B]).then_inc(ps_t_full, 1)
                take(pe, t_full)
                mm(ps_o[0:B, 0:D], gt[:, :], bd_sb[:, :], start=True, stop=True).then_inc(ps_full, 1)
                for q in range(E0 // 2):
                    take(pe, y_free[q % 2])
                    for j in range(J0):
                        last = mm(ps_y[q % 2][0:B, :], ht[:, j, :], wd_sb[:, j, 2 * q:2 * q + 2, :].rearrange("p e d -> p (e d)"),
                                  start=(j == 0), stop=(j == J0 - 1))
                    last.then_inc(y_full[q % 2], 1)
                take(pe, v_full)
                turn2(row_b[:, D:2 * D]).then_inc(ps_t_full, 1)
                take(pe, t_full)
                for c in range(KC):
                    last = mm(ps_h0[0:B, :], t2[:, c, :], wqkv1[:, c, 0:512], start=(c == 0), stop=(c == 1))
                last.then_inc(pa_full, 1)
                for c in range(KC):
                    last = mm(ps_h1[0:B, 0:D], t2[:, c, :], wqkv1[:, c, 512:768], start=(c == 0), stop=(c == 1))
                last.then_inc(pb_full, 1)
                take(pe, v_full)
                for c in range(KC):
                    last = mm(ps_kv[:, 129 * c:129 * c + 129], ek[:, 128 * c:128 * c + 128], v1[:, c, :], start=False,
                              stop=False, skip_group_check=True)
                last.then_inc(kn_free, 1)
            zero(ps_kv, 258, False, True).then_inc(ps_full, 1)
            take(pe, v_full)

            pe.wait_ge(l_c, 128)
            pe.wait_ge(l_moe1, 32 * E1)
            total = pe.value_load(cum_tab[0:1, NB:NB + 1], min_val=NB, max_val=MAXCH * NB)
            with pe.Fori(0, NB) as b:
                aggregate(b, D + 1, total)
                take(pe, v_full)
                turn2(agg_s[:, :])
                turn2(row_b[:, 2 * D:3 * D], 2 * B).then_inc(ps_t_full, 1)
                take(pe, t_full)
                for c in range(KC):
                    mm(ps_o[0:B, 0:D], t4[:, c, :], wn[:, c, :], start=(c == 0), stop=(c == 1))
                for c in range(KC):
                    last = mm(ps_h0[0:B, 132 * c:132 * c + 132], t4[:, 2 + c, :], kvd[:, c, :], start=True, stop=True)
                last.then_inc(ps_full, 1)
                take(pe, v_full)
                turn2(y).then_inc(ps_t_full, 1)
                take(pe, t_full)
                for c in range(KC):
                    last = mm(ps_o[0:B, 0:D], t2[:, c, :], wo[:, c, :], start=(c == 0), stop=(c == 1))
                last.then_inc(ps_full, 1)
                take(pe, v_full)
                turn2(x1).then_inc(ps_t_full, 1)
                take(pe, t_full)
                for i in range(2):
                    for j in range(4):
                        for c in range(KC):
                            last = mm(ps_h[i][:, B * j:B * j + B], w_h[:, c, 128 * (4 * i + j):128 * (4 * i + j) + 128],
                                      t2[:, c, :], start=(c == 0), stop=(c == 1))
                    last.then_inc(h_full[i], 1)
                for i in range(2):
                    take(pe, ht_full[i])
                    for j in range(4 * i, 4 * i + 4):
                        last = mm(ps_o[0:B, 0:D], ht[:, j, :], w2m[:, j, :], start=(j == 0), stop=(j == JF - 1))
                last.then_inc(ps_full, 1)
                take(pe, v_full)
                turn2(y).then_inc(ps_t_full, 1)
                take(pe, t_full)
                for c in range(KC):
                    last = mm(ps_t[0:B, 0:E1], t2[:, c, :], wg[:, c, :], start=(c == 0), stop=(c == 1))
                last.then_inc(ps_full, 1)

                def hidden(e):
                    for j in range(J1):
                        for c in range(KC):
                            last = mm(ps_h[e % 2][:, B * j:B * j + B], w1e_sb[:, e, c, 128 * j:128 * j + 128],
                                      t2[:, c, :], start=(c == 0), stop=(c == 1))
                    last.then_inc(h_full[e % 2], 1)

                hidden(0)
                hidden(1)
                take(pe, v_full)
                pe.transpose(ps_t[0:E1, 0:B], gate[:, :], ident[0:B, 0:B]).then_inc(ps_t_full, 1)
                take(pe, t_full)
                mm(ps_o[0:B, 0:D], gt[:, :], bd_sb[:, :], start=True, stop=True).then_inc(ps_full, 1)
                for e in range(E1):
                    take(pe, ht_full[e % 2])
                    take(pe, y_free[e % 2])
                    for j in range(J1):
                        last = mm(ps_y[e % 2][0:B, 0:D], ht[:, 4 * (e % 2) + j, :], w2e_sb[:, e, j, :],
                                  start=(j == 0), stop=(j == J1 - 1))
                    last.then_inc(y_full[e % 2], 1)
                    if e + 2 < E1:
                        hidden(e + 2)

        @block.scalar
        def _(act):
            chain = Chain(act, act_s)

            def turned(dst, rows=128, cols=None):
                take(act, ps_t_full)
                act.activation(dst, ps_t[0:rows, 0:cols], ACT.Copy).then_inc(t_full, 1)

            def root(o, i):
                take(act, act_in)
                act.activation(o, i, ACT.Sqrt).then_inc(act_out, 1)

            t2f = t2[:, :, :].rearrange("p a b -> p (a b)")
            t4flat = t4[:, :, :].rearrange("p a b -> p (a b)")
            root(rs_all[:, :], rs_all[:, :])
            root(inv_out[:, :], inv_out[:, :])
            with act.Fori(0, NB) as b:
                act.activation(y[:, :], xn_big[:, ds(b, 1), :].rearrange("p a d -> p (a d)"), ACT.Copy).then_inc(xa_full, 1)
                turned(t2f, cols=2 * B)
                take(act, act_in)
                chain(act.activation(ek[:, 0:D], qk[:, 0:D], ACT.Square, accum_out=st[:, 0:1]))
                act.activation(qk[:, D:2 * D], qk[:, D:2 * D], ACT.Square, accum_out=st[:, 1:2])
                chain(act.activation(x1[:, :], ek[:, 0:D], ACT.Square, accum_out=st[:, 2:3]))
                act.activation(st[:, 3:4], st[:, 2:3], ACT.Sqrt).then_inc(act_out, 1)
                take(act, act_in)
                act.activation(ek[:, D:2 * D], ek[:, 0:D], ACT.Square).then_inc(k4_full, 1)
                chain.restart()
            root(st2[:, 0:2], st2[:, 0:2])

            def gelus(i, bias, func):
                take(act, h_full[i])
                for j in range(4):
                    last = act.activation(ht[:, 4 * i + j, :], ps_h[i][:, B * j:B * j + B], func, bias=bias(j))
                last.then_inc(ht_full[i], 1)

            act.wait_ge(l_moe0, 16 * (E0 + 1))
            with act.Fori(0, NB) as b:
                turned(t4flat, cols=4 * B)
                root(sd[:, 0:1], sd[:, 0:1])
                turned(t2f, cols=2 * B)
                for i in range(2):
                    gelus(i, lambda j: b1_col[:, 4 * i + j:4 * i + j + 1], ACT.Gelu)
                take(act, act_in)
                act.activation(lt[:, :], lg[:, :], ACT.Exp, accum_out=st[:, 0:1]).then_inc(act_out, 1)
                turned(gt[:, :], rows=E0, cols=B)
                root(sd[:, 0:1], sd[:, 0:1])
                turned(t2f, cols=2 * B)
                take(act, act_in)
                act.activation(ek[:, :], ek[:, :], ACT.Exp).then_inc(act_out, 1)
            act.wait_ge(l_c, 128)
            act.wait_ge(l_l1, 16 * 14)
            with act.Fori(0, NB) as b:
                root(sd[:, 0:1], sd[:, 0:1])
                turned(t4flat, cols=4 * B)
                take(act, act_in)
                act.activation(ek[:, 0:D], ek[:, 0:D], ACT.Exp).then_inc(act_out, 1)
                turned(t2f, cols=2 * B)
                root(sd[:, 0:1], sd[:, 0:1])
                turned(t2f, cols=2 * B)
                for i in range(2):
                    gelus(i, lambda j: b1_col[:, 4 * i + j:4 * i + j + 1], ACT.Relu)
                root(sd[:, 0:1], sd[:, 0:1])
                root(sd[:, 0:1], sd[:, 0:1])
                turned(t2f, cols=2 * B)
                for e in range(E1):
                    if e == 1:
                        turned(gt[:, :], rows=E1, cols=B)
                    gelus1 = lambda j, e=e: b1e_col[:, e, j:j + 1]
                    if e >= 2:
                        take(act, ht_free[e % 2])
                    gelus(e % 2, gelus1, ACT.Gelu)

        @block.vector
        def _(dve):
            chain = Chain(dve, dve_s)
            ts, tt, stt = dve.tensor_scalar, dve.tensor_tensor, dve.scalar_tensor_tensor

            def root(o_in):
                dve.sem_inc(act_in, 1)
                take(dve, act_out)

            def norm(dst, src, g=None, bias=None):
                chain(dve.bn_stats(bn6[:, :], src))
                chain(dve.bn_aggr(mv[:, :], bn6[:, :]))
                chain(ts(sd[:, 0:1], mv[:, 1:2], LN_EPS, None, ALU.add))
                root(sd)
                chain(dve.reciprocal(rs[:, :], sd[:, 0:1]))
                last = ts(dst, src, mv[:, 0:1], rs[:, 0:1], ALU.subtract, ALU.mult)
                if g is not None:
                    chain(last)
                    chain(tt(dst, dst, g, ALU.mult))
                    last = tt(dst, dst, bias, ALU.add)
                return last

            dve.wait_ge(const_full, 1)
            dve.wait_ge(l_x, 80)
            with dve.Fori(0, NB) as b:
                chain(dve.bn_stats(bn6[:, :], x_big[:, ds(b, 1), :].rearrange("p a d -> p (a d)")))
                chain(dve.bn_aggr(mv[:, :], bn6[:, :]))
                chain(dve.tensor_copy(mv_all[:, ds(b, 1), :].rearrange("p a d -> p (a d)"), mv[:, :]))
                chain.restart()
            chain(ts(rs_all[:, :], mv_all[:, :, 1], LN_EPS, None, ALU.add))
            root(rs_all)
            chain(dve.reciprocal(rs_all[:, :], rs_all[:, :]))
            chain.restart()
            with dve.Fori(0, NB) as b:
                chain(ts(xn_big[:, ds(b, 1), :].rearrange("p a d -> p (a d)"),
                         x_big[:, ds(b, 1), :].rearrange("p a d -> p (a d)"),
                         mv_all[:, ds(b, 1), 0:1].rearrange("p a d -> p (a d)"), rs_all[:, ds(b, 1)],
                         ALU.subtract, ALU.mult))
                chain.restart()
            dve.sem_inc(feat0_full, 1)
            dve.wait_ge(l_edge, 48)
            dve.tensor_copy(e_f32[0], e_i32[0])
            chain(dve.tensor_copy(e_f32[1], e_i32[1]))
            dve.sem_inc(edge_f_full, 1)
            dv = e_f32[0].rearrange("q (c e) -> q c e", c=TC)
            dve.tensor_reduce(st_min[:, :], dv, AX.X, ALU.min)
            chain(dve.tensor_reduce(st_max[:, :], dv, AX.X, ALU.max))
            dve.sem_inc(minmax_full, 1)
            for g in range(6):
                dve.wait_ge(edge_ps_full, g + 1)
                ps = ps_h[g % 2][0:B, 0:4 * TR].rearrange("p (c q) -> p c q", c=4)
                c0 = 4 * (g % 2)
                view = lambda t: t[:, 0:NT].rearrange("p (q c) -> p c q", c=TC)[:, c0:c0 + 4, :]
                if g // 2 == 1:
                    dve.tensor_copy(view(src_i), ps)
                last = dve.tensor_copy(view((dst_f, src_f, w_f)[g // 2]), ps)
                chain(last)
                if g < 4:
                    dve.sem_inc(edge_ps_free, 1)
            dve.wait_ge(minmax_stored, 32)
            dve.sem_inc(iota_full, 1)
            dve.sem_inc(tabs_full, 1)
            big = 12582912.0
            chain(ts(src_hi, src_f, 1.0 / B, 0.004 - 0.5, ALU.mult, ALU.add))
            chain(ts(src_hi, src_hi, big, -big, ALU.add, ALU.add))
            chain(stt(out=src_lo, in0=src_hi, scalar=-float(B), in1=src_f, op0=ALU.mult, op1=ALU.add))
            dve.wait_ge(minmax_loaded, 32)
            take(dve, tile_iota)
            chain(ts(t_msk, t_max, base_col[:, 0:1], None, ALU.is_ge))
            chain(ts(t_min, t_min, base_col[:, 0:1], float(B), ALU.subtract, ALU.is_lt))
            chain(tt(t_msk, t_msk, t_min, ALU.mult))
            chain(tt(t_val, t_msk, t_iot, ALU.mult))
            chain(dve.tensor_reduce(blk[:, 1:2], t_val, AX.X, ALU.max))
            chain(ts(t_msk, t_msk, -10000.0, 10000.0, ALU.mult, ALU.add))
            chain(tt(t_val, t_val, t_msk, ALU.add))
            chain(dve.tensor_reduce(blk[:, 0:1], t_val, AX.X, ALU.min))
            chain(ts(blk[:, 2:3], blk[:, 0:1], 9000.0, None, ALU.is_lt))
            chain(tt(blk[:, 0:1], blk[:, 0:1], blk[:, 2:3], ALU.mult))
            chain(tt(blk[:, 1:2], blk[:, 1:2], blk[:, 0:1], ALU.subtract))
            chain(ts(t_msk[:, 0:MAXCH], t_iot[:, 0:MAXCH], float(CH), float(CH), ALU.mult, ALU.add))
            chain(ts(t_msk[:, 0:MAXCH], t_msk[:, 0:MAXCH], blk[:, 1:2], None, ALU.is_le))
            chain(dve.tensor_reduce(blk[:, 2:3], t_msk[:, 0:MAXCH], AX.X, ALU.add))
            chain(ts(blk[:, 1:2], blk[:, 2:3], 1.0, None, ALU.add))
            chain(dve.tensor_copy(blk_i[:, 0:2], blk[:, 0:2]))
            dve.sem_inc(blk_full, 1)
            chain.restart()
            dve.wait_ge(l_w0, 112)
            dve.sem_inc(w_prep, 1)
            wq4 = wqkvs[:, :, 0:512].rearrange("p c (h n) -> p c h n", h=2)
            chain(dve.tensor_reduce(st4, wq4, AX.X, ALU.add))
            chain(ts(st4, st4, 1.0 / D, None, ALU.mult))
            chain(tt(wq4, wq4, st4.unsqueeze(3).to_broadcast([128, KC, 2, D]), ALU.subtract))
            bq2 = bias0[:, 0:512].rearrange("p (h n) -> p h n", h=2)
            chain(dve.tensor_reduce(st[:, 0:2], bq2, AX.X, ALU.add))
            chain(ts(st[:, 0:2], st[:, 0:2], 1.0 / D, None, ALU.mult))
            chain(tt(bq2, bq2, st[:, 0:2].unsqueeze(2).to_broadcast([B, 2, D]), ALU.subtract))
            take(dve, w_prep_ps)
            for c in range(KC):
                dve.tensor_scalar(ht[:, 5 + c, :], ones[:, :], b1_col[:, c:c + 1], None, ALU.mult)
            chain(dve.tensor_copy(t4f, ps_y0[:, :]))
            dve.sem_inc(w_prep2, 1)
            take(dve, w_prep_ps)
            sv = wqkvs[:, :, 3 * D:4 * D]
            chain(tt(sv, sv, ps_y1[:, :].rearrange("p (c n) -> p c n", c=KC), ALU.add))
            chain(tt(b_tmp[:, :], b_tmp[:, :], ps_o[0:B, 0:D], ALU.add))
            chain(tt(bias0[:, 3 * D:], bias0[:, 3 * D:], b_tmp[:, :], ALU.add))
            chain.restart()
            for j in range(2):
                dve.sem_inc(deg_free[j], 1)
            with dve.Fori(0, NT // HT_ // 2) as i:
                for j in range(2):
                    take(dve, deg_free[j])
                    t0 = i * 2 * HT_ + j * HT_
                    for o, dig, n in ((oh_lo[j], src_lo, B), (oh_hi[j], src_hi, NB)):
                        last = tt(o, iota[:, 0:n].unsqueeze(1).to_broadcast([B, HT_, n]),
                                  dig[:, ds(t0, HT_)].unsqueeze(2).to_broadcast([B, HT_, n]), ALU.is_equal)
                    last.then_inc(deg_full[j], 1)
            take(dve, deg_ps_full)
            dve.sem_inc(xg_clear, 1)
            chain(ts(inv_out[:, :], ps_kv[0:B, 0:NB], 1.0, None, ALU.max))
            root(inv_out)
            chain(dve.reciprocal(inv_out[:, :], inv_out[:, :]))
            dve.sem_inc(w_prep, 1)
            chain.restart()

            dve.sem_inc(pa_free, 1)
            dve.sem_inc(pb_free, 1)
            with dve.Fori(0, NB) as b:
                take(dve, pa_full)
                chain(tt(qk[:, :], ps_h0[0:B, :], bias0[:, 0:512], ALU.add))
                dve.sem_inc(pa_free, 1)
                dve.sem_inc(act_in, 1)
                take(dve, act_out)
                chain(ts(st[:, 4:6], st[:, 0:2], 1e-7, None, ALU.add))
                chain(dve.reciprocal(st[:, 6:8], st[:, 4:6]))
                chain(tt(st[:, 8:9], st[:, 6:7], st[:, 3:4], ALU.mult))
                chain(ts(st[:, 9:10], st[:, 8:9], 1e-12, None, ALU.max))
                chain(dve.reciprocal(st[:, 10:11], st[:, 9:10]))
                chain(tt(st[:, 11:12], st[:, 10:11], st[:, 6:7], ALU.mult))
                take(dve, rowa_free, 16)
                chain(ts(row_a[:, D:2 * D], ek[:, 0:D], st[:, 11:12], None, ALU.mult))
                chain(ts(ek[:, 0:D], qk[:, D:2 * D], st[:, 7:8], None, ALU.mult))
                dve.sem_inc(act_in, 1)
                take(dve, pb_full)
                tt(row_a[:, 0:D], ps_h1[0:B, D:2 * D], bias0[:, 3 * D:4 * D], ALU.add)
                chain(tt(agg_s[:, :], ps_h1[0:B, 0:D], bias0[:, 2 * D:3 * D], ALU.add))
                dve.sem_inc(v_full, 1)
                chain(tt(row_a[:, 0:D], row_a[:, 0:D], x_big[:, ds(b, 1), :].rearrange("p a d -> p (a d)"), ALU.add))
                dve.sem_inc(pb_free, 1)
                dve.sem_inc(rowa_full, 1)
                chain.restart()
            take(dve, ps_full)
            dve.sem_inc(loop_a_done, 1)
            chain(dve.tensor_copy(st2[:, 0:2], ps_y1[:, 0:2]))
            root(st2)
            chain(ts(st2[:, 0:2], st2[:, 0:2], 1e-12, None, ALU.max))
            chain(dve.reciprocal(st2[:, 0:2], st2[:, 0:2]))
            for c in range(KC):
                last = ts(kvf[:, D * c:D * c + D], ps_kv[:, D * c:D * c + D], st2[:, c:c + 1], 1.0 / math.sqrt(N),
                          ALU.mult, ALU.mult)
            chain(last)
            dve.sem_inc(v_full, 1)
            take(dve, ps_full)
            chain(dve.tensor_copy(t4f, ps_y0[:, :]))
            dve.sem_inc(v_full, 1)
            take(dve, ps_full)
            chain(dve.tensor_copy(kvo[:, :, :], ps_y1[:, :].rearrange("p (c n) -> p c n", c=KC)))
            take(dve, rowa_free, 16)
            dve.sem_inc(v_full, 1)
            chain.restart()

            def onehots(b, weighted):
                n = dve.value_load(n_tab[0:1, ds(b, 1)], min_val=1, max_val=MAXCH)
                lo = dve.value_load(lo_tab[0:1, ds(b, 1)], min_val=0, max_val=NT - 1)
                with dve.Fori(0, n) as c:
                    t0 = nc.s_assert_within(dve.snap(lo + c * CH), 0, NT - 1,
                                            skip_runtime_bounds_check_because="a block's chunks start inside its span")
                    take(dve, oh_free)
                    if weighted:
                        dve.tensor_copy(w_cur[:, :], w_f[:, ds(t0, CH)])
                    chain(ts(dst_cur[:, :], dst_f[:, ds(t0, CH)], base[:, ds(b, 1)], None, ALU.subtract))
                    for s in range(CH):
                        if weighted:
                            last = ts(oh[:, s, :], iota[:, :], dst_cur[:, s:s + 1], w_cur[:, s:s + 1],
                                      ALU.is_equal, ALU.mult)
                        else:
                            last = ts(oh[:, s, :], iota[:, :], dst_cur[:, s:s + 1], None, ALU.is_equal)
                    last.then_inc(oh_full, 1)
                    chain.restart()

            def first_max(src, mask):
                chain(dve.tensor_reduce(st[:, 1:2], src, AX.X, ALU.max))
                chain(ts(mask, src, st[:, 1:2], -8.0, ALU.is_ge, ALU.mult))
                chain(tt(mask, mask, iota[:, 0:8], ALU.add))
                chain(dve.tensor_reduce(st[:, 2:3], mask, AX.X, ALU.min))
                return ts(mask, mask, st[:, 2:3], None, ALU.is_equal)

            dve.wait_ge(blk_loaded, 32)
            chain(dve.memset(cum_f[:, :], 0.0))
            chain(dve.tensor_copy(n_f[:, :], n_tab[:, :]))
            chain(dve.tensor_tensor_scan(cum_f[:, 1:NB + 1], ones[0:1, 0:NB], n_f[:, :], 0.0, ALU.mult, ALU.add))
            chain(dve.tensor_copy(cum_tab[:, :], cum_f[:, :]))
            dve.sem_inc(cum_full, 1)
            chain.restart()
            dve.wait_ge(l_wh, 80)
            dve.wait_ge(l_l1, 16 * 14)
            dve.sem_inc(agg_free, 1)
            dve.sem_inc(rowa_used, 1)
            for i in range(2):
                dve.sem_inc(y_free[i], 1)
            with dve.Fori(0, NB) as b:
                onehots(b, True)
                take(dve, agg_full)
                chain(dve.tensor_copy(agg_s[:, :], ps_agg[0:B, 0:D]))
                dve.sem_inc(agg_free, 1)
                take(dve, rowa_in, 16)
                dve.sem_inc(v_full, 1)
                take(dve, ps_full)
                chain(tt(x1[:, :], ps_o[0:B, 0:D], row_a[:, 0:D], ALU.add))
                chain(norm(y[:, :], x1[:, :]))
                dve.sem_inc(v_full, 1)
                take(dve, ps_full)
                chain(tt(lg[:, :], ps_t[0:B, 0:E0], bg_bc[:, :], ALU.add))
                chain(dve.tensor_reduce(st[:, 1:2], lg[:, :], AX.X, ALU.max))
                chain(ts(lg[:, :], lg[:, :], st[:, 1:2], None, ALU.subtract))
                dve.sem_inc(act_in, 1)
                take(dve, act_out)
                chain(dve.reciprocal(st[:, 3:4], st[:, 0:1]))
                chain(ts(lt[:, :], lt[:, :], st[:, 3:4], None, ALU.mult))
                chain(first_max(lt[:, :], lu[:, :]))
                chain(tt(gate[:, :], lt[:, :], lu[:, :], ALU.mult))
                dve.sem_inc(v_full, 1)
                take(dve, ps_full)
                chain(tt(acc[:, :], x1[:, :], ps_o[0:B, 0:D], ALU.add))
                take(dve, rowb_free, 16)
                for q in range(E0 // 2):
                    take(dve, y_full[q % 2])
                    for h in range(2):
                        e = 2 * q + h
                        dst = row_b[:, 0:D] if e == E0 - 1 else acc[:, :]
                        chain(stt(out=dst, in0=ps_y[q % 2][0:B, D * h:D * h + D], scalar=gate[:, e:e + 1],
                                  in1=acc[:, :], op0=ALU.mult, op1=ALU.add))
                    dve.sem_inc(y_free[q % 2], 1)
                chain(norm(row_b[:, D:2 * D], row_b[:, 0:D]))
                dve.sem_inc(v_full, 1)
                take(dve, fout_free, 16)
                chain(ts(f_out[:, :], row_b[:, D:2 * D], inv_out[:, ds(b, 1)], None, ALU.mult))
                dve.sem_inc(fout_full, 1)
                take(dve, pa_full)
                chain(tt(qk[:, :], ps_h0[0:B, :], bias1[:, 0:512], ALU.add))
                chain(ts(ek[:, :], qk[:, :], 0.0, None, ALU.min))
                dve.sem_inc(act_in, 1)
                take(dve, act_out)
                take(dve, pb_full)
                tt(v1[:, :, 0:128], ps_h1[0:B, 0:D].rearrange("p (c n) -> p c n", c=2),
                   bias1[:, 2 * D:3 * D].rearrange("p (c n) -> p c n", c=2), ALU.add)
                chain(stt(out=row_b[:, 2 * D:3 * D], in0=qk[:, 0:D], scalar=0.0, in1=ek[:, 0:D], op0=ALU.max, op1=ALU.add))
                chain(stt(out=ek[:, 0:D], in0=qk[:, D:2 * D], scalar=0.0, in1=ek[:, D:2 * D], op0=ALU.max, op1=ALU.add))
                dve.sem_inc(v_full, 1)
                dve.sem_inc(rowb_full, 1)
                take(dve, kn_free)
                dve.sem_inc(rowa_used, 1)
                chain.restart()
            take(dve, ps_full)
            chain(dve.memset(kvd[:, :, :], 0.0))
            for h in range(4):
                p = slice(DH * h, DH * h + DH)
                kv = ps_kv[p, 0:258].rearrange("p (c n) -> p c n", c=KC)
                dve.tensor_copy(kvd[p, :, DH * h:DH * h + DH], kv[:, :, DH * h:DH * h + DH])
                last = dve.tensor_copy(kvd[p, :, 128 + h:129 + h], kv[:, :, 128:129])
            chain(last)
            take(dve, rowb_free, 16)
            take(dve, fout_free, 16)
            dve.sem_inc(stored, 1)
            dve.sem_inc(v_full, 1)
            dve.sem_inc(loop_b_done, 1)
            chain.restart()

            dve.sem_inc(rowb_used, 1)
            dve.wait_ge(l_c, 128)
            with dve.Fori(0, NB) as b:
                onehots(b, False)
                take(dve, agg_full)
                chain(ts(sd[:, 0:1], ps_agg[0:B, D:D + 1], 1.0, None, ALU.max))
                root(sd)
                chain(dve.reciprocal(rs[:, :], sd[:, 0:1]))
                chain(ts(agg_s[:, :], ps_agg[0:B, 0:D], rs[:, 0:1], None, ALU.mult))
                dve.sem_inc(agg_free, 1)
                take(dve, rowb_in, 16)
                dve.sem_inc(v_full, 1)
                take(dve, ps_full)
                chain(tt(qk[:, 0:D], ps_o[0:B, 0:D], bc[:, 0, :], ALU.add))
                chain(ts(ek[:, 0:D], qk[:, 0:D], 0.0, None, ALU.min))
                dve.sem_inc(act_in, 1)
                num = ps_h0[0:B, 0:264].rearrange("p (c n) -> p c n", c=KC)
                chain(ts(lt[:, :].rearrange("p (c h) -> p c h", c=KC), num[:, :, 128:132], 1e-6, None, ALU.add))
                chain(dve.reciprocal(lt[:, :], lt[:, :]))
                for c in range(KC):
                    last = tt(y[:, 128 * c:128 * c + 128].rearrange("p (h n) -> p h n", h=4),
                              num[:, c, 0:128].rearrange("p (h n) -> p h n", h=4),
                              lt[:, 4 * c:4 * c + 4].unsqueeze(2).to_broadcast([B, 4, DH]), ALU.mult)
                chain(last)
                dve.sem_inc(v_full, 1)
                take(dve, act_out)
                chain(stt(out=ek[:, 0:D], in0=qk[:, 0:D], scalar=0.0, in1=ek[:, 0:D], op0=ALU.max, op1=ALU.add))
                chain(stt(out=row_b[:, 0:D], in0=ek[:, 0:D], scalar=-1.0, in1=row_b[:, 0:D], op0=ALU.add, op1=ALU.add))
                take(dve, ps_full)
                chain(tt(x1[:, :], ps_o[0:B, 0:D], bc[:, 1, :], ALU.add))
                chain(tt(x1[:, :], x1[:, :], row_b[:, D:2 * D], ALU.add))
                chain(norm(x1[:, :], x1[:, :], bc[:, 3, :], bc[:, 4, :]))
                dve.sem_inc(v_full, 1)
                chain(tt(y[:, :], x1[:, :], bc[:, 2, :], ALU.add))
                take(dve, ps_full)
                chain(tt(y[:, :], y[:, :], ps_o[0:B, 0:D], ALU.add))
                chain(norm(y[:, :], y[:, :], bc[:, 5, :], bc[:, 6, :]))
                chain(tt(x1[:, :], y[:, :], row_b[:, 0:D], ALU.add))
                chain(norm(y[:, :], x1[:, :]))
                dve.sem_inc(v_full, 1)
                take(dve, ps_full)
                chain(tt(lg[:, :], ps_t[0:B, 0:E1], bg_bc[:, :], ALU.add))
                chain(first_max(lg[:, :], lt[:, :]))
                chain(stt(out=lg[:, :], in0=lt[:, :], scalar=-3.0e38, in1=lg[:, :], op0=ALU.mult, op1=ALU.add))
                chain(first_max(lg[:, :], lu[:, :]))
                chain(tt(gate[:, :], lt[:, :], lu[:, :], ALU.add))
                dve.sem_inc(v_full, 1)
                take(dve, ps_full)
                chain(tt(acc[:, :], x1[:, :], ps_o[0:B, 0:D], ALU.add))
                take(dve, fout_free, 16)
                for e in range(E1):
                    take(dve, y_full[e % 2])
                    dst = f_out[:, :] if e == E1 - 1 else acc[:, :]
                    chain(stt(out=dst, in0=ps_y[e % 2][0:B, 0:D], scalar=gate[:, e:e + 1],
                              in1=acc[:, :], op0=ALU.mult, op1=ALU.add))
                    dve.sem_inc(y_free[e % 2], 1)
                    if e + 2 < E1:
                        dve.sem_inc(ht_free[e % 2], 1)
                dve.sem_inc(fout_full, 1)
                dve.sem_inc(rowb_used, 1)
                chain.restart()


_NAMES = """x src dst edge_weight L0_gnn_W_self L0_gnn_W_neighbor L0_gnn_bias L0_mix_W_qkv L0_mix_b_qkv
L0_mix_W_out L0_mix_b_out L0_ffn_W1 L0_ffn_b1 L0_ffn_Wg L0_ffn_bg L0_ffn_Wd L0_ffn_bd L1_gnn_weight
L1_gnn_bias L1_mix_Wq L1_mix_bq L1_mix_Wk L1_mix_bk L1_mix_Wv L1_mix_bv L1_mix_Wo L1_mix_bo L1_mix_W1
L1_mix_b1 L1_mix_W2 L1_mix_b2 L1_mix_ln1_g L1_mix_ln1_b L1_mix_ln2_g L1_mix_ln2_b L1_ffn_Wg L1_ffn_bg
L1_ffn_W1 L1_ffn_b1 L1_ffn_W2 L1_ffn_b2""".split()


def kernel(**inputs):
    import numpy as np
    import concourse.bacc as bacc
    from concourse.bass_utils import run_bass_kernel_spmd

    nc = bacc.Bacc("TRN2", target_bir_lowering=False, num_devices=1)
    arrays, aps = {}, {}
    for name in _NAMES:
        v = np.ascontiguousarray(inputs[name])
        arrays["in_" + name] = v
        aps[name] = nc.dram_tensor("in_" + name, v.shape, mybir.dt.from_np(v.dtype), kind="ExternalInput").ap()
    out = nc.dram_tensor("out_rows", (N, D), F32, kind="ExternalOutput").ap()
    program(nc, aps, out)
    r = run_bass_kernel_spmd(nc, [arrays], core_ids=[0])
    return r.results[0]["out_rows"]
```

```python
import math
from contextlib import ExitStack

import concourse.bass as bass
from concourse import mybir

F32 = mybir.dt.float32
BF16 = mybir.dt.bfloat16
I32 = mybir.dt.int32
ALU = mybir.AluOpType
ACT = mybir.ActivationFunctionType
AX = mybir.AxisListType

N, E, D = 3125, 100000, 256
B = 125
NB = N // B
NT = E // B
KC = D // 128
GS, GR = 6, 6
CH = GS * GR
NTP = NT + CH
MAXCH = -(-NT // CH)
TR, TC = 100, NT // 100
H0, E0 = 1024, 8
H1, E1 = 512, 8
J0, J1 = H0 // 128, H1 // 128
FF = 1024
JF = FF // 128
HEADS, DH = 8, 32
LN_EPS = 1e-5
G = 5
NS = NB // G
HALVES = ((0, 3 * B), (3 * B, G * B))
DT = 20
ds = bass.ds


def take(eng, sem, n=1):
    eng.wait_ge(sem, n)
    eng.sem_clear(sem)


class Chain:

    def __init__(self, eng, sem):
        self.eng, self.sem, self.n = eng, sem, 0

    def __call__(self, ins):
        ins.then_inc(self.sem, 1)
        self.n += 1
        self.eng.wait_ge(self.sem, self.n)

    def restart(self):
        if self.n:
            self.eng.sem_clear(self.sem)
        self.n = 0


def program(nc, a, out, dbg=None):
    ctx = ExitStack()
    with ctx:
        def sb(name, shape, dt=F32):
            return ctx.enter_context(nc.sbuf_tensor(name, shape, dt))

        def sem(name):
            return ctx.enter_context(nc.semaphore(name))

        def pair(name):
            return [sem(name + "0"), sem(name + "1")]

        banks = [ctx.enter_context(nc.psum_tensor(f"bank{i}", [128, 512], F32)) for i in range(8)]
        ps_agg, ps_kv = banks[0], banks[7]
        ps_t, ps_h, ps_y = banks[1:3], banks[3:5], banks[5:7]

        feat0 = nc.dram_tensor("feat0", (N, D), F32).ap()
        feat1 = nc.dram_tensor("feat1", (N, D), F32).ap()
        rows_a = nc.dram_tensor("rows_a", (N, 2 * D), F32).ap()
        rows_b = nc.dram_tensor("rows_b", (N, 3 * D), F32).ap()
        tile_min = nc.dram_tensor("tile_min", (TR, TC), F32).ap()
        tile_max = nc.dram_tensor("tile_max", (TR, TC), F32).ap()
        block_lo = nc.dram_tensor("block_lo", (NB, 1), I32).ap()
        block_n = nc.dram_tensor("block_n", (NB, 1), I32).ap()

        ident = sb("ident", [128, 128])
        iota = sb("iota", [B, B])
        base = sb("base", [B, NB])
        base_col = sb("base_col", [NB, 1])
        ones = sb("ones", [128, B])
        zero_w = sb("zero_w", [1, 128], BF16)
        zero_r = sb("zero_r", [1, 512], BF16)

        dst_f = sb("dst_f", [B, NTP])
        w_f = sb("w_f", [B, NTP])
        src_i = sb("src_i", [B, NTP], I32)
        lo_tab = sb("lo_tab", [1, NB], I32)
        n_tab = sb("n_tab", [1, NB], I32)
        cum_tab = sb("cum_tab", [1, NB + 1], I32)
        cum_f = sb("cum_f", [1, NB + 1])
        n_f = sb("n_f", [1, NB])
        idx_cur = sb("idx_cur", [B, CH], I32)
        dst_cur = sb("dst_cur", [B, CH])
        w_cur = sb("w_cur", [B, CH])
        xg = sb("xg", [B, CH, D + 1])
        oh = sb("oh", [B, CH, B])
        inv_out = sb("inv_out", [B, NB])

        w_exp = [sb(f"w_exp{i}", [128, 2 * KC * H1]) for i in range(2)]
        wd_sb = [w[:, :].rearrange("p (j d) -> p j d", j=J0) for w in w_exp]
        w1e_sb = [w[:, 0:KC * H1].rearrange("p (c h) -> p c h", c=KC) for w in w_exp]
        w2e_sb = [w[:, KC * H1:].rearrange("p (j d) -> p j d", j=J1) for w in w_exp]
        w_h = sb("w_h", [128, KC, H0])
        w_x = sb("w_x", [128, 8 * D])
        wqkvs = w_x[:, :].rearrange("p (c n) -> p c n", c=KC)
        w2m = w_x[:, :].rearrange("p (j n) -> p j n", j=JF)
        wqkv1 = sb("wqkv1", [128, KC, 3 * D])
        wn = sb("wn", [128, KC, D])
        wo = sb("wo", [128, KC, D])
        kvo = sb("kvo", [128, KC, D])
        kvd = sb("kvd", [128, KC, 132])
        wg = sb("wg", [128, J0, E0])
        bd_sb = sb("bd_sb", [E0, D])
        b1_col = sb("b1_col", [128, J0])
        b1e_col = sb("b1e_col", [128, E1, J1])
        bias = sb("bias", [B, 7, D])
        bias_f = bias[:, :, :].rearrange("p k d -> p (k d)")
        bias0 = bias_f[:, 0:4 * D]
        bias1 = bias_f[:, 4 * D:7 * D]
        bc = bias
        bg_bc = sb("bg_bc", [B, E0])
        b_tmp = sb("b_tmp", [B, D])

        arena = sb("arena", [128, 19020])

        def cut(at, n, parts=B):
            return arena[0:parts, at:at + n]

        row_a = cut(0, 2560).rearrange("p (i n) -> p i n", i=G)
        row_b = cut(2560, 3840).rearrange("p (i n) -> p i n", i=G)
        x1, y, f_out = (cut(n, 1280).rearrange("p (i n) -> p i n", i=G) for n in (6400, 7680, 8960))
        t4 = cut(10240, 2500, 128).rearrange("p (k n) -> p k n", k=4)
        ht = cut(12740, 5000, 128).rearrange("p (j n) -> p j n", j=8)
        ek = cut(12740, 2560).rearrange("p (i n) -> p i n", i=G)
        v1 = cut(15300, G * 258).rearrange("p (i c n) -> p i c n", i=G, c=2)
        t4f = cut(12740, 512, 128)
        bv_rows = cut(13252, 250, 128).rearrange("p (c n) -> p c n", c=2)
        x_big = cut(0, 6400).rearrange("p (b d) -> p b d", b=NB)
        agg_s = sb("agg_s", [B, G, D + 1])
        kvf = cut(17740, 512, 128)
        st = sb("st", [B, 12, G])
        bn6 = sb("bn6", [B, G, 6])
        mv = sb("mv", [B, G, 2])
        sd = sb("sd", [B, G])
        rs = sb("rs", [B, G])
        lg, lt, lu, gate = (sb(n, [B, G, 8]) for n in ("lg", "lt", "lu", "gate"))
        gt = sb("gt", [8, G * B])
        mv_all = sb("mv_all", [B, NB, 2])
        rs_all = sb("rs_all", [B, NB])
        st_min, st_max = sb("st_min", [TR, TC]), sb("st_max", [TR, TC])
        blk, blk_i = sb("blk", [NB, 3]), sb("blk_i", [NB, 2], I32)
        st4 = sb("st4", [128, KC, 2])[:, :, :]
        st2 = sb("st2", [128, 2])

        def scratch(rows, at, n):
            return xg[0:rows, at:at + n, :].rearrange("p a b -> p (a b)")

        e_i32 = [scratch(TR, 4 * i, 4)[:, 0:TC * B].bitcast(I32) for i in range(2)]
        e_f32 = [scratch(TR, 8 + 4 * i, 4)[:, 0:TC * B] for i in range(3)]
        src_f, src_hi, src_lo = (scratch(B, n, 4)[:, 0:NT] for n in (20, 24, 28))
        oh_f = oh[:, :, :].rearrange("p a b -> p (a b)")
        oh_lo = [oh_f[:, 2000 * i:2000 * i + DT * B // 2].bitcast(BF16).rearrange("p (t l) -> p t l", t=DT)
                 for i in range(2)]
        oh_hi = [oh_f[:, 2000 * i + 1250:2000 * i + 1250 + DT * NB // 2].bitcast(BF16)
                 .rearrange("p (t l) -> p t l", t=DT) for i in range(2)]
        range_t = scratch(NB, 0, 16)
        t_min, t_max, t_msk, t_val, t_iot = (range_t[:, NT * i:NT * i + NT] for i in range(5))

        l_x, l_edge, l_w0, l_wh, l_l1, l_c, l_b1 = (
            sem(n) for n in ("x_loaded", "edges_loaded", "w_mix0_loaded", "w_hid0_loaded", "w_layer1_loaded",
                             "w_c_loaded", "b1_loaded"))
        const_full, edge_f_full, edge_ps_full, edge_ps_free = (
            sem(n) for n in ("consts_made", "edges_as_float", "edge_turn_full", "edge_turn_free"))
        minmax_full, minmax_stored, minmax_loaded, tile_iota, scratch_free, tabs_full = (
            sem(n) for n in ("tile_range_made", "tile_range_stored", "tile_range_loaded", "tile_numbers_made",
                             "edge_rows_free", "edge_tables_made"))
        blk_full, blk_stored, blk_loaded, cum_full = (
            sem(n) for n in ("block_range_made", "block_range_stored", "block_range_loaded", "chunk_sums_made"))
        feat0_full, feat0_stored = sem("feat0_made"), sem("feat0_stored")
        deg_full, deg_free, deg_ps_full = pair("degree_onehot_full"), pair("degree_onehot_free"), sem("degree_counted")
        xg_clear, w_prep, w_prep_ps, w_prep2, setup_done = (
            sem(n) for n in ("gather_buffer_clear", "w_prep", "w_prep_ps", "w_prep2", "setup_done"))
        xg_full = [sem(f"rows_full{k}") for k in range(GR)]
        xg_free = [sem(f"rows_free{k}") for k in range(GR)]
        oh_full, oh_free, idx_full = sem("onehot_full"), sem("onehot_free"), sem("indices_full")
        agg_full, agg_free = sem("agg_ps_full"), sem("agg_ps_free")
        t_act, t_free = pair("turned_ps_full"), pair("turned_ps_free")
        h_act, h_dve, h_free = pair("hidden_ps_full"), pair("proj_ps_full"), pair("hidden_ps_free")
        y_dve, y_free = pair("y_ps_full"), pair("y_ps_free")
        ps_full = sem("ps_stage_full")
        t_full = sem("turned_full")
        v_full = sem("vector_stage_full")
        ht_full = pair("hidden_full")
        act_in, act_out = sem("act_in"), sem("act_out")
        sums_full = sem("sums_over_nodes_full")
        k4_full, k4_used = sem("key4_full"), sem("keys_used")
        agg_s_full, aggs_full = sem("agg_rows_full"), sem("agg_sums_full")
        w_full, w_free = pair("expert_w_full"), pair("expert_w_free")
        xa_in, xa_used = sem("x_rows_loaded"), sem("x_rows_used")
        rowa_full, rowa_free, rowa_in, rowa_used = (
            sem(n) for n in ("row_a_full", "row_a_stored", "row_a_loaded", "row_a_used"))
        rowb_full, rowb_free, rowb_in, rowb_used = (
            sem(n) for n in ("row_b_full", "row_b_stored", "row_b_loaded", "row_b_used"))
        fout_full, fout_free = sem("f_out_full"), sem("f_out_stored")
        loop_a_done, loop_b_done, feat1_done, dbg_stored = (
            sem(n) for n in ("loop_a_done", "loop_b_done", "feat1_done", "dbg_stored"))
        dve_s, act_s = sem("vector_steps"), sem("scalar_steps")

        def rows(ap, s):
            return ap[ds(s * (G * B), G * B), :].rearrange("(i p) d -> p i d", p=B)

        def wview(w):
            return w.rearrange("(c p) n -> p c n", p=128)

        def row(v, p=B):
            return v.partition_broadcast(p)

        def flat(ap):
            return ap.rearrange("p a d -> p (a d)")

        ctx.enter_context(nc.allow_non_contiguous_dma(reason="bias columns and block tables, a few KB"))
        block = ctx.enter_context(nc.Block())

        @block.sync
        def _(sp):
            for s in (rowa_free, rowb_free, fout_free):
                sp.sem_inc(s, 16)
            xv = a["x"].rearrange("(b p) d -> p b d", p=B)
            for i in range(5):
                sp.dma_start(x_big[:, 5 * i:5 * i + 5, :], xv[:, 5 * i:5 * i + 5, :]).then_inc(l_x, 16)
            sp.dma_start(wqkvs[:, :, 0:3 * D], wview(a["L0_mix_W_qkv"])).then_inc(l_w0, 16)
            sp.dma_start(wqkvs[:, :, 3 * D:4 * D], wview(a["L0_gnn_W_self"])).then_inc(l_w0, 16)
            sp.dma_start(wo[:, :, :], wview(a["L0_mix_W_out"])).then_inc(l_w0, 16)
            sp.dma_start(b1_col[:, 0:KC], a["L0_mix_b_qkv"][2 * D:3 * D].rearrange("(c p) -> p c", p=128)).then_inc(l_w0, 16)
            sp.dma_start(bias0[:, 0:3 * D], row(a["L0_mix_b_qkv"])).then_inc(l_w0, 16)
            sp.dma_start(bias0[:, 3 * D:], row(a["L0_gnn_bias"])).then_inc(l_w0, 16)
            sp.dma_start(b_tmp[:, :], row(a["L0_mix_b_out"])).then_inc(l_w0, 16)
            fv = feat0.rearrange("(b p) d -> p b d", p=B)
            take(sp, feat0_full)
            for i in range(5):
                sp.dma_start(fv[:, 5 * i:5 * i + 5, :], x_big[:, 5 * i:5 * i + 5, :]).then_inc(feat0_stored, 16)
            take(sp, minmax_full)
            sp.dma_start(tile_min, st_min[:, :]).then_inc(minmax_stored, 16)
            sp.dma_start(tile_max, st_max[:, :]).then_inc(minmax_stored, 16)
            sp.wait_ge(minmax_stored, 32)
            take(sp, tabs_full)
            sp.dma_start(t_min, tile_min.rearrange("q c -> (q c)").partition_broadcast(NB)).then_inc(minmax_loaded, 16)
            sp.dma_start(t_max, tile_max.rearrange("q c -> (q c)").partition_broadcast(NB)).then_inc(minmax_loaded, 16)
            take(sp, blk_full)
            sp.dma_start(block_lo, blk_i[:, 0:1]).then_inc(blk_stored, 16)
            sp.dma_start(block_n, blk_i[:, 1:2]).then_inc(blk_stored, 16)
            sp.wait_ge(blk_stored, 32)
            sp.dma_start(lo_tab[:, :], block_lo.rearrange("b o -> o b")).then_inc(blk_loaded, 16)
            sp.dma_start(n_tab[:, :], block_n.rearrange("b o -> o b")).then_inc(blk_loaded, 16)
            sp.dma_start(w_h[:, :, :], wview(a["L0_ffn_W1"])).then_inc(l_wh, 16)
            sp.dma_start(wn[:, :, :], wview(a["L0_gnn_W_neighbor"])).then_inc(l_wh, 16)
            sp.dma_start(wg[:, :, :], a["L0_ffn_Wg"].rearrange("(j p) e -> p j e", p=128)).then_inc(l_wh, 16)
            sp.dma_start(bg_bc[:, :], row(a["L0_ffn_bg"])).then_inc(l_wh, 16)
            sp.dma_start(bd_sb[:, :], a["L0_ffn_bd"]).then_inc(l_wh, 16)
            for i, n in enumerate("qkv"):
                sp.dma_start(wqkv1[:, :, D * i:D * i + D], wview(a["L1_mix_W" + n])).then_inc(l_l1, 16)
                sp.dma_start(bias1[:, D * i:D * i + D], row(a["L1_mix_b" + n])).then_inc(l_l1, 16)
            sp.dma_start(b1e_col[:, :, :], a["L1_ffn_b1"].rearrange("e (j p) -> p e j", p=128)).then_inc(l_l1, 16)
            sp.wait_ge(feat0_stored, 80)
            with sp.Fori(0, NS) as s:
                take(sp, xa_used)
                sp.dma_start(x1, rows(a["x"], s)).then_inc(xa_in, 16)
                sp.dma_start(y, rows(feat0, s)).then_inc(xa_in, 16)
                take(sp, rowa_full)
                sp.dma_start(rows(rows_a, s), row_a).then_inc(rowa_free, 16)
            take(sp, loop_a_done)
            sp.dma_start(b1_col[:, :], a["L0_ffn_b1"].rearrange("(j p) -> p j", p=128)).then_inc(l_b1, 16)
            with sp.Fori(0, NS) as s:
                take(sp, rowa_used)
                sp.dma_start(row_a, rows(rows_a, s)).then_inc(rowa_in, 16)
                for e in range(E0):
                    take(sp, w_free[e % 2])
                    sp.dma_start(wd_sb[e % 2], a["L0_ffn_Wd"][e].rearrange("(j p) d -> p j d", p=128)).then_inc(w_full[e % 2], 16)
                take(sp, rowb_full)
                sp.dma_start(rows(rows_b, s), row_b).then_inc(rowb_free, 16)
                take(sp, fout_full)
                sp.dma_start(rows(feat1, s), f_out).then_inc(fout_free, 16)
            take(sp, loop_b_done)
            if dbg is not None:
                sp.dma_start(dbg, rows_b).then_inc(dbg_stored, 16)
                sp.wait_ge(dbg_stored, 16)
            sp.dma_start(wn[:, :, :], wview(a["L1_gnn_weight"])).then_inc(l_c, 16)
            sp.dma_start(wo[:, :, :], wview(a["L1_mix_Wo"])).then_inc(l_c, 16)
            for i, n in enumerate(("L1_gnn_bias", "L1_mix_bo", "L1_mix_b2", "L1_mix_ln1_g", "L1_mix_ln1_b",
                                   "L1_mix_ln2_g", "L1_mix_ln2_b")):
                sp.dma_start(bc[:, i, :], row(a[n])).then_inc(l_c, 16)
            sp.dma_start(w_h[:, :, :], wview(a["L1_mix_W1"])).then_inc(l_c, 16)
            sp.dma_start(b1_col[:, :], a["L1_mix_b1"].rearrange("(j p) -> p j", p=128)).then_inc(l_c, 16)
            sp.dma_start(w2m, a["L1_mix_W2"].rearrange("(j p) n -> p j n", p=128)).then_inc(l_c, 16)
            sp.dma_start(wg[:, 0:KC, :], wview(a["L1_ffn_Wg"])).then_inc(l_c, 16)
            sp.dma_start(bg_bc[:, :], row(a["L1_ffn_bg"])).then_inc(l_c, 16)
            sp.dma_start(bd_sb[:, :], a["L1_ffn_b2"]).then_inc(l_c, 16)
            with sp.Fori(0, NS) as s:
                take(sp, rowb_used)
                sp.dma_start(row_b, rows(rows_b, s)).then_inc(rowb_in, 16)
                for e in range(E1):
                    take(sp, w_free[e % 2])
                    sp.dma_start(w1e_sb[e % 2], wview(a["L1_ffn_W1"][e])).then_inc(w_full[e % 2], 16)
                    sp.dma_start(w2e_sb[e % 2], a["L1_ffn_W2"][e].rearrange("(j p) d -> p j d", p=128)).then_inc(w_full[e % 2], 16)
                take(sp, fout_full)
                sp.dma_start(rows(out, s), f_out).then_inc(fout_free, 16)
            sp.wait_ge(fout_free, 16)

        @block.gpsimd
        def _(pool):
            chain = Chain(pool, idx_full)
            for i, n in enumerate(("dst", "src")):
                pool.dma_start(e_i32[i], a[n].rearrange("(q n) -> q n", q=TR)).then_inc(l_edge, 16)
            pool.dma_start(e_f32[2], a["edge_weight"].rearrange("(q n) -> q n", q=TR)).then_inc(l_edge, 16)
            chain(pool.memset(ident[:, :], 0.0))
            pool.memset(zero_w[:, :], 0.0)
            pool.memset(zero_r[:, :], 0.0)
            pool.memset(ones[:, :], 1.0)
            chain(pool.affine_select(out=ident[:, :], in_=ident[:, :], compare_op=ALU.not_equal, fill=1.0,
                                     base=0, pattern=[[-1, 128]], channel_multiplier=1))
            pool.iota(iota[:, :], [[1, B]], base=0, channel_multiplier=0, allow_small_or_imprecise_dtypes=True)
            pool.iota(base[:, :], [[B, NB]], base=0, channel_multiplier=0, allow_small_or_imprecise_dtypes=True)
            chain(pool.iota(base_col[:, :], [[1, 1]], base=0, channel_multiplier=B, allow_small_or_imprecise_dtypes=True))
            pool.memset(dst_f[:, NT:], -1.0)
            pool.memset(w_f[:, NT:], 0.0)
            chain(pool.memset(src_i[:, NT:], 0))
            chain.restart()
            pool.sem_inc(const_full, 1)
            take(pool, scratch_free)
            pool.iota(t_iot, [[1, NT]], base=0, channel_multiplier=0,
                      allow_small_or_imprecise_dtypes=True).then_inc(tile_iota, 1)
            take(pool, xg_clear)
            chain(pool.memset(xg[:, :, D:D + 1], 1.0))
            chain.restart()
            pool.wait_ge(feat0_stored, 80)
            pool.wait_ge(blk_loaded, 32)

            def gather(b, feat):
                n = pool.value_load(n_tab[0:1, ds(b, 1)], min_val=1, max_val=MAXCH)
                lo = pool.value_load(lo_tab[0:1, ds(b, 1)], min_val=0, max_val=NT - 1)
                with pool.Fori(0, n) as c:
                    t0 = nc.s_assert_within(pool.snap(lo + c * CH), 0, NT - 1,
                                            skip_runtime_bounds_check_because="a block's chunks start inside its span")
                    for k in range(GR):
                        take(pool, xg_free[k])
                        pool.tensor_copy(idx_cur[:, GS * k:GS * k + GS],
                                         src_i[:, ds(t0 + GS * k, GS)]).then_inc(idx_full, 1)
                        take(pool, idx_full)
                        for s in range(GS * k, GS * k + GS):
                            pool.indirect_dma_start(
                                xg[:, s, 0:D], None, feat,
                                bass.IndirectOffsetOnAxis(ap=idx_cur[:, s:s + 1], axis=0)).then_inc(xg_full[k], 16)

            with pool.Fori(0, NB) as b:
                gather(b, feat0)
            take(pool, feat1_done)
            with pool.Fori(0, NB) as b:
                gather(b, feat1)

        @block.tensor
        def _(pe):
            def mm(o, w, r, first, last, check=True):
                return pe.matmul(o, w, r, start=first, stop=last, skip_group_check=not check)

            def zero(ps, cols, start, stop):
                return mm(ps[:, 0:cols], zero_w[:, :], zero_r[:, 0:cols], start, stop, False)

            def turn(ps, at, src, n=B):
                return pe.transpose(ps[:, at:at + n], src, ident[0:n, 0:n])

            def turn_rows(*srcs):
                for i in range(G):
                    take(pe, t_free[i % 2])
                    for n, src in enumerate(srcs):
                        for c in range(KC):
                            last = turn(ps_t[i % 2], B * (KC * n + c), src[:, i, 128 * c:128 * c + 128])
                    last.then_inc(t_act[i % 2], 1)

            def turned(i):
                pe.wait_ge(t_full, i + 1)
                if i == G - 1:
                    pe.sem_clear(t_full)

            def at(k, i):
                return t4[:, k, B * i:B * i + B]

            pe.wait_ge(const_full, 1)
            for s in xg_free + [oh_free, agg_free] + t_free + h_free + y_free + w_free:
                pe.sem_inc(s, 1)
            take(pe, edge_f_full)
            for g in range(6):
                if g >= 2:
                    pe.wait_ge(edge_ps_free, g - 1)
                ps = ps_h[g % 2]
                for c in range(4):
                    last = pe.transpose(ps[0:B, TR * c:TR * c + TR],
                                        e_f32[g // 2][:, B * (4 * (g % 2) + c):B * (4 * (g % 2) + c + 1)],
                                        ident[0:TR, 0:TR])
                last.then_inc(edge_ps_full, 1)
            pe.wait_ge(l_w0, 112)
            take(pe, w_prep)
            for r in range(KC):
                for c in range(KC):
                    last = turn(ps_y[0], 128 * (KC * r + c), wqkvs[:, r, 2 * D + 128 * c:2 * D + 128 * c + 128], 128)
            last.then_inc(w_prep_ps, 1)
            take(pe, w_prep2)
            for r in range(KC):
                for c in range(KC):
                    mm(ps_y[1][:, D * r:D * r + D], t4f[:, 128 * (KC * r + c):128 * (KC * r + c) + 128],
                       wo[:, c, :], c == 0, c == KC - 1)
            for c in range(KC):
                last = mm(ps_t[0][0:B, 0:D], bv_rows[:, c, :], wo[:, c, :], c == 0, c == KC - 1)
            last.then_inc(w_prep_ps, 1)
            zero(ps_kv, NB, True, False)
            with pe.Fori(0, NT // DT // 2) as i:
                for j in range(2):
                    take(pe, deg_full[j])
                    for t in range(DT):
                        last = mm(ps_kv[0:B, 0:NB], oh_lo[j][:, t, :], oh_hi[j][:, t, :], False, False, False)
                    last.then_inc(deg_free[j], 1)
            zero(ps_kv, NB, False, True).then_inc(deg_ps_full, 1)
            take(pe, setup_done)

            def aggregate(b, cols, before):
                first = pe.value_load(cum_tab[0:1, ds(b, 1)], min_val=0, max_val=MAXCH * NB)
                n = pe.value_load(n_tab[0:1, ds(b, 1)], min_val=1, max_val=MAXCH)
                take(pe, agg_free)
                zero(ps_agg, cols, True, False)
                with pe.Fori(0, n) as c:
                    take(pe, oh_full)
                    landed = pe.snap((before + first + c + 1) * (16 * GS))
                    for k in range(GR):
                        pe.wait_ge(xg_full[k], landed)
                        for s in range(GS * k, GS * k + GS):
                            last = mm(ps_agg[0:B, 0:cols], oh[:, s, :], xg[:, s, 0:cols], False, False, False)
                        last.then_inc(xg_free[k], 1)
                    zero(ps_agg, cols, False, False).then_inc(oh_free, 1)
                zero(ps_agg, cols, False, True).then_inc(agg_full, 1)

            def hidden(w, slot, k0=0):
                for j in range(w.shape[2] // 128):
                    for half, (lo, hi) in enumerate(HALVES):
                        take(pe, h_free[half])
                        for c in range(KC):
                            last = mm(ps_h[half][:, 0:hi - lo], w[:, c, 128 * j:128 * j + 128], t4[:, c, lo:hi],
                                      c == 0, c == KC - 1)
                        last.then_inc(h_act[half], 1)

            def gates(lhs, n):
                take(pe, t_free[0])
                for i in range(G):
                    for j in range(n):
                        last = mm(ps_t[0][0:B, 8 * i:8 * i + 8], lhs(j, i), wg[:, j, :], j == 0, j == n - 1)
                last.then_inc(ps_full, 1)

            def gate_bias():
                take(pe, v_full)
                for half, blocks in enumerate((range(4), range(4, G))):
                    take(pe, t_free[half])
                    for i in blocks:
                        last = pe.transpose(ps_t[half][0:8, B * (i % 4):B * (i % 4) + B], gate[:, i, :], ident[0:B, 0:B])
                    last.then_inc(t_act[half], 1)
                pe.wait_ge(t_full, 2)
                pe.sem_clear(t_full)
                for i in range(G):
                    take(pe, y_free[i % 2])
                    mm(ps_y[i % 2][0:B, 0:D], gt[:, B * i:B * i + B], bd_sb[:, :], True, True).then_inc(y_dve[i % 2], 1)

            take(pe, cum_full)
            zero(ps_kv, 512, True, False)
            zero(ps_agg, 2, True, True)
            with pe.Fori(0, NS) as s:
                take(pe, v_full)
                turn_rows(y)
                for i in range(G):
                    turned(i)
                    take(pe, h_free[i % 2])
                    for c in range(KC):
                        last = mm(ps_h[i % 2][0:B, :], at(c, i), wqkvs[:, c, 0:512], c == 0, c == 1)
                    last.then_inc(h_dve[i % 2], 1)
                    take(pe, y_free[i % 2])
                    for c in range(KC):
                        last = mm(ps_y[i % 2][0:B, :], at(c, i), wqkvs[:, c, 512:1024], c == 0, c == 1)
                    last.then_inc(y_dve[i % 2], 1)
                aggregate(s, D, 0)
                take(pe, k4_full)
                take(pe, v_full)
                take(pe, t_free[0])
                for c in range(KC):
                    for i in range(G):
                        last = mm(ps_t[0][:, c:c + 1], ek[:, i, D + 128 * c:D + 128 * c + 128], ones[0:B, 0:1],
                                  i == 0, i == G - 1)
                last.then_inc(ps_full, 1)
                for i in range(G):
                    for c in range(KC):
                        last = mm(ps_kv[:, D * c:D * c + D], ek[:, i, 128 * c:128 * c + 128], f_out[:, i, :],
                                  False, False, False)
                last.then_inc(k4_used, 1)
            zero(ps_kv, 512, False, True).then_inc(sums_full, 1)
            take(pe, v_full)
            take(pe, y_free[0])
            for r in range(KC):
                for c in range(KC):
                    last = turn(ps_y[0], 128 * (KC * r + c), kvf[:, D * r + 128 * c:D * r + 128 * c + 128], 128)
            last.then_inc(y_dve[0], 1)
            take(pe, v_full)
            take(pe, y_free[1])
            for r in range(KC):
                for c in range(KC):
                    last = mm(ps_y[1][:, D * r:D * r + D], t4f[:, 128 * (KC * r + c):128 * (KC * r + c) + 128],
                              wo[:, c, :], c == 0, c == KC - 1)
            last.then_inc(y_dve[1], 1)
            pe.wait_ge(l_wh, 80)
            pe.wait_ge(l_l1, 16 * 7)
            zero(ps_kv, 258, True, False)

            def layer0(s, more):
                def agg(i):
                    if more:
                        aggregate(s * G + G + i, D, 0)

                take(pe, v_full)
                turn_rows(agg_s, row_a[:, :, D:2 * D])
                for i in range(G):
                    turned(i)
                    take(pe, y_free[i % 2])
                    for k, w in enumerate((wn, wn, kvo, kvo)):
                        last = mm(ps_y[i % 2][0:B, 0:D], at(k, i), w[:, k % 2, :], k == 0, k == 3)
                    last.then_inc(y_dve[i % 2], 1)
                agg(0)
                take(pe, v_full)
                turn_rows(y)
                for i in range(G):
                    turned(i)
                hidden(w_h, 0)
                take(pe, ht_full[0])
                gates(lambda j, i: ht[:, j, B * i:B * i + B], J0)
                agg(1)
                gate_bias()
                for e in range(E0):
                    take(pe, w_full[e % 2], 16)
                    for i in range(G):
                        take(pe, y_free[i % 2])
                        for j in range(J0):
                            last = mm(ps_y[i % 2][0:B, 0:D], ht[:, j, B * i:B * i + B], wd_sb[e % 2][:, j, :],
                                      j == 0, j == J0 - 1)
                        last.then_inc(y_dve[i % 2], 1)
                    if e in (2, 5):
                        agg(2 + e // 3)
                agg(4)
                take(pe, v_full)
                turn_rows(row_b[:, :, D:2 * D])
                for i in range(G):
                    turned(i)
                    take(pe, h_free[i % 2])
                    for c in range(KC):
                        last = mm(ps_h[i % 2][0:B, :], at(c, i), wqkv1[:, c, 0:512], c == 0, c == 1)
                    last.then_inc(h_dve[i % 2], 1)
                    take(pe, y_free[i % 2])
                    for c in range(KC):
                        last = mm(ps_y[i % 2][0:B, 0:D], at(c, i), wqkv1[:, c, 512:768], c == 0, c == 1)
                    last.then_inc(y_dve[i % 2], 1)
                take(pe, v_full)
                for i in range(G):
                    for c in range(KC):
                        last = mm(ps_kv[:, 129 * c:129 * c + 129], ek[:, i, 128 * c:128 * c + 128], v1[:, i, c, :],
                                  False, False, False)
                last.then_inc(k4_used, 1)

            with pe.Fori(0, NS - 1) as s:
                layer0(s, True)
            layer0(NS - 1, False)
            zero(ps_kv, 258, False, True).then_inc(sums_full, 1)
            take(pe, v_full)

            total = pe.value_load(cum_tab[0:1, NB:NB + 1], min_val=NB, max_val=MAXCH * NB)
            with pe.Fori(0, G) as i:
                aggregate(i, D + 1, total)
            pe.wait_ge(l_c, 16 * 15)

            def layer1(s, more):
                def agg(i):
                    if more:
                        aggregate(s * G + G + i, D + 1, total)

                take(pe, v_full)
                turn_rows(agg_s, row_b[:, :, 2 * D:3 * D])
                for i in range(G):
                    turned(i)
                    take(pe, h_free[i % 2])
                    for c in range(KC):
                        last = mm(ps_h[i % 2][0:B, 132 * c:132 * c + 132], at(2 + c, i), kvd[:, c, :], True, True)
                    last.then_inc(h_dve[i % 2], 1)
                    take(pe, y_free[i % 2])
                    for c in range(KC):
                        last = mm(ps_y[i % 2][0:B, 0:D], at(c, i), wn[:, c, :], c == 0, c == 1)
                    last.then_inc(y_dve[i % 2], 1)
                agg(0)
                take(pe, v_full)
                turn_rows(y)
                for i in range(G):
                    turned(i)
                    take(pe, y_free[i % 2])
                    for c in range(KC):
                        last = mm(ps_y[i % 2][0:B, 0:D], at(c, i), wo[:, c, :], c == 0, c == 1)
                    last.then_inc(y_dve[i % 2], 1)
                agg(1)
                take(pe, v_full)
                turn_rows(x1)
                for i in range(G):
                    turned(i)
                hidden(w_h, 0)
                take(pe, ht_full[0])
                for i in range(G):
                    take(pe, y_free[i % 2])
                    for j in range(JF):
                        last = mm(ps_y[i % 2][0:B, 0:D], ht[:, j, B * i:B * i + B], w2m[:, j, :], j == 0, j == JF - 1)
                    last.then_inc(y_dve[i % 2], 1)
                agg(2)
                take(pe, v_full)
                turn_rows(y)
                for i in range(G):
                    turned(i)
                gates(lambda j, i: at(j, i), KC)
                for e in range(2):
                    take(pe, w_full[e], 32)
                    hidden(w1e_sb[e], e)
                gate_bias()
                for e in range(E1):
                    take(pe, ht_full[e % 2])
                    for i in range(G):
                        take(pe, y_free[i % 2])
                        for j in range(J1):
                            last = mm(ps_y[i % 2][0:B, 0:D], ht[:, 4 * (e % 2) + j, B * i:B * i + B],
                                      w2e_sb[e % 2][:, j, :], j == 0, j == J1 - 1)
                        last.then_inc(y_dve[i % 2], 1)
                    if e in (2, 4):
                        agg(2 + e // 2)
                    if e + 2 < E1:
                        take(pe, w_full[e % 2], 32)
                        hidden(w1e_sb[e % 2], e % 2)

            with pe.Fori(0, NS - 1) as s:
                layer1(s, True)
            layer1(NS - 1, False)

        @block.scalar
        def _(act):
            chain = Chain(act, act_s)

            def copy_turned(n):
                for i in range(G):
                    take(act, t_act[i % 2])
                    chain(act.activation(t4[:, 0:n, B * i:B * i + B],
                                         ps_t[i % 2][:, 0:n * B].rearrange("p (k n) -> p k n", k=n), ACT.Copy))
                    act.sem_inc(t_free[i % 2], 1)
                    act.sem_inc(t_full, 1)
                chain.restart()

            def copy_gates():
                for half, (lo, hi) in enumerate(((0, 4 * B), (4 * B, G * B))):
                    take(act, t_act[half])
                    chain(act.activation(gt[:, lo:hi], ps_t[half][0:8, 0:hi - lo], ACT.Copy))
                    act.sem_inc(t_free[half], 1)
                    act.sem_inc(t_full, 1)
                chain.restart()

            def root(o):
                take(act, act_in)
                act.activation(o, o, ACT.Sqrt).then_inc(act_out, 1)

            def exp(x):
                take(act, act_in)
                act.activation(x, x, ACT.Exp).then_inc(act_out, 1)

            def units(slot, n, b, func):
                for j in range(n):
                    for half, (lo, hi) in enumerate(HALVES):
                        take(act, h_act[half])
                        last = act.activation(ht[:, slot + j, lo:hi], ps_h[half][:, 0:hi - lo], func, bias=b(j))
                        if j < n - 1 or half == 0:
                            last.then_inc(h_free[half], 1)
                chain(last)
                act.sem_inc(h_free[1], 1)
                act.sem_inc(ht_full[slot // 4], 1)
                chain.restart()

            def keep_aggregate(i):
                take(act, agg_full)
                chain(act.activation(agg_s[:, i, :] if isinstance(i, int) else flat(agg_s[:, ds(i, 1), :]),
                                     ps_agg[0:B, 0:D + 1], ACT.Copy))
                act.sem_inc(agg_free, 1)
                act.sem_inc(aggs_full, 1)
                chain.restart()

            def keep_aggregate0(i):
                take(act, agg_full)
                chain(act.activation(agg_s[:, i, 0:D] if isinstance(i, int) else flat(agg_s[:, ds(i, 1), 0:D]),
                                     ps_agg[0:B, 0:D], ACT.Copy))
                act.sem_inc(agg_free, 1)
                act.sem_inc(aggs_full, 1)
                chain.restart()

            root(rs_all[:, :])
            root(inv_out[:, :])
            with act.Fori(0, NS) as s:
                copy_turned(2)
                take(act, act_in)
                for i in range(G):
                    act.activation(row_b[:, i, 0:D], row_b[:, i, 0:D], ACT.Square, accum_out=st[:, 0, i:i + 1])
                    last = act.activation(row_b[:, i, D:2 * D], row_b[:, i, D:2 * D], ACT.Square,
                                          accum_out=st[:, 1, i:i + 1])
                chain(last)
                for i in range(G):
                    last = act.activation(row_b[:, i, 2 * D:3 * D], row_b[:, i, 0:D], ACT.Square,
                                          accum_out=st[:, 2, i:i + 1])
                chain(last)
                act.activation(st[:, 3, :], st[:, 2, :], ACT.Sqrt).then_inc(act_out, 1)
                chain.restart()
                take(act, act_in)
                act.activation(ek[:, :, D:2 * D], ek[:, :, 0:D], ACT.Square).then_inc(k4_full, 1)
                keep_aggregate0(s)
            root(st2[:, 0:2])
            act.wait_ge(l_b1, 16)

            def layer0(more):
                def agg(i):
                    if more:
                        keep_aggregate0(i)

                copy_turned(4)
                agg(0)
                root(sd[:, :])
                copy_turned(2)
                units(0, J0, lambda j: b1_col[:, j:j + 1], ACT.Gelu)
                exp(lt[:, :, :])
                agg(1)
                copy_gates()
                for i in range(2, G):
                    agg(i)
                root(sd[:, :])
                copy_turned(2)
                exp(ek[:, :, :])

            with act.Fori(0, NS - 1) as s:
                layer0(True)
            layer0(False)
            with act.Fori(0, G) as i:
                keep_aggregate(i)
            act.wait_ge(l_c, 16 * 15)
            act.wait_ge(l_l1, 16 * 7)

            def layer1(more):
                def agg(i):
                    if more:
                        keep_aggregate(i)

                root(sd[:, :])
                copy_turned(4)
                agg(0)
                copy_turned(2)
                exp(row_a[:, :, D:2 * D])
                agg(1)
                root(sd[:, :])
                copy_turned(2)
                units(0, JF, lambda j: b1_col[:, j:j + 1], ACT.Relu)
                agg(2)
                root(sd[:, :])
                root(sd[:, :])
                copy_turned(2)
                for e in range(E1):
                    units(4 * (e % 2), J1, lambda j, e=e: b1e_col[:, e, j:j + 1], ACT.Gelu)
                    if e == 1:
                        copy_gates()
                    if e in (4, 6):
                        agg(1 + e // 2)

            with act.Fori(0, NS - 1) as s:
                layer1(True)
            layer1(False)

        @block.vector
        def _(dve):
            chain = Chain(dve, dve_s)
            ts, tt, stt = dve.tensor_scalar, dve.tensor_tensor, dve.scalar_tensor_tensor

            def root():
                dve.sem_inc(act_in, 1)
                take(dve, act_out)

            def each(op, full, free):
                for i in range(G):
                    take(dve, full[i % 2])
                    last = op(i)
                    if i < G - 1:
                        last.then_inc(free[i % 2], 1)
                chain(last)
                dve.sem_inc(free[(G - 1) % 2], 1)

            def across(t):
                return t.unsqueeze(1).to_broadcast([B, G, D])

            def norm(dst, src, g=None, beta=None):
                for i in range(G):
                    last = dve.bn_stats(bn6[:, i, :], src[:, i, :])
                chain(last)
                for i in range(G):
                    last = dve.bn_aggr(mv[:, i, :], bn6[:, i, :])
                chain(last)
                chain(ts(sd[:, :], mv[:, :, 1], LN_EPS, None, ALU.add))
                root()
                chain(dve.reciprocal(rs[:, :], sd[:, :]))
                for i in range(G):
                    last = ts(dst[:, i, :], src[:, i, :], mv[:, i, 0:1], rs[:, i:i + 1], ALU.subtract, ALU.mult)
                chain(last)
                if g is not None:
                    chain(tt(dst, dst, across(g), ALU.mult))
                    chain(tt(dst, dst, across(beta), ALU.add))

            dve.wait_ge(const_full, 1)
            dve.wait_ge(l_x, 80)
            with dve.Fori(0, NS) as s:
                for i in range(G):
                    last = dve.bn_stats(bn6[:, i, :], flat(x_big[:, ds(s * G + i, 1), :]))
                chain(last)
                for i in range(G):
                    last = dve.bn_aggr(mv[:, i, :], bn6[:, i, :])
                chain(last)
                chain(dve.tensor_copy(mv_all[:, ds(s * G, G), :], mv[:, :, :]))
                chain.restart()
            chain(ts(rs_all[:, :], mv_all[:, :, 1], LN_EPS, None, ALU.add))
            root()
            chain(dve.reciprocal(rs_all[:, :], rs_all[:, :]))
            chain.restart()
            with dve.Fori(0, NB) as b:
                ts(flat(x_big[:, ds(b, 1), :]), flat(x_big[:, ds(b, 1), :]), flat(mv_all[:, ds(b, 1), 0:1]),
                   rs_all[:, ds(b, 1)], ALU.subtract, ALU.mult)
            chain(dve.memset(sd[:, :], 0.0))
            dve.sem_inc(feat0_full, 1)
            dve.wait_ge(l_edge, 48)
            dve.tensor_copy(e_f32[0], e_i32[0])
            chain(dve.tensor_copy(e_f32[1], e_i32[1]))
            dve.sem_inc(edge_f_full, 1)
            dv = e_f32[0].rearrange("q (c e) -> q c e", c=TC)
            dve.tensor_reduce(st_min[:, :], dv, AX.X, ALU.min)
            chain(dve.tensor_reduce(st_max[:, :], dv, AX.X, ALU.max))
            dve.sem_inc(minmax_full, 1)
            for g in range(6):
                dve.wait_ge(edge_ps_full, g + 1)
                ps = ps_h[g % 2][0:B, 0:4 * TR].rearrange("p (c q) -> p c q", c=4)
                c0 = 4 * (g % 2)
                view = lambda t: t[:, 0:NT].rearrange("p (q c) -> p c q", c=TC)[:, c0:c0 + 4, :]
                if g // 2 == 1:
                    dve.tensor_copy(view(src_i), ps)
                chain(dve.tensor_copy(view((dst_f, src_f, w_f)[g // 2]), ps))
                if g < 4:
                    dve.sem_inc(edge_ps_free, 1)
            dve.wait_ge(minmax_stored, 32)
            dve.sem_inc(scratch_free, 1)
            dve.sem_inc(tabs_full, 1)
            big = 12582912.0
            chain(ts(src_hi, src_f, 1.0 / B, 0.004 - 0.5, ALU.mult, ALU.add))
            chain(ts(src_hi, src_hi, big, -big, ALU.add, ALU.add))
            chain(stt(out=src_lo, in0=src_hi, scalar=-float(B), in1=src_f, op0=ALU.mult, op1=ALU.add))
            dve.wait_ge(minmax_loaded, 32)
            take(dve, tile_iota)
            chain(ts(t_msk, t_max, base_col[:, 0:1], None, ALU.is_ge))
            chain(ts(t_min, t_min, base_col[:, 0:1], float(B), ALU.subtract, ALU.is_lt))
            chain(tt(t_msk, t_msk, t_min, ALU.mult))
            chain(tt(t_val, t_msk, t_iot, ALU.mult))
            chain(dve.tensor_reduce(blk[:, 1:2], t_val, AX.X, ALU.max))
            chain(ts(t_msk, t_msk, -10000.0, 10000.0, ALU.mult, ALU.add))
            chain(tt(t_val, t_val, t_msk, ALU.add))
            chain(dve.tensor_reduce(blk[:, 0:1], t_val, AX.X, ALU.min))
            chain(ts(blk[:, 2:3], blk[:, 0:1], 9000.0, None, ALU.is_lt))
            chain(tt(blk[:, 0:1], blk[:, 0:1], blk[:, 2:3], ALU.mult))
            chain(tt(blk[:, 1:2], blk[:, 1:2], blk[:, 0:1], ALU.subtract))
            chain(ts(t_msk[:, 0:MAXCH], t_iot[:, 0:MAXCH], float(CH), float(CH), ALU.mult, ALU.add))
            chain(ts(t_msk[:, 0:MAXCH], t_msk[:, 0:MAXCH], blk[:, 1:2], None, ALU.is_le))
            chain(dve.tensor_reduce(blk[:, 2:3], t_msk[:, 0:MAXCH], AX.X, ALU.add))
            chain(ts(blk[:, 1:2], blk[:, 2:3], 1.0, None, ALU.add))
            chain(dve.tensor_copy(blk_i[:, 0:2], blk[:, 0:2]))
            dve.sem_inc(blk_full, 1)
            chain.restart()
            dve.wait_ge(l_w0, 112)
            dve.sem_inc(w_prep, 1)
            wq4 = wqkvs[:, :, 0:512].rearrange("p c (h n) -> p c h n", h=2)
            chain(dve.tensor_reduce(st4, wq4, AX.X, ALU.add))
            chain(ts(st4, st4, 1.0 / D, None, ALU.mult))
            chain(tt(wq4, wq4, st4.unsqueeze(3).to_broadcast([128, KC, 2, D]), ALU.subtract))
            bq2 = bias0[:, 0:512].rearrange("p (h n) -> p h n", h=2)
            chain(dve.tensor_reduce(st[:, 0, 0:2], bq2, AX.X, ALU.add))
            chain(ts(st[:, 0, 0:2], st[:, 0, 0:2], 1.0 / D, None, ALU.mult))
            chain(tt(bq2, bq2, st[:, 0, 0:2].unsqueeze(2).to_broadcast([B, 2, D]), ALU.subtract))
            take(dve, w_prep_ps)
            for c in range(KC):
                ts(bv_rows[:, c, :], ones[:, :], b1_col[:, c:c + 1], None, ALU.mult)
            chain(dve.tensor_copy(t4f, ps_y[0][:, :]))
            dve.sem_inc(w_prep2, 1)
            take(dve, w_prep_ps)
            sv = wqkvs[:, :, 3 * D:4 * D]
            chain(tt(sv, sv, ps_y[1][:, :].rearrange("p (c n) -> p c n", c=KC), ALU.add))
            chain(tt(b_tmp[:, :], b_tmp[:, :], ps_t[0][0:B, 0:D], ALU.add))
            chain(tt(bias0[:, 3 * D:], bias0[:, 3 * D:], b_tmp[:, :], ALU.add))
            chain.restart()
            for j in range(2):
                dve.sem_inc(deg_free[j], 1)
            with dve.Fori(0, NT // DT // 2) as i:
                for j in range(2):
                    take(dve, deg_free[j])
                    t0 = i * 2 * DT + j * DT
                    for o, dig, n in ((oh_lo[j], src_lo, B), (oh_hi[j], src_hi, NB)):
                        last = tt(o, iota[:, 0:n].unsqueeze(1).to_broadcast([B, DT, n]),
                                  dig[:, ds(t0, DT)].unsqueeze(2).to_broadcast([B, DT, n]), ALU.is_equal)
                    last.then_inc(deg_full[j], 1)
            take(dve, deg_ps_full)
            dve.sem_inc(xg_clear, 1)
            chain(ts(inv_out[:, :], ps_kv[0:B, 0:NB], 1.0, None, ALU.max))
            root()
            chain(dve.reciprocal(inv_out[:, :], inv_out[:, :]))
            dve.wait_ge(blk_loaded, 32)
            chain(dve.memset(cum_f[:, :], 0.0))
            chain(dve.tensor_copy(n_f[:, :], n_tab[:, :]))
            chain(dve.tensor_tensor_scan(cum_f[:, 1:NB + 1], ones[0:1, 0:NB], n_f[:, :], 0.0, ALU.mult, ALU.add))
            chain(dve.tensor_copy(cum_tab[:, :], cum_f[:, :]))
            dve.sem_inc(cum_full, 1)
            chain(dve.memset(st2[:, :], 0.0))
            dve.sem_inc(setup_done, 1)
            dve.sem_inc(xa_used, 1)
            chain.restart()

            def onehots(b, weighted):
                n = dve.value_load(n_tab[0:1, ds(b, 1)], min_val=1, max_val=MAXCH)
                lo = dve.value_load(lo_tab[0:1, ds(b, 1)], min_val=0, max_val=NT - 1)
                chain.restart()
                with dve.Fori(0, n) as c:
                    t0 = nc.s_assert_within(dve.snap(lo + c * CH), 0, NT - 1,
                                            skip_runtime_bounds_check_because="a block's chunks start inside its span")
                    take(dve, oh_free)
                    if weighted:
                        dve.tensor_copy(w_cur[:, :], w_f[:, ds(t0, CH)])
                    chain(ts(dst_cur[:, :], dst_f[:, ds(t0, CH)], base[:, ds(b, 1)], None, ALU.subtract))
                    for s in range(CH):
                        if weighted:
                            last = ts(oh[:, s, :], iota[:, :], dst_cur[:, s:s + 1], w_cur[:, s:s + 1],
                                      ALU.is_equal, ALU.mult)
                        else:
                            last = ts(oh[:, s, :], iota[:, :], dst_cur[:, s:s + 1], None, ALU.is_equal)
                    last.then_inc(oh_full, 1)
                    chain.restart()

            def wide(t):
                return t.unsqueeze(2).to_broadcast([B, G, 8])

            def first_max(src, mask):
                chain(dve.tensor_reduce(st[:, 1, :], src, AX.X, ALU.max))
                chain(tt(mask, src, wide(st[:, 1, :]), ALU.is_ge))
                chain(stt(out=mask, in0=mask, scalar=-8.0, in1=iota[:, 0:8].unsqueeze(1).to_broadcast([B, G, 8]),
                          op0=ALU.mult, op1=ALU.add))
                chain(dve.tensor_reduce(st[:, 2, :], mask, AX.X, ALU.min))
                chain(tt(mask, mask, wide(st[:, 2, :]), ALU.is_equal))

            with dve.Fori(0, NS) as s:
                onehots(s, True)
                take(dve, xa_in, 32)
                dve.sem_inc(v_full, 1)
                for i in range(G):
                    take(dve, h_dve[i % 2])
                    tt(row_b[:, i, 0:512], ps_h[i % 2][0:B, :], bias0[:, 0:512], ALU.add).then_inc(h_free[i % 2], 1)
                    take(dve, y_dve[i % 2])
                    if i == 0:
                        take(dve, rowa_free, 16)
                    tt(f_out[:, i, :], ps_y[i % 2][0:B, 0:D], bias0[:, 2 * D:3 * D], ALU.add)
                    last = tt(row_a[:, i, 0:D], ps_y[i % 2][0:B, D:2 * D], bias0[:, 3 * D:4 * D], ALU.add)
                    if i < G - 1:
                        last.then_inc(y_free[i % 2], 1)
                chain(last)
                dve.sem_inc(y_free[0], 1)
                dve.sem_inc(act_in, 1)
                chain(tt(row_a[:, :, 0:D], row_a[:, :, 0:D], x1, ALU.add))
                take(dve, act_out)
                chain(ts(st[:, 4:6, :], st[:, 0:2, :], 1e-7, None, ALU.add))
                chain(dve.reciprocal(st[:, 6:8, :], st[:, 4:6, :]))
                chain(tt(st[:, 8, :], st[:, 6, :], st[:, 3, :], ALU.mult))
                chain(ts(st[:, 9, :], st[:, 8, :], 1e-12, None, ALU.max))
                chain(dve.reciprocal(st[:, 10, :], st[:, 9, :]))
                chain(tt(st[:, 11, :], st[:, 10, :], st[:, 6, :], ALU.mult))
                for i in range(G):
                    last = ts(ek[:, i, 0:D], row_b[:, i, D:2 * D], st[:, 7, i:i + 1], None, ALU.mult)
                chain(last)
                dve.sem_inc(act_in, 1)
                dve.sem_inc(v_full, 1)
                for i in range(G):
                    last = ts(row_a[:, i, D:2 * D], row_b[:, i, 0:D], st[:, 11, i:i + 1], None, ALU.mult)
                chain(last)
                dve.sem_inc(rowa_full, 1)
                take(dve, ps_full)
                chain(tt(st2[:, 0:2], st2[:, 0:2], ps_t[0][:, 0:2], ALU.add))
                dve.sem_inc(t_free[0], 1)
                take(dve, k4_used)
                dve.sem_inc(xa_used, 1)
                chain.restart()
            take(dve, sums_full)
            dve.sem_inc(loop_a_done, 1)
            root()
            chain(ts(st2[:, 0:2], st2[:, 0:2], 1e-12, None, ALU.max))
            chain(dve.reciprocal(st2[:, 0:2], st2[:, 0:2]))
            for c in range(KC):
                last = ts(kvf[:, D * c:D * c + D], ps_kv[:, D * c:D * c + D], st2[:, c:c + 1], 1.0 / math.sqrt(N),
                          ALU.mult, ALU.mult)
            chain(last)
            dve.sem_inc(v_full, 1)
            take(dve, y_dve[0])
            chain(dve.tensor_copy(t4f, ps_y[0][:, :]))
            dve.sem_inc(y_free[0], 1)
            dve.sem_inc(v_full, 1)
            take(dve, y_dve[1])
            chain(dve.tensor_copy(kvo[:, :, :], ps_y[1][:, :].rearrange("p (c n) -> p c n", c=KC)))
            dve.sem_inc(y_free[1], 1)
            take(dve, rowa_free, 16)
            dve.sem_inc(rowa_used, 1)
            dve.wait_ge(aggs_full, G)
            dve.sem_clear(aggs_full)
            dve.wait_ge(l_wh, 80)
            dve.wait_ge(l_l1, 16 * 7)
            chain.restart()

            def experts(acc, n, agg_after, s):
                for e in range(n):
                    each(lambda i: stt(out=acc[:, i, :], in0=ps_y[i % 2][0:B, 0:D], scalar=gate[:, i, e:e + 1],
                                       in1=acc[:, i, :], op0=ALU.mult, op1=ALU.add), y_dve, y_free)
                    dve.sem_inc(w_free[e % 2], 1)
                    if e in agg_after:
                        onehots(s * G + G + agg_after[e], n_weighted[0])

            n_weighted = [True]

            def layer0(s, more):
                def hots(i):
                    if more:
                        onehots(s * G + G + i, True)

                take(dve, rowa_in, 16)
                dve.sem_inc(v_full, 1)
                hots(0)
                each(lambda i: tt(x1[:, i, :], ps_y[i % 2][0:B, 0:D], row_a[:, i, 0:D], ALU.add), y_dve, y_free)
                norm(y, x1)
                dve.sem_inc(v_full, 1)
                hots(1)
                take(dve, ps_full)
                pg = ps_t[0][0:B, 0:8 * G].rearrange("p (i e) -> p i e", i=G)
                chain(tt(lg[:, :, :], pg, bg_bc[:, :].unsqueeze(1).to_broadcast([B, G, 8]), ALU.add))
                dve.sem_inc(t_free[0], 1)
                chain(dve.tensor_reduce(st[:, 1, :], lg[:, :, :], AX.X, ALU.max))
                chain(tt(lt[:, :, :], lg[:, :, :], wide(st[:, 1, :]), ALU.subtract))
                dve.sem_inc(act_in, 1)
                take(dve, act_out)
                chain(dve.tensor_reduce(st[:, 0, :], lt[:, :, :], AX.X, ALU.add))
                chain(dve.reciprocal(st[:, 3, :], st[:, 0, :]))
                chain(tt(lt[:, :, :], lt[:, :, :], wide(st[:, 3, :]), ALU.mult))
                first_max(lt[:, :, :], lu[:, :, :])
                chain(tt(gate[:, :, :], lt[:, :, :], lu[:, :, :], ALU.mult))
                dve.sem_inc(v_full, 1)
                take(dve, rowb_free, 16)
                x2 = row_b[:, :, 0:D]
                each(lambda i: tt(x2[:, i, :], ps_y[i % 2][0:B, 0:D], x1[:, i, :], ALU.add), y_dve, y_free)
                experts(x2, E0, {1: 2, 4: 3, 6: 4} if more else {}, s)
                norm(row_b[:, :, D:2 * D], x2)
                dve.sem_inc(v_full, 1)
                take(dve, fout_free, 16)
                iv = inv_out[:, ds(s * G, G)].unsqueeze(2).to_broadcast([B, G, D])
                chain(tt(f_out, row_b[:, :, D:2 * D], iv, ALU.mult))
                dve.sem_inc(fout_full, 1)
                dve.memset(v1[:, :, :, 128:129], 1.0)
                for i in range(G):
                    take(dve, h_dve[i % 2])
                    tt(row_a[:, i, :], ps_h[i % 2][0:B, :], bias1[:, 0:512], ALU.add).then_inc(h_free[i % 2], 1)
                    take(dve, y_dve[i % 2])
                    last = tt(v1[:, i, :, 0:128], ps_y[i % 2][0:B, 0:D].rearrange("p (c n) -> p c n", c=2),
                              bias1[:, 2 * D:3 * D].rearrange("p (c n) -> p c n", c=2), ALU.add)
                    if i < G - 1:
                        last.then_inc(y_free[i % 2], 1)
                chain(last)
                dve.sem_inc(y_free[0], 1)
                chain(ts(ek, row_a, 0.0, None, ALU.min))
                dve.sem_inc(act_in, 1)
                take(dve, act_out)
                chain(stt(out=row_b[:, :, 2 * D:3 * D], in0=row_a[:, :, 0:D], scalar=0.0, in1=ek[:, :, 0:D],
                          op0=ALU.max, op1=ALU.add))
                dve.sem_inc(rowb_full, 1)
                chain(stt(out=ek[:, :, 0:D], in0=row_a[:, :, D:2 * D], scalar=0.0, in1=ek[:, :, D:2 * D],
                          op0=ALU.max, op1=ALU.add))
                dve.sem_inc(v_full, 1)
                dve.sem_inc(rowa_used, 1)
                take(dve, k4_used)
                if more:
                    dve.wait_ge(aggs_full, G)
                    dve.sem_clear(aggs_full)
                chain.restart()

            with dve.Fori(0, NS - 1) as s:
                layer0(s, True)
            layer0(NS - 1, False)
            take(dve, sums_full)
            take(dve, rowb_free, 16)
            take(dve, fout_free, 16)
            dve.sem_inc(feat1_done, 1)
            dve.sem_inc(loop_b_done, 1)
            dve.sem_inc(rowb_used, 1)
            dve.sem_inc(fout_free, 16)
            chain(dve.memset(kvd[:, :, :], 0.0))
            for h in range(4):
                p = slice(DH * h, DH * h + DH)
                kv = ps_kv[p, 0:258].rearrange("p (c n) -> p c n", c=KC)
                dve.tensor_copy(kvd[p, :, DH * h:DH * h + DH], kv[:, :, DH * h:DH * h + DH])
                last = dve.tensor_copy(kvd[p, :, 128 + h:129 + h], kv[:, :, 128:129])
            chain(last)
            dve.sem_inc(v_full, 1)
            chain.restart()

            n_weighted[0] = False
            with dve.Fori(0, G) as i:
                onehots(i, False)
            dve.wait_ge(aggs_full, G)
            dve.sem_clear(aggs_full)
            dve.wait_ge(l_c, 16 * 15)

            def layer1(s, more):
                def hots(i):
                    if more:
                        onehots(s * G + G + i, False)

                chain(ts(sd[:, :], agg_s[:, :, D], 1.0, None, ALU.max))
                root()
                chain(dve.reciprocal(rs[:, :], sd[:, :]))
                for i in range(G):
                    last = ts(agg_s[:, i, 0:D], agg_s[:, i, 0:D], rs[:, i:i + 1], None, ALU.mult)
                chain(last)
                take(dve, rowb_in, 16)
                dve.sem_inc(v_full, 1)
                hots(0)
                for i in range(G):
                    take(dve, h_dve[i % 2])
                    num = ps_h[i % 2][0:B, 0:264].rearrange("p (c n) -> p c n", c=KC)
                    chain(ts(lt[:, i, :].rearrange("p (c h) -> p c h", c=KC), num[:, :, 128:132], 1e-6, None, ALU.add))
                    chain(dve.reciprocal(lt[:, i, :], lt[:, i, :]))
                    for c in range(KC):
                        last = tt(y[:, i, 128 * c:128 * c + 128].rearrange("p (h n) -> p h n", h=4),
                                  num[:, c, 0:128].rearrange("p (h n) -> p h n", h=4),
                                  lt[:, i, 4 * c:4 * c + 4].unsqueeze(2).to_broadcast([B, 4, DH]), ALU.mult)
                    last.then_inc(h_free[i % 2], 1)
                    take(dve, y_dve[i % 2])
                    last = tt(row_a[:, i, 0:D], ps_y[i % 2][0:B, 0:D], bc[:, 0, :], ALU.add)
                    if i < G - 1:
                        last.then_inc(y_free[i % 2], 1)
                chain(last)
                dve.sem_inc(y_free[0], 1)
                dve.sem_inc(v_full, 1)
                chain(ts(row_a[:, :, D:2 * D], row_a[:, :, 0:D], 0.0, None, ALU.min))
                dve.sem_inc(act_in, 1)
                hots(1)
                each(lambda i: tt(x1[:, i, :], ps_y[i % 2][0:B, 0:D], row_b[:, i, D:2 * D], ALU.add), y_dve, y_free)
                chain(tt(x1, x1, across(bc[:, 1, :]), ALU.add))
                take(dve, act_out)
                norm(x1, x1, bc[:, 3, :], bc[:, 4, :])
                dve.sem_inc(v_full, 1)
                chain(stt(out=row_a[:, :, 0:D], in0=row_a[:, :, 0:D], scalar=0.0, in1=row_a[:, :, D:2 * D],
                          op0=ALU.max, op1=ALU.add))
                chain(stt(out=row_b[:, :, 0:D], in0=row_a[:, :, 0:D], scalar=-1.0, in1=row_b[:, :, 0:D],
                          op0=ALU.add, op1=ALU.add))
                hots(2)
                each(lambda i: tt(y[:, i, :], ps_y[i % 2][0:B, 0:D], x1[:, i, :], ALU.add), y_dve, y_free)
                chain(tt(y, y, across(bc[:, 2, :]), ALU.add))
                norm(y, y, bc[:, 5, :], bc[:, 6, :])
                chain(tt(x1, y, row_b[:, :, 0:D], ALU.add))
                norm(y, x1)
                dve.sem_inc(v_full, 1)
                take(dve, ps_full)
                pg = ps_t[0][0:B, 0:8 * G].rearrange("p (i e) -> p i e", i=G)
                chain(tt(lg[:, :, :], pg, bg_bc[:, :].unsqueeze(1).to_broadcast([B, G, 8]), ALU.add))
                dve.sem_inc(t_free[0], 1)
                first_max(lg[:, :, :], lt[:, :, :])
                chain(stt(out=lg[:, :, :], in0=lt[:, :, :], scalar=-3.0e38, in1=lg[:, :, :], op0=ALU.mult, op1=ALU.add))
                first_max(lg[:, :, :], lu[:, :, :])
                chain(tt(gate[:, :, :], lt[:, :, :], lu[:, :, :], ALU.add))
                dve.sem_inc(v_full, 1)
                take(dve, fout_free, 16)
                each(lambda i: tt(f_out[:, i, :], ps_y[i % 2][0:B, 0:D], x1[:, i, :], ALU.add), y_dve, y_free)
                experts(f_out, E1, {1: 3, 3: 4} if more else {}, s)
                dve.sem_inc(fout_full, 1)
                dve.sem_inc(rowb_used, 1)
                if more:
                    dve.wait_ge(aggs_full, G)
                    dve.sem_clear(aggs_full)
                chain.restart()

            with dve.Fori(0, NS - 1) as s:
                layer1(s, True)
            layer1(NS - 1, False)


_NAMES = """x src dst edge_weight L0_gnn_W_self L0_gnn_W_neighbor L0_gnn_bias L0_mix_W_qkv L0_mix_b_qkv
L0_mix_W_out L0_mix_b_out L0_ffn_W1 L0_ffn_b1 L0_ffn_Wg L0_ffn_bg L0_ffn_Wd L0_ffn_bd L1_gnn_weight
L1_gnn_bias L1_mix_Wq L1_mix_bq L1_mix_Wk L1_mix_bk L1_mix_Wv L1_mix_bv L1_mix_Wo L1_mix_bo L1_mix_W1
L1_mix_b1 L1_mix_W2 L1_mix_b2 L1_mix_ln1_g L1_mix_ln1_b L1_mix_ln2_g L1_mix_ln2_b L1_ffn_Wg L1_ffn_bg
L1_ffn_W1 L1_ffn_b1 L1_ffn_W2 L1_ffn_b2""".split()


def kernel(**inputs):
    import numpy as np
    import concourse.bacc as bacc
    from concourse.bass_utils import run_bass_kernel_spmd

    nc = bacc.Bacc("TRN2", target_bir_lowering=False, num_devices=1)
    arrays, aps = {}, {}
    for name in _NAMES:
        v = np.ascontiguousarray(inputs[name])
        arrays["in_" + name] = v
        aps[name] = nc.dram_tensor("in_" + name, v.shape, mybir.dt.from_np(v.dtype), kind="ExternalInput").ap()
    out = nc.dram_tensor("out_rows", (N, D), F32, kind="ExternalOutput").ap()
    program(nc, aps, out)
    r = run_bass_kernel_spmd(nc, [arrays], core_ids=[0])
    return r.results[0]["out_rows"]
```

```python
import math
from contextlib import ExitStack

import concourse.bass as bass
from concourse import mybir

F32 = mybir.dt.float32
BF16 = mybir.dt.bfloat16
I32 = mybir.dt.int32
ALU = mybir.AluOpType
ACT = mybir.ActivationFunctionType
AX = mybir.AxisListType

N, E, D = 3125, 100000, 256
B = 125
NB = N // B
NT = E // B
KC = D // 128
GS, GR = 7, 5
CH = GS * GR
NTP = NT + CH
MAXCH = -(-NT // CH)
TR, TC = 100, NT // 100
H0, E0 = 1024, 8
H1, E1 = 512, 8
J0, J1 = H0 // 128, H1 // 128
FF = 1024
JF = FF // 128
DH = 32
LN_EPS = 1e-5
G = 5
NS = NB // G
HALVES = ((0, 3 * B), (3 * B, G * B))
PT = 2 * B
MAXP = -(-N // PT)
CAP = N + PT
ALLP = 2 * N // PT + E0
DT = 20
AA, AB = 2, 4
FOUR, TWO, AG = (0, 2, 3, 4), (2, 3), 3
AC = 2 * len(FOUR)
AP = len(TWO) + AG
AR = NB - AC - AP * (NS - 2)
ds = bass.ds


def take(eng, sem, n=1):
    eng.wait_ge(sem, n)
    eng.sem_clear(sem)


class Chain:

    def __init__(self, eng, sem):
        self.eng, self.sem, self.n = eng, sem, 0

    def __call__(self, ins):
        ins.then_inc(self.sem, 1)
        self.n += 1
        self.eng.wait_ge(self.sem, self.n)

    def restart(self):
        if self.n:
            self.eng.sem_clear(self.sem)
        self.n = 0


def program(nc, a, out):
    ctx = ExitStack()
    with ctx:
        def sb(name, shape, dt=F32):
            return ctx.enter_context(nc.sbuf_tensor(name, shape, dt))

        def sem(name):
            return ctx.enter_context(nc.semaphore(name))

        def pair(name):
            return [sem(name + "0"), sem(name + "1")]

        banks = [ctx.enter_context(nc.psum_tensor(f"bank{i}", [128, 512], F32)) for i in range(8)]
        ps_agg, ps_kv = banks[0], banks[7]
        ps_t, ps_h, ps_y = banks[1:3], banks[3:5], banks[5:7]

        feat0 = nc.dram_tensor("feat0", (N, D), F32).ap()
        feat1 = nc.dram_tensor("feat1", (N, D), F32).ap()
        rows_a = nc.dram_tensor("rows_a", (N, 2 * D), F32).ap()
        rows_b = nc.dram_tensor("rows_b", (N, 3 * D), F32).ap()
        agg_rows0 = nc.dram_tensor("agg_rows0", (N, D), F32).ap()
        agg_rows1 = nc.dram_tensor("agg_rows1", (N, D + 1), F32).ap()
        rows_x = nc.dram_tensor("rows_x", (N, D), F32).ap()
        sorted_in = nc.dram_tensor("sorted_in", (E0 * CAP, D), F32).ap()
        sorted_out = nc.dram_tensor("sorted_out", (ALLP * PT, D), F32).ap()
        tile_min = nc.dram_tensor("tile_min", (TR, TC), F32).ap()
        tile_max = nc.dram_tensor("tile_max", (TR, TC), F32).ap()
        block_lo = nc.dram_tensor("block_lo", (NB, 1), I32).ap()
        block_n = nc.dram_tensor("block_n", (NB, 1), I32).ap()

        ident = sb("ident", [128, 128])
        iota = sb("iota", [B, B])
        base = sb("base", [B, NB])
        base_col = sb("base_col", [NB, 1])
        ones = sb("ones", [128, B])
        upper = sb("upper", [B, B])
        next_col = sb("next_col", [B, 1])
        zeros = sb("zeros", [B, D])
        region = sb("region", [B, E0])
        pair_at = sb("pair_at", [B, MAXP])
        zero_w = sb("zero_w", [1, 128], BF16)
        zero_r = sb("zero_r", [1, 512], BF16)

        dst_f = sb("dst_f", [B, NTP])
        w_f = sb("w_f", [B, NTP])
        src_i = sb("src_i", [B, NTP], I32)
        lo_tab = sb("lo_tab", [1, NB], I32)
        n_tab = sb("n_tab", [1, NB], I32)
        cum_tab = sb("cum_tab", [1, NB + 1], I32)
        cum_f = sb("cum_f", [1, NB + 1])
        n_f = sb("n_f", [1, NB])
        idx_cur = sb("idx_cur", [B, CH], I32)
        dst_cur = sb("dst_cur", [B, CH])
        w_cur = sb("w_cur", [B, CH])
        xg = sb("xg", [B, CH, D + 1])
        oh = sb("oh", [B, CH, B])
        inv_out = sb("inv_out", [B, NB])

        pos_f = sb("pos_f", [B, 2, NB])
        pos_up = sb("pos_up", [B, 2, NB])
        pos_out = sb("pos_out", [B, 2, NB])
        pos_tab = sb("pos_tab", [B, 2, NB], I32)
        pos_cur = sb("pos_cur", [B, 2, G], I32)
        pos_get = [sb(f"pos_get{j}", [B, 2, G], I32) for j in range(2)]
        p_tab = sb("p_tab", [B, NB])
        p_cur = sb("p_cur", [B, G])
        cnt = sb("cnt", [B, E0])
        count = sb("count", [B, E0])
        pair_msk = sb("pair_msk", [B, E0, MAXP])
        pairs_f = sb("pairs_f", [B, E0])
        before_f = sb("before_f", [B, E0 + 1])
        shift = sb("shift", [B, E0])
        before_tab = sb("before_tab", [1, E0], I32)
        tail_tab = sb("tail_tab", [1, E0], I32)
        pair_tab = sb("pair_tab", [1, E0], I32)

        w_exp = [sb(f"w_exp{i}", [128, 2 * KC * H1]) for i in range(2)]
        wd_sb = [w[:, :].rearrange("p (j d) -> p j d", j=J0) for w in w_exp]
        w1e_sb = [w[:, 0:KC * H1].rearrange("p (c h) -> p c h", c=KC) for w in w_exp]
        w2e_sb = [w[:, KC * H1:].rearrange("p (j d) -> p j d", j=J1) for w in w_exp]
        w_h = sb("w_h", [128, KC, H0])
        w_x = sb("w_x", [128, 8 * D])
        wqkvs = w_x[:, :].rearrange("p (c n) -> p c n", c=KC)
        w2m = w_x[:, :].rearrange("p (j n) -> p j n", j=JF)
        wqkv1 = sb("wqkv1", [128, KC, 3 * D])
        wn = sb("wn", [128, KC, D])
        wo = sb("wo", [128, KC, D])
        kvo = sb("kvo", [128, KC, D])
        kvd = sb("kvd", [128, KC, 132])
        wg = sb("wg", [128, J0, E0])
        be = sb("be", [B, 2, D])
        b1_col = sb("b1_col", [128, J0])
        b1e_col = sb("b1e_col", [128, E1, J1])
        bias = sb("bias", [B, 7, D])
        bias_f = bias[:, :, :].rearrange("p k d -> p (k d)")
        bias0 = bias_f[:, 0:4 * D]
        bias1 = bias_f[:, 4 * D:7 * D]
        bc = bias
        bg_bc = sb("bg_bc", [B, E0])

        arena = sb("arena", [128, 19020])

        def cut(at, n, parts=B):
            return arena[0:parts, at:at + n]

        row_a = cut(0, 2560).rearrange("p (i n) -> p i n", i=G)
        row_b = cut(2560, 3840).rearrange("p (i n) -> p i n", i=G)
        x1, y, f_out = (cut(n, 1280).rearrange("p (i n) -> p i n", i=G) for n in (6400, 7680, 8960))
        x_in = cut(8960, PT // B * D).rearrange("p (i n) -> p i n", i=2)
        y_out = cut(8960 + PT // B * D, PT // B * D).rearrange("p (i n) -> p i n", i=2)
        t4 = cut(10240, 2500, 128).rearrange("p (k n) -> p k n", k=4)
        ht = cut(12740, 5000, 128).rearrange("p (j n) -> p j n", j=8)
        ek = cut(12740, 2560).rearrange("p (i n) -> p i n", i=G)
        v1 = cut(15300, G * 258).rearrange("p (i c n) -> p i c n", i=G, c=2)
        t4f = cut(12740, 512, 128)
        bv_rows = cut(13252, 250, 128).rearrange("p (c n) -> p c n", c=2)
        sums = [(x1, y, row_a[:, :, 0:D], f_out),
                tuple(xg[:, G * k:G * k + G, 0:D] for k in range(4))]
        x_big = cut(0, 6400).rearrange("p (b d) -> p b d", b=NB)
        agg_t = sb("agg_t", [B, D + 1])
        b_tmp = agg_t[:, 0:D]
        agg_s = sb("agg_s", [B, G, D + 1])
        kvf = cut(17740, 512, 128)
        st = sb("st", [B, 12, G])
        bn6 = sb("bn6", [B, G, 6])
        mv = sb("mv", [B, G, 2])
        sd = sb("sd", [B, G])
        rs = sb("rs", [B, G])
        lg, lt, lu, gate = (sb(n, [B, G, 8]) for n in ("lg", "lt", "lu", "gate"))
        st_min, st_max = sb("st_min", [TR, TC]), sb("st_max", [TR, TC])
        blk, blk_i = sb("blk", [NB, 3]), sb("blk_i", [NB, 2], I32)
        st4 = sb("st4", [128, KC, 2])[:, :, :]
        st2 = sb("st2", [128, 2])

        def scratch(rows, at, n):
            return xg[0:rows, at:at + n, :].rearrange("p a b -> p (a b)")

        e_i32 = [scratch(TR, 4 * i, 4)[:, 0:TC * B].bitcast(I32) for i in range(2)]
        e_f32 = [scratch(TR, 8 + 4 * i, 4)[:, 0:TC * B] for i in range(3)]
        src_hi, src_lo = cut(8960, NT), cut(2560, NT)
        oh_lo = [cut(2560 + NT + i * (DT * B // 2), DT * B // 2).bitcast(BF16)
                 .rearrange("p (t l) -> p t l", t=DT) for i in range(2)]
        oh_hi = [cut(18300 + i * (DT * NB // 2), DT * NB // 2).bitcast(BF16)
                 .rearrange("p (t l) -> p t l", t=DT) for i in range(2)]
        range_t = scratch(NB, 0, 16)
        t_min, t_max, t_msk, t_val, t_iot = (range_t[:, NT * i:NT * i + NT] for i in range(5))

        l_x, l_edge, l_w0, l_wh, l_l1, l_c, l_bc, l_b1 = (
            sem(n) for n in ("x_loaded", "edges_loaded", "w_mix0_loaded", "w_hid0_loaded", "w_layer1_loaded",
                             "w_c_loaded", "biases_c_loaded", "b1_loaded"))
        const_full, edge_f_full, edge_ps_full, edge_ps_free = (
            sem(n) for n in ("consts_made", "edges_as_float", "edge_turn_full", "edge_turn_free"))
        minmax_full, minmax_stored, minmax_loaded, tile_iota, scratch_free, tabs_full = (
            sem(n) for n in ("tile_range_made", "tile_range_stored", "tile_range_loaded", "tile_numbers_made",
                             "edge_rows_free", "edge_tables_made"))
        blk_full, blk_stored, blk_loaded, cum_full = (
            sem(n) for n in ("block_range_made", "block_range_stored", "block_range_loaded", "chunk_sums_made"))
        feat0_full, feat0_stored = sem("feat0_made"), sem("feat0_stored")
        deg_full, deg_free, deg_ps_full = pair("degree_onehot_full"), pair("degree_onehot_free"), sem("degree_counted")
        xg_clear, w_prep, w_prep_ps, w_prep2, setup_done = (
            sem(n) for n in ("gather_buffer_clear", "w_prep", "w_prep_ps", "w_prep2", "setup_done"))
        xg_full = [sem(f"rows_full{k}") for k in range(GR)]
        xg_free = [sem(f"rows_free{k}") for k in range(GR)]
        oh_full, oh_free, idx_full = sem("onehot_full"), sem("onehot_free"), sem("indices_full")
        agg_full, agg_free = sem("agg_ps_full"), sem("agg_ps_free")
        t_act, t_free = pair("turned_ps_full"), pair("turned_ps_free")
        h_act, h_dve, h_free = pair("hidden_ps_full"), pair("proj_ps_full"), pair("hidden_ps_free")
        y_dve, y_free = pair("y_ps_full"), pair("y_ps_free")
        ps_full = sem("ps_stage_full")
        t_full = sem("turned_full")
        v_full = sem("vector_stage_full")
        ht_full = pair("hidden_full")
        act_in2, act_out2 = pair("phi_act_in"), pair("phi_act_out")
        act_in, act_out = sem("act_in"), sem("act_out")
        sums_full = sem("sums_over_nodes_full")
        k4_full, k4_used = sem("key4_full"), sem("keys_used")
        aggt_free, aggs_ready, aggs_in = sem("agg_rows_stored"), sem("step_aggs_stored"), sem("step_aggs_loaded")
        w_full, w_free = pair("expert_w_full"), pair("expert_w_free")
        xa_in, xa_used = sem("x_rows_loaded"), sem("x_rows_used")
        rowa_full, rowa_free, rowa_in, rowa_used = (
            sem(n) for n in ("row_a_full", "row_a_stored", "row_a_loaded", "row_a_used"))
        rowb_full, rowb_free, rowb_in, rowb_used = (
            sem(n) for n in ("row_b_full", "row_b_stored", "row_b_loaded", "row_b_used"))
        q_full, q_free, phi_full = sem("queries1_full"), sem("queries1_stored"), sem("phi_full")
        rowx_full, rowx_free, rowx_in, rowx_used = (
            sem(n) for n in ("resid_full", "resid_stored", "resid_loaded", "resid_used"))
        pos_full, scattered = sem("positions_made"), sem("rows_scattered")
        got, got_used, sum_in = pair("results_gathered"), pair("results_used"), pair("sum_rows_loaded")
        sum_full, sum_free = pair("sum_full"), pair("sum_stored")
        routes_full, tails_stored, sorted_done, out_filled = (
            sem(n) for n in ("routes_made", "tails_stored", "results_stored", "results_filled"))
        xin_full, xin_free, yout_full, yout_free = (
            sem(n) for n in ("sorted_rows_loaded", "sorted_rows_used", "results_full", "results_out"))
        fout_full, fout_free, fout_ok = sem("f_out_full"), sem("f_out_stored"), sem("f_out_free")
        loop_a_done, loop_b_done = sem("loop_a_done"), sem("loop_b_done")
        dve_s, act_s = sem("vector_steps"), sem("scalar_steps")

        def rows(ap, s):
            return ap[ds(s * (G * B), G * B), :].rearrange("(i p) d -> p i d", p=B)

        def wview(w):
            return w.rearrange("(c p) n -> p c n", p=128)

        def row(v, p=B):
            return v.partition_broadcast(p)

        def pair_rows(ap, e, t):
            if isinstance(t, int):
                return ap[t * PT + e * CAP:t * PT + e * CAP + PT, :].rearrange("(i p) d -> p i d", p=B)
            return ap[ds(t * PT + e * CAP, PT), :].rearrange("(i p) d -> p i d", p=B)

        def loads(layer, e):
            return 16 * (2, 3)[layer] * (e // 2 + 1) + 16 * 2 * (E0 // 2) * layer

        def flat(ap):
            return ap.rearrange("p a d -> p (a d)")

        ctx.enter_context(nc.allow_non_contiguous_dma(reason="bias columns and block tables, a few KB"))
        block = ctx.enter_context(nc.Block())

        @block.sync
        def _(sp):
            for s in (rowa_free, rowb_free, rowx_free, yout_free, aggt_free, q_free):
                sp.sem_inc(s, 16)
            sp.sem_inc(xin_free, 1)

            def sorted_rows(layer):
                sp.wait_ge(routes_full, layer + 1)
                for e in range(E0):
                    tail = sp.value_load(tail_tab[0:1, e:e + 1], min_val=CAP * e, max_val=CAP * e + N)
                    sp.dma_start(sorted_in[ds(tail, PT), :].rearrange("(i p) d -> p i d", p=B),
                                 zeros[:, :].unsqueeze(1).to_broadcast([B, PT // B, D])).then_inc(tails_stored, 16)
                sp.wait_ge(tails_stored, 16 * E0 * (layer + 1))
                sp.wait_ge((rowx_free, fout_free)[layer], 16)
                sp.wait_ge(scattered, 16 * (NB * (1, 3)[layer] + 1))
                for e in range(E0):
                    n = sp.value_load(pair_tab[0:1, e:e + 1], min_val=1, max_val=MAXP)
                    with sp.Fori(0, n) as t:
                        take(sp, xin_free)
                        sp.dma_start(x_in, pair_rows(sorted_in, e, t)).then_inc(xin_full, 16)
                take(sp, xin_free)
                sp.dma_start(x_in, pair_rows(sorted_in, 0, 0)).then_inc(xin_full, 16)
            for i, n in enumerate(("dst", "src")):
                sp.dma_start(e_i32[i], a[n].rearrange("(q n) -> q n", q=TR)).then_inc(l_edge, 16)
            sp.dma_start(e_f32[2], a["edge_weight"].rearrange("(q n) -> q n", q=TR)).then_inc(l_edge, 16)
            xv = a["x"].rearrange("(b p) d -> p b d", p=B)
            for i in range(5):
                sp.dma_start(x_big[:, 5 * i:5 * i + 5, :], xv[:, 5 * i:5 * i + 5, :]).then_inc(l_x, 16)
            sp.dma_start(wqkvs[:, :, 0:3 * D], wview(a["L0_mix_W_qkv"])).then_inc(l_w0, 16)
            sp.dma_start(wqkvs[:, :, 3 * D:4 * D], wview(a["L0_gnn_W_self"])).then_inc(l_w0, 16)
            sp.dma_start(wo[:, :, :], wview(a["L0_mix_W_out"])).then_inc(l_w0, 16)
            sp.dma_start(b1_col[:, 0:KC], a["L0_mix_b_qkv"][2 * D:3 * D].rearrange("(c p) -> p c", p=128)).then_inc(l_w0, 16)
            sp.dma_start(bias0[:, 0:3 * D], row(a["L0_mix_b_qkv"])).then_inc(l_w0, 16)
            sp.dma_start(bias0[:, 3 * D:], row(a["L0_gnn_bias"])).then_inc(l_w0, 16)
            sp.dma_start(b_tmp, row(a["L0_mix_b_out"])).then_inc(l_w0, 16)
            take(sp, minmax_full)
            sp.dma_start(tile_min, st_min[:, :]).then_inc(minmax_stored, 16)
            sp.dma_start(tile_max, st_max[:, :]).then_inc(minmax_stored, 16)
            sp.wait_ge(minmax_stored, 32)
            take(sp, tabs_full)
            sp.dma_start(t_min, tile_min.rearrange("q c -> (q c)").partition_broadcast(NB)).then_inc(minmax_loaded, 16)
            sp.dma_start(t_max, tile_max.rearrange("q c -> (q c)").partition_broadcast(NB)).then_inc(minmax_loaded, 16)
            fv = feat0.rearrange("(b p) d -> p b d", p=B)
            for i in range(NS):
                sp.wait_ge(feat0_full, i + 1)
                sp.dma_start(fv[:, G * i:G * i + G, :], x_big[:, G * i:G * i + G, :]).then_inc(feat0_stored, 16)
            take(sp, blk_full)
            sp.dma_start(block_lo, blk_i[:, 0:1]).then_inc(blk_stored, 16)
            sp.dma_start(block_n, blk_i[:, 1:2]).then_inc(blk_stored, 16)
            sp.wait_ge(blk_stored, 32)
            sp.dma_start(lo_tab[:, :], block_lo.rearrange("b o -> o b")).then_inc(blk_loaded, 16)
            sp.dma_start(n_tab[:, :], block_n.rearrange("b o -> o b")).then_inc(blk_loaded, 16)
            sp.dma_start(w_h[:, :, :], wview(a["L0_ffn_W1"])).then_inc(l_wh, 16)
            sp.dma_start(wn[:, :, :], wview(a["L0_gnn_W_neighbor"])).then_inc(l_wh, 16)
            sp.dma_start(wg[:, :, :], a["L0_ffn_Wg"].rearrange("(j p) e -> p j e", p=128)).then_inc(l_wh, 16)
            sp.dma_start(bg_bc[:, :], row(a["L0_ffn_bg"])).then_inc(l_wh, 16)
            for i, n in enumerate("qkv"):
                sp.dma_start(wqkv1[:, :, D * i:D * i + D], wview(a["L1_mix_W" + n])).then_inc(l_l1, 16)
                sp.dma_start(bias1[:, D * i:D * i + D], row(a["L1_mix_b" + n])).then_inc(l_l1, 16)
            sp.dma_start(b1e_col[:, :, :], a["L1_ffn_b1"].rearrange("e (j p) -> p e j", p=128)).then_inc(l_l1, 16)
            sp.wait_ge(feat0_stored, 80)
            with sp.Fori(0, NS) as s:
                take(sp, xa_used)
                sp.dma_start(x1, rows(a["x"], s)).then_inc(xa_in, 16)
                sp.dma_start(y, rows(feat0, s)).then_inc(xa_in, 16)
                take(sp, rowa_full)
                sp.dma_start(rows(rows_a, s), row_a).then_inc(rowa_free, 16)
            take(sp, loop_a_done)
            sp.dma_start(b1_col[:, :], a["L0_ffn_b1"].rearrange("(j p) -> p j", p=128)).then_inc(l_b1, 16)
            sp.wait_ge(const_full, 1)
            ov = sorted_out.rearrange("(g i p) d -> g p i d", p=B, i=6)
            for g in range(ALLP // 3):
                sp.dma_start(ov[g], zeros[:, :].unsqueeze(1).to_broadcast([B, 6, D])).then_inc(out_filled, 16)
            with sp.Fori(0, NS) as s:
                take(sp, rowa_used)
                sp.dma_start(row_a, rows(rows_a, s)).then_inc(rowa_in, 16)
                take(sp, aggs_ready)
                sp.dma_start(agg_s[:, :, 0:D], rows(agg_rows0, s)).then_inc(rowa_in, 16)
                take(sp, rowx_full)
                sp.dma_start(rows(rows_x, s), x1).then_inc(rowx_free, 16)
            sorted_rows(0)

            def residual(s):
                take(sp, rowx_used)
                sp.dma_start(x1, rows(rows_x, s)).then_inc(rowx_in, 16)

            def project1(s, more):
                take(sp, rowb_full)
                sp.dma_start(rows(rows_b[:, 0:2 * D], s), row_b[:, :, 0:2 * D]).then_inc(rowb_free, 16)
                take(sp, fout_full)
                sp.dma_start(rows(feat1, s), f_out).then_inc(fout_free, 16)
                if more:
                    residual(s + 1)
                take(sp, q_full)
                sp.dma_start(rows(rows_b[:, 2 * D:3 * D], s), row_b[:, :, 2 * D:3 * D]).then_inc(q_free, 16)

            residual(0)
            project1(0, True)
            sp.dma_start(wn[:, :, :], wview(a["L1_gnn_weight"])).then_inc(l_c, 16)
            sp.dma_start(wo[:, :, :], wview(a["L1_mix_Wo"])).then_inc(l_c, 16)
            sp.dma_start(w_h[:, :, :], wview(a["L1_mix_W1"])).then_inc(l_c, 16)
            sp.dma_start(b1_col[:, :], a["L1_mix_b1"].rearrange("(j p) -> p j", p=128)).then_inc(l_c, 16)
            sp.dma_start(w2m, a["L1_mix_W2"].rearrange("(j p) n -> p j n", p=128)).then_inc(l_c, 16)
            sp.dma_start(wg[:, 0:KC, :], wview(a["L1_ffn_Wg"])).then_inc(l_c, 16)
            sp.dma_start(bg_bc[:, :], row(a["L1_ffn_bg"])).then_inc(l_c, 16)
            with sp.Fori(1, NS - 1) as s:
                project1(s, True)
            project1(NS - 1, False)
            take(sp, loop_b_done)
            for i, n in enumerate(("L1_gnn_bias", "L1_mix_bo", "L1_mix_b2", "L1_mix_ln1_g", "L1_mix_ln1_b",
                                   "L1_mix_ln2_g", "L1_mix_ln2_b")):
                sp.dma_start(bc[:, i, :], row(a[n])).then_inc(l_bc, 16)

            def mixer(s):
                take(sp, rowb_used)
                sp.dma_start(row_b, rows(rows_b, s)).then_inc(rowb_in, 16)
                take(sp, rowx_full)
                sp.dma_start(rows(rows_x, s), x1).then_inc(rowx_free, 16)

            def graph(s):
                take(sp, rowx_used)
                take(sp, fout_free, 16)
                sp.dma_start(f_out, rows(rows_x, s)).then_inc(aggs_in, 16)
                take(sp, aggs_ready)
                sp.dma_start(agg_s[:, :, :], rows(agg_rows1, s)).then_inc(aggs_in, 16)
                take(sp, fout_full)
                sp.dma_start(rows(rows_x, s), f_out).then_inc(fout_free, 16)

            with sp.Fori(0, 2) as s:
                mixer(s)
            with sp.Fori(0, NS - 2) as p:
                mixer(p + 2)
                graph(p)
            sp.wait_ge(rowx_free, 16)
            for s in range(NS - 2, NS):
                graph(s)
            sorted_rows(1)

            def sum_step(s, j):
                if not (isinstance(s, int) and s < 2):
                    take(sp, sum_full[j])
                    sp.dma_start(rows(out, s - 2), sums[j][3]).then_inc(sum_free[j], 16)
                sp.dma_start(sums[j][0], rows(rows_x, s)).then_inc(sum_in[j], 16)

            take(sp, rowx_used)
            for j in range(2):
                sum_step(j, j)
            with sp.Fori(1, NS // 2) as p:
                for j in range(2):
                    sum_step(p * 2 + j, j)
            sum_step(NS - 1, 0)
            for j, s in ((1, NS - 2), (0, NS - 1)):
                take(sp, sum_full[j])
                sp.dma_start(rows(out, s), sums[j][3]).then_inc(sum_free[j], 16)
            for j in range(2):
                sp.wait_ge(sum_free[j], 16)

        @block.gpsimd
        def _(pool):
            chain = Chain(pool, idx_full)
            chain(pool.memset(ident[:, :], 0.0))
            pool.memset(zero_w[:, :], 0.0)
            pool.memset(zero_r[:, :], 0.0)
            pool.memset(ones[:, :], 1.0)
            pool.memset(zeros[:, :], 0.0)
            pool.iota(next_col[:, :], [[1, 1]], base=1, channel_multiplier=1, allow_small_or_imprecise_dtypes=True)
            pool.iota(region[:, :], [[CAP, E0]], base=0, channel_multiplier=0, allow_small_or_imprecise_dtypes=True)
            pool.iota(pair_at[:, :], [[PT, MAXP]], base=0, channel_multiplier=0, allow_small_or_imprecise_dtypes=True)
            chain(pool.affine_select(out=ident[:, :], in_=ident[:, :], compare_op=ALU.not_equal, fill=1.0,
                                     base=0, pattern=[[-1, 128]], channel_multiplier=1))
            pool.iota(iota[:, :], [[1, B]], base=0, channel_multiplier=0, allow_small_or_imprecise_dtypes=True)
            pool.iota(base[:, :], [[B, NB]], base=0, channel_multiplier=0, allow_small_or_imprecise_dtypes=True)
            chain(pool.iota(base_col[:, :], [[1, 1]], base=0, channel_multiplier=B, allow_small_or_imprecise_dtypes=True))
            pool.memset(dst_f[:, NT:], -1.0)
            pool.memset(w_f[:, NT:], 0.0)
            chain(pool.memset(src_i[:, NT:], 0))
            chain.restart()
            pool.sem_inc(const_full, 1)
            pool.dma_start(sorted_in[0:1, :], zeros[0:1, :]).then_inc(scattered, 16)
            take(pool, scratch_free)
            pool.iota(t_iot, [[1, NT]], base=0, channel_multiplier=0,
                      allow_small_or_imprecise_dtypes=True).then_inc(tile_iota, 1)
            take(pool, xg_clear)
            chain(pool.memset(xg[:, :, D:D + 1], 1.0))
            chain.restart()
            pool.wait_ge(feat0_stored, 80)
            pool.wait_ge(blk_loaded, 32)

            def gather(b, feat):
                n = pool.value_load(n_tab[0:1, ds(b, 1)], min_val=1, max_val=MAXCH)
                lo = pool.value_load(lo_tab[0:1, ds(b, 1)], min_val=0, max_val=NT - 1)
                with pool.Fori(0, n) as c:
                    t0 = nc.s_assert_within(pool.snap(lo + c * CH), 0, NT - 1,
                                            skip_runtime_bounds_check_because="a block's chunks start inside its span")
                    for k in range(GR):
                        take(pool, xg_free[k])
                        pool.tensor_copy(idx_cur[:, GS * k:GS * k + GS],
                                         src_i[:, ds(t0 + GS * k, GS)]).then_inc(idx_full, 1)
                        take(pool, idx_full)
                        for s in range(GS * k, GS * k + GS):
                            pool.indirect_dma_start(
                                xg[:, s, 0:D], None, feat,
                                bass.IndirectOffsetOnAxis(ap=idx_cur[:, s:s + 1], axis=0)).then_inc(xg_full[k], 16)

            def expert_w(layer, e):
                if layer or e >= 2:
                    take(pool, w_free[e % 2])
                full = w_full[e % 2]
                if layer == 0:
                    pool.dma_start(wd_sb[e % 2], a["L0_ffn_Wd"][e].rearrange("(j p) d -> p j d", p=128)).then_inc(full, 16)
                    pool.dma_start(be[:, e % 2, :], row(a["L0_ffn_bd"][e])).then_inc(full, 16)
                else:
                    pool.dma_start(w1e_sb[e % 2], wview(a["L1_ffn_W1"][e])).then_inc(full, 16)
                    pool.dma_start(w2e_sb[e % 2], a["L1_ffn_W2"][e].rearrange("(j p) d -> p j d", p=128)).then_inc(full, 16)
                    pool.dma_start(be[:, e % 2, :], row(a["L1_ffn_b2"][e])).then_inc(full, 16)

            def scatter(n, src):
                take(pool, pos_full)
                for k in range(n):
                    for i in range(G):
                        pool.indirect_dma_start(
                            sorted_in, bass.IndirectOffsetOnAxis(ap=pos_cur[:, k, i:i + 1], axis=0),
                            src[:, i, :], None).then_inc(scattered, 16)

            def collect(s, j, dsts):
                take(pool, got_used[j])
                n = len(dsts)
                chain(pool.tensor_copy(pos_get[j][:, 0:n, :], pos_tab[:, 0:n, ds(s * G, G)]))
                chain.restart()
                for k, dst in enumerate(dsts):
                    for i in range(G):
                        pool.indirect_dma_start(
                            dst[:, i, :], None, sorted_out,
                            bass.IndirectOffsetOnAxis(ap=pos_get[j][:, k, i:i + 1], axis=0)).then_inc(got[j], 16)

            with pool.Fori(0, AA * NS) as b:
                gather(b, feat0)
            for e in range(2):
                expert_w(0, e)
            with pool.Fori(AA * NS, AA * NS + AB) as b:
                gather(b, feat0)
            with pool.Fori(0, NS - 3) as s:
                gather(s * AB + (AA * NS + AB), feat0)
                scatter(1, y)
                with pool.Fori(1, AB) as i:
                    gather(s * AB + (AA * NS + AB) + i, feat0)
            gather(AA * NS + AB * (NS - 2), feat0)
            scatter(1, y)
            with pool.Fori(AA * NS + AB * (NS - 2) + 1, NB) as b:
                gather(b, feat0)
            scatter(1, y)
            scatter(1, y)
            for e in range(2, E0):
                expert_w(0, e)
            take(pool, sorted_done)
            def feat1_landed():
                take(pool, fout_free, 16)
                pool.sem_inc(fout_ok, 1)

            pool.sem_inc(fout_ok, 1)
            collect(0, 0, (y,))
            with pool.Fori(1, NS) as s:
                collect(s, 0, (y,))
                feat1_landed()
            feat1_landed()
            with pool.Fori(0, AC + AP) as b:
                gather(b, feat1)
            for e in range(2):
                expert_w(1, e)
            with pool.Fori(1, NS - 2) as p:
                gather(p * AP + AC, feat1)
                scatter(2, row_a[:, :, D:2 * D])
                with pool.Fori(1, AP) as i:
                    gather(p * AP + AC + i, feat1)
            for b in range(AC + AP * (NS - 2), NB):
                gather(b, feat1)
                scatter(2, row_a[:, :, D:2 * D])
            scatter(2, row_a[:, :, D:2 * D])
            for e in range(2, E1):
                expert_w(1, e)
            take(pool, sorted_done)
            with pool.Fori(0, NS // 2) as p:
                for j in range(2):
                    collect(p * 2 + j, j, sums[j][1:3])
            collect(NS - 1, 0, sums[0][1:3])

        @block.tensor
        def _(pe):
            def mm(o, w, r, first, last, check=True):
                return pe.matmul(o, w, r, start=first, stop=last, skip_group_check=not check)

            def zero(ps, cols, start, stop):
                return mm(ps[:, 0:cols], zero_w[:, :], zero_r[:, 0:cols], start, stop, False)

            def turn(ps, at, src, n=B):
                return pe.transpose(ps[:, at:at + n], src, ident[0:n, 0:n])

            def turn_rows(*srcs):
                for i in range(G):
                    take(pe, t_free[i % 2])
                    for n, src in enumerate(srcs):
                        for c in range(KC):
                            last = turn(ps_t[i % 2], B * (KC * n + c), src[:, i, 128 * c:128 * c + 128])
                    last.then_inc(t_act[i % 2], 1)

            def turned(i):
                pe.wait_ge(t_full, i + 1)
                if i == G - 1:
                    pe.sem_clear(t_full)

            def at(k, i):
                return t4[:, k, B * i:B * i + B]

            pe.wait_ge(const_full, 1)
            for s in xg_free + [oh_free, agg_free] + t_free + h_free + y_free:
                pe.sem_inc(s, 1)
            take(pe, edge_f_full)
            for g in range(6):
                if g >= 2:
                    pe.wait_ge(edge_ps_free, g - 1)
                ps = ps_h[g % 2]
                for c in range(4):
                    last = pe.transpose(ps[0:B, TR * c:TR * c + TR],
                                        e_f32[g // 2][:, B * (4 * (g % 2) + c):B * (4 * (g % 2) + c + 1)],
                                        ident[0:TR, 0:TR])
                last.then_inc(edge_ps_full, 1)
            pe.wait_ge(l_w0, 112)
            take(pe, w_prep)
            for r in range(KC):
                for c in range(KC):
                    last = turn(ps_y[0], 128 * (KC * r + c), wqkvs[:, r, 2 * D + 128 * c:2 * D + 128 * c + 128], 128)
            last.then_inc(w_prep_ps, 1)
            take(pe, w_prep2)
            for r in range(KC):
                for c in range(KC):
                    mm(ps_y[1][:, D * r:D * r + D], t4f[:, 128 * (KC * r + c):128 * (KC * r + c) + 128],
                       wo[:, c, :], c == 0, c == KC - 1)
            for c in range(KC):
                last = mm(ps_t[0][0:B, 0:D], bv_rows[:, c, :], wo[:, c, :], c == 0, c == KC - 1)
            last.then_inc(w_prep_ps, 1)
            take(pe, setup_done)

            def aggregate(b, cols, before):
                first = pe.value_load(cum_tab[0:1, ds(b, 1)], min_val=0, max_val=MAXCH * NB)
                n = pe.value_load(n_tab[0:1, ds(b, 1)], min_val=1, max_val=MAXCH)
                take(pe, agg_free)
                zero(ps_agg, cols, True, False)
                with pe.Fori(0, n) as c:
                    take(pe, oh_full)
                    landed = pe.snap((before + first + c + 1) * (16 * GS))
                    for k in range(GR):
                        pe.wait_ge(xg_full[k], landed)
                        for s in range(GS * k, GS * k + GS):
                            last = mm(ps_agg[0:B, 0:cols], oh[:, s, :], xg[:, s, 0:cols], False, False, False)
                        last.then_inc(xg_free[k], 1)
                    zero(ps_agg, cols, False, False).then_inc(oh_free, 1)
                zero(ps_agg, cols, False, True).then_inc(agg_full, 1)

            def degrees():
                for j in range(2):
                    take(pe, deg_full[j])
                    for t in range(DT):
                        last = mm(ps_kv[0:B, 0:NB], oh_lo[j][:, t, :], oh_hi[j][:, t, :], False, False, False)
                    last.then_inc(deg_free[j], 1)

            def hidden(w):
                for j in range(w.shape[2] // 128):
                    for half, (lo, hi) in enumerate(HALVES):
                        take(pe, h_free[half])
                        for c in range(KC):
                            last = mm(ps_h[half][:, 0:hi - lo], w[:, c, 128 * j:128 * j + 128], t4[:, c, lo:hi],
                                      c == 0, c == KC - 1)
                        last.then_inc(h_act[half], 1)

            def gates(lhs, n):
                take(pe, t_free[0])
                for i in range(G):
                    for j in range(n):
                        last = mm(ps_t[0][0:B, 8 * i:8 * i + 8], lhs(j, i), wg[:, j, :], j == 0, j == n - 1)
                last.then_inc(ps_full, 1)

            def ranks():
                take(pe, v_full)
                take(pe, t_free[0])
                for i in range(G):
                    o = ps_t[0][0:B, E0 * i:E0 * i + E0]
                    mm(o, upper[:, :], gate[:, i, :], True, i == 0)
                    for j in range(i):
                        mm(o, ones[0:B, :], gate[:, j, :], False, j == i - 1)
                for i in range(G):
                    last = mm(ps_t[0][0:B, E0 * G:E0 * G + E0], ones[0:B, :], gate[:, i, :], i == 0, i == G - 1)
                last.then_inc(ps_full, 1)

            def experts(layer, w1, w2, n):
                def turn_pair():
                    take(pe, xin_full, 16)
                    take(pe, t_free[0])
                    for c in range(KC):
                        for i in range(2):
                            last = turn(ps_t[0], PT * c + B * i, x_in[:, i, 128 * c:128 * c + 128])
                    last.then_inc(t_act[0], 1)

                pe.wait_ge(routes_full, layer + 1)
                turn_pair()
                for e in range(E0):
                    trips = pe.value_load(pair_tab[0:1, e:e + 1], min_val=1, max_val=MAXP)
                    pe.wait_ge(w_full[e % 2], loads(layer, e))
                    with pe.Fori(0, trips):
                        take(pe, t_full)
                        for j in range(n):
                            take(pe, h_free[j % 2])
                            for c in range(KC):
                                last = mm(ps_h[j % 2][:, 0:PT], w1(e)[:, c, 128 * j:128 * j + 128], t4[:, c, 0:PT],
                                          c == 0, c == KC - 1)
                            last.then_inc(h_act[j % 2], 1)
                        turn_pair()
                        take(pe, ht_full[0])
                        for i in range(2):
                            take(pe, y_free[i])
                            for j in range(n):
                                last = mm(ps_y[i][0:B, 0:D], ht[:, j, B * i:B * i + B], w2(e)[:, j, :],
                                          j == 0, j == n - 1)
                            last.then_inc(y_dve[i], 1)
                take(pe, t_full)

            take(pe, cum_full)
            zero(ps_kv, 512, True, False)
            zero(ps_agg, 2, True, True)
            with pe.Fori(0, NS) as s:
                take(pe, v_full)
                turn_rows(y)
                for i in range(G):
                    turned(i)
                    take(pe, h_free[i % 2])
                    for c in range(KC):
                        last = mm(ps_h[i % 2][0:B, :], at(c, i), wqkvs[:, c, 0:512], c == 0, c == 1)
                    last.then_inc(h_dve[i % 2], 1)
                    take(pe, y_free[i % 2])
                    for c in range(KC):
                        last = mm(ps_y[i % 2][0:B, :], at(c, i), wqkvs[:, c, 512:1024], c == 0, c == 1)
                    last.then_inc(y_dve[i % 2], 1)
                aggregate(s * AA, D, 0)
                take(pe, k4_full)
                take(pe, v_full)
                take(pe, t_free[0])
                for c in range(KC):
                    for i in range(G):
                        last = mm(ps_t[0][:, c:c + 1], ek[:, i, D + 128 * c:D + 128 * c + 128], ones[0:B, 0:1],
                                  i == 0, i == G - 1)
                last.then_inc(ps_full, 1)
                for i in range(G):
                    for c in range(KC):
                        last = mm(ps_kv[:, D * c:D * c + D], ek[:, i, 128 * c:128 * c + 128], f_out[:, i, :],
                                  False, False, False)
                last.then_inc(k4_used, 1)
                aggregate(s * AA + 1, D, 0)
            zero(ps_kv, 512, False, True).then_inc(sums_full, 1)
            take(pe, v_full)
            take(pe, y_free[0])
            for r in range(KC):
                for c in range(KC):
                    last = turn(ps_y[0], 128 * (KC * r + c), kvf[:, D * r + 128 * c:D * r + 128 * c + 128], 128)
            last.then_inc(y_dve[0], 1)
            take(pe, v_full)
            take(pe, y_free[1])
            for r in range(KC):
                for c in range(KC):
                    last = mm(ps_y[1][:, D * r:D * r + D], t4f[:, 128 * (KC * r + c):128 * (KC * r + c) + 128],
                              wo[:, c, :], c == 0, c == KC - 1)
            last.then_inc(y_dve[1], 1)
            pe.wait_ge(l_wh, 64)
            pe.wait_ge(l_l1, 16 * 7)
            zero(ps_kv, NB, True, False)

            def layer0(s, more):
                def agg(i):
                    if i < more:
                        aggregate(s * AB + AA * NS + i, D, 0)
                    if more:
                        degrees()

                agg(0)
                take(pe, v_full)
                turn_rows(agg_s, row_a[:, :, D:2 * D])
                for i in range(G):
                    turned(i)
                    take(pe, y_free[i % 2])
                    for k, w in enumerate((wn, wn, kvo, kvo)):
                        last = mm(ps_y[i % 2][0:B, 0:D], at(k, i), w[:, k % 2, :], k == 0, k == 3)
                    last.then_inc(y_dve[i % 2], 1)
                agg(1)
                take(pe, v_full)
                turn_rows(y)
                for i in range(G):
                    turned(i)
                hidden(w_h)
                agg(2)
                take(pe, ht_full[0])
                gates(lambda j, i: ht[:, j, B * i:B * i + B], J0)
                agg(3)
                ranks()
                if more:
                    degrees()

            def project1():
                take(pe, v_full)
                turn_rows(row_b[:, :, D:2 * D])
                for i in range(G):
                    turned(i)
                    take(pe, h_free[i % 2])
                    for c in range(KC):
                        last = mm(ps_h[i % 2][0:B, :], at(c, i), wqkv1[:, c, 0:512], c == 0, c == 1)
                    last.then_inc(h_dve[i % 2], 1)
                    take(pe, y_free[i % 2])
                    for c in range(KC):
                        last = mm(ps_y[i % 2][0:B, 0:D], at(c, i), wqkv1[:, c, 512:768], c == 0, c == 1)
                    last.then_inc(y_dve[i % 2], 1)
                take(pe, phi_full)
                for i in range(G):
                    for c in range(KC):
                        last = mm(ps_kv[:, 129 * c:129 * c + 129], ek[:, i, D + 128 * c:D + 128 * c + 128], v1[:, i, c, :],
                                  False, False, False)
                last.then_inc(k4_used, 1)

            with pe.Fori(0, NS - 2) as s:
                layer0(s, AB)
            layer0(NS - 2, AB - 1)
            layer0(NS - 1, 0)
            zero(ps_kv, NB, False, True).then_inc(deg_ps_full, 1)
            experts(0, lambda e: w_h, lambda e: wd_sb[e % 2], J0)
            zero(ps_kv, 258, True, False)
            with pe.Fori(0, NS):
                project1()
            zero(ps_kv, 258, False, True).then_inc(sums_full, 1)

            total = pe.value_load(cum_tab[0:1, NB:NB + 1], min_val=NB, max_val=MAXCH * NB)
            pe.wait_ge(l_c, 16 * 7)

            def mixer(b, stages):
                def agg(i):
                    if i in stages:
                        aggregate(b + stages.index(i), D + 1, total)

                agg(0)
                take(pe, v_full)
                turn_rows(row_b[:, :, 2 * D:3 * D])
                for i in range(G):
                    turned(i)
                    take(pe, h_free[i % 2])
                    for c in range(KC):
                        last = mm(ps_h[i % 2][0:B, 132 * c:132 * c + 132], at(c, i), kvd[:, c, :], True, True)
                    last.then_inc(h_dve[i % 2], 1)
                agg(1)
                take(pe, v_full)
                turn_rows(y)
                for i in range(G):
                    turned(i)
                    take(pe, y_free[i % 2])
                    for c in range(KC):
                        last = mm(ps_y[i % 2][0:B, 0:D], at(c, i), wo[:, c, :], c == 0, c == 1)
                    last.then_inc(y_dve[i % 2], 1)
                agg(2)
                take(pe, v_full)
                turn_rows(x1)
                for i in range(G):
                    turned(i)
                hidden(w_h)
                agg(3)
                take(pe, ht_full[0])
                for i in range(G):
                    take(pe, y_free[i % 2])
                    for j in range(JF):
                        last = mm(ps_y[i % 2][0:B, 0:D], ht[:, j, B * i:B * i + B], w2m[:, j, :], j == 0, j == JF - 1)
                    last.then_inc(y_dve[i % 2], 1)
                agg(4)

            def graph(b, n):
                if n:
                    aggregate(b, D + 1, total)
                take(pe, v_full)
                turn_rows(agg_s)
                for i in range(G):
                    turned(i)
                    take(pe, y_free[i % 2])
                    for c in range(KC):
                        last = mm(ps_y[i % 2][0:B, 0:D], at(c, i), wn[:, c, :], c == 0, c == 1)
                    last.then_inc(y_dve[i % 2], 1)
                if n > 1:
                    aggregate(b + 1, D + 1, total)
                take(pe, v_full)
                turn_rows(row_a[:, :, D:2 * D])
                for i in range(G):
                    turned(i)
                gates(lambda j, i: at(j, i), KC)
                if n > 2:
                    aggregate(b + 2, D + 1, total)
                ranks()

            with pe.Fori(0, 2) as s:
                mixer(s * len(FOUR), FOUR)
            with pe.Fori(0, NS - 2) as p:
                mixer(p * AP + AC, TWO)
                graph(p * AP + (AC + len(TWO)), AG)
            graph(NB - AR, AR)
            graph(NB, 0)
            experts(1, lambda e: w1e_sb[e % 2], lambda e: w2e_sb[e % 2], J1)

        @block.scalar
        def _(act):
            chain = Chain(act, act_s)

            def copy_turned(n):
                for i in range(G):
                    take(act, t_act[i % 2])
                    chain(act.activation(t4[:, 0:n, B * i:B * i + B],
                                         ps_t[i % 2][:, 0:n * B].rearrange("p (k n) -> p k n", k=n), ACT.Copy))
                    act.sem_inc(t_free[i % 2], 1)
                    act.sem_inc(t_full, 1)
                chain.restart()

            def root(o):
                take(act, act_in)
                act.activation(o, o, ACT.Sqrt).then_inc(act_out, 1)

            def exp(x):
                take(act, act_in)
                act.activation(x, x, ACT.Exp).then_inc(act_out, 1)

            def units(slot, n, b, func):
                for j in range(n):
                    for half, (lo, hi) in enumerate(HALVES):
                        take(act, h_act[half])
                        last = act.activation(ht[:, slot + j, lo:hi], ps_h[half][:, 0:hi - lo], func, bias=b(j))
                        if j < n - 1 or half == 0:
                            last.then_inc(h_free[half], 1)
                chain(last)
                act.sem_inc(h_free[1], 1)
                act.sem_inc(ht_full[slot // 4], 1)
                chain.restart()

            def keep_aggregate(b, ap):
                cols = ap.shape[1]
                take(act, agg_full)
                take(act, aggt_free, 16)
                chain(act.activation(agg_t[:, 0:cols], ps_agg[0:B, 0:cols], ACT.Copy))
                act.sem_inc(agg_free, 1)
                act.dma_start(ap[ds(b * B, B), :], agg_t[:, 0:cols]).then_inc(aggt_free, 16)
                chain.restart()

            def step_ready():
                take(act, aggt_free, 16)
                act.sem_inc(aggt_free, 16)
                act.sem_inc(aggs_ready, 1)

            def experts(layer, n, b):
                def copy_pair():
                    take(act, t_act[0])
                    act.sem_inc(xin_free, 1)
                    chain(act.activation(t4[:, 0:KC, 0:PT], ps_t[0][:, 0:KC * PT].rearrange("p (k n) -> p k n", k=KC),
                                         ACT.Copy))
                    act.sem_inc(t_free[0], 1)
                    act.sem_inc(t_full, 1)

                act.wait_ge(routes_full, layer + 1)
                act.wait_ge(out_filled, 16 * (ALLP // 3))
                copy_pair()
                chain.restart()
                for e in range(E0):
                    trips = act.value_load(pair_tab[0:1, e:e + 1], min_val=1, max_val=MAXP)
                    first = act.value_load(before_tab[0:1, e:e + 1], min_val=e, max_val=ALLP - E0 + e)
                    with act.Fori(0, trips) as t:
                        for j in range(n):
                            take(act, h_act[j % 2])
                            last = act.activation(ht[:, j, 0:PT], ps_h[j % 2][:, 0:PT], ACT.Gelu, bias=b(e, j))
                            if j < n - 1:
                                last.then_inc(h_free[j % 2], 1)
                        chain(last)
                        act.sem_inc(ht_full[0], 1)
                        act.sem_inc(h_free[(n - 1) % 2], 1)
                        copy_pair()
                        take(act, yout_full)
                        pair = nc.s_assert_within(act.snap(first + t), 0, ALLP - 1,
                                                  skip_runtime_bounds_check_because="ALLP pairs hold all rows")
                        act.dma_start(sorted_out[ds(pair * PT, PT), :].rearrange("(i p) d -> p i d", p=B),
                                      y_out).then_inc(yout_free, 16)
                        chain.restart()

            with act.Fori(0, NS):
                root(sd[:, :])
            with act.Fori(0, NS) as s:
                copy_turned(2)
                take(act, act_in)
                for i in range(G):
                    act.activation(row_b[:, i, 0:D], row_b[:, i, 0:D], ACT.Square, accum_out=st[:, 0, i:i + 1])
                    last = act.activation(row_b[:, i, D:2 * D], row_b[:, i, D:2 * D], ACT.Square,
                                          accum_out=st[:, 1, i:i + 1])
                chain(last)
                for i in range(G):
                    last = act.activation(row_b[:, i, 2 * D:3 * D], row_b[:, i, 0:D], ACT.Square,
                                          accum_out=st[:, 2, i:i + 1])
                chain(last)
                act.activation(st[:, 3, :], st[:, 2, :], ACT.Sqrt).then_inc(act_out, 1)
                chain.restart()
                take(act, act_in)
                act.activation(ek[:, :, D:2 * D], ek[:, :, 0:D], ACT.Square).then_inc(k4_full, 1)
                for i in range(AA):
                    keep_aggregate(s * AA + i, agg_rows0)
            step_ready()
            root(st2[:, 0:2])
            act.wait_ge(l_b1, 16)

            def layer0(s, more):
                def agg(i):
                    if i < more:
                        keep_aggregate(s * AB + AA * NS + i, agg_rows0)

                agg(0)
                copy_turned(4)
                root(sd[:, :])
                agg(1)
                if more == AB:
                    step_ready()
                copy_turned(2)
                units(0, J0, lambda j: b1_col[:, j:j + 1], ACT.Gelu)
                agg(2)
                exp(lt[:, :, :])
                agg(3)
                if 0 < more < AB:
                    step_ready()

            def project1(more):
                copy_turned(2)
                for n in (1, 0):
                    take(act, act_in2[n])
                    x = ek[:, :, D * n:D * n + D]
                    act.activation(x, x, ACT.Exp).then_inc(act_out2[n], 1)
                if more:
                    root(sd[:, :])

            with act.Fori(0, NS - 2) as s:
                layer0(s, AB)
            layer0(NS - 2, AB - 1)
            layer0(NS - 1, 0)
            root(inv_out[:, :])
            experts(0, J0, lambda e, j: b1_col[:, j:j + 1])
            root(sd[:, :])
            with act.Fori(0, NS - 1):
                project1(True)
            project1(False)
            act.wait_ge(l_c, 16 * 7)
            act.wait_ge(l_l1, 16 * 7)

            def mixer(b, stages):
                def agg(i):
                    if i in stages:
                        keep_aggregate(b + stages.index(i), agg_rows1)

                agg(0)
                copy_turned(2)
                agg(1)
                copy_turned(2)
                root(sd[:, :])
                agg(2)
                copy_turned(2)
                units(0, JF, lambda j: b1_col[:, j:j + 1], ACT.Relu)
                agg(3)
                root(sd[:, :])
                agg(4)

            def graph(b, n):
                root(sd[:, :])
                if n:
                    keep_aggregate(b, agg_rows1)
                copy_turned(2)
                exp(row_a[:, :, D:2 * D])
                root(sd[:, :])
                if n > 1:
                    keep_aggregate(b + 1, agg_rows1)
                copy_turned(2)
                if n > 2:
                    keep_aggregate(b + 2, agg_rows1)

            with act.Fori(0, 2) as s:
                mixer(s * len(FOUR), FOUR)
            with act.Fori(0, NS - 2) as p:
                mixer(p * AP + AC, TWO)
                step_ready()
                graph(p * AP + (AC + len(TWO)), AG)
            step_ready()
            graph(NB - AR, AR)
            step_ready()
            graph(NB, 0)
            experts(1, J1, lambda e, j: b1e_col[:, e, j:j + 1])

        @block.vector
        def _(dve):
            chain = Chain(dve, dve_s)
            ts, tt, stt = dve.tensor_scalar, dve.tensor_tensor, dve.scalar_tensor_tensor

            def root():
                dve.sem_inc(act_in, 1)
                take(dve, act_out)

            def each(op, full, free):
                for i in range(G):
                    take(dve, full[i % 2])
                    last = op(i)
                    if i < G - 1:
                        last.then_inc(free[i % 2], 1)
                chain(last)
                dve.sem_inc(free[(G - 1) % 2], 1)

            def across(t):
                return t.unsqueeze(1).to_broadcast([B, G, D])

            def norm_sums(src):
                for i in range(G):
                    last = dve.bn_stats(bn6[:, i, :], src[:, i, :])
                chain(last)
                for i in range(G):
                    last = dve.bn_aggr(mv[:, i, :], bn6[:, i, :])
                chain(last)

            def norm(dst, src, g=None, beta=None):
                norm_sums(src)
                norm_rows(dst, src, g, beta)

            def norm_rows(dst, src, g=None, beta=None):
                chain(ts(sd[:, :], mv[:, :, 1], LN_EPS, None, ALU.add))
                root()
                chain(dve.reciprocal(rs[:, :], sd[:, :]))
                for i in range(G):
                    last = ts(dst[:, i, :], src[:, i, :], mv[:, i, 0:1], rs[:, i:i + 1], ALU.subtract, ALU.mult)
                chain(last)
                if g is not None:
                    chain(tt(dst, dst, across(g), ALU.mult))
                    chain(tt(dst, dst, across(beta), ALU.add))

            dve.wait_ge(const_full, 1)
            ts(upper[:, :], iota[:, :], next_col[:, 0:1], None, ALU.is_ge)
            dve.tensor_copy(cnt[:, :], region[:, :])
            dve.wait_ge(l_edge, 48)
            dve.tensor_copy(e_f32[0], e_i32[0])
            chain(dve.tensor_copy(e_f32[1], e_i32[1]))
            dve.sem_inc(edge_f_full, 1)
            dv = e_f32[0].rearrange("q (c e) -> q c e", c=TC)
            dve.tensor_reduce(st_min[:, :], dv, AX.X, ALU.min)
            chain(dve.tensor_reduce(st_max[:, :], dv, AX.X, ALU.max))
            dve.sem_inc(minmax_full, 1)
            for g in range(6):
                dve.wait_ge(edge_ps_full, g + 1)
                ps = ps_h[g % 2][0:B, 0:4 * TR].rearrange("p (c q) -> p c q", c=4)
                c0 = 4 * (g % 2)
                view = lambda t: t[:, 0:NT].rearrange("p (q c) -> p c q", c=TC)[:, c0:c0 + 4, :]
                chain(dve.tensor_copy(view((dst_f, src_i, w_f)[g // 2]), ps))
                if g < 4:
                    dve.sem_inc(edge_ps_free, 1)
            dve.wait_ge(minmax_stored, 32)
            dve.sem_inc(scratch_free, 1)
            dve.sem_inc(tabs_full, 1)
            dve.wait_ge(l_x, 80)
            chain.restart()
            with dve.Fori(0, NS) as s:
                for i in range(G):
                    last = dve.bn_stats(bn6[:, i, :], flat(x_big[:, ds(s * G + i, 1), :]))
                chain(last)
                for i in range(G):
                    last = dve.bn_aggr(mv[:, i, :], bn6[:, i, :])
                chain(last)
                chain(ts(sd[:, :], mv[:, :, 1], LN_EPS, None, ALU.add))
                root()
                chain(dve.reciprocal(rs[:, :], sd[:, :]))
                for i in range(G):
                    rows_i = flat(x_big[:, ds(s * G + i, 1), :])
                    last = ts(rows_i, rows_i, mv[:, i, 0:1], rs[:, i:i + 1], ALU.subtract, ALU.mult)
                chain(last)
                dve.sem_inc(feat0_full, 1)
                chain.restart()
            dve.wait_ge(minmax_loaded, 32)
            take(dve, tile_iota)
            chain(ts(t_msk, t_max, base_col[:, 0:1], None, ALU.is_ge))
            chain(ts(t_min, t_min, base_col[:, 0:1], float(B), ALU.subtract, ALU.is_lt))
            chain(tt(t_msk, t_msk, t_min, ALU.mult))
            chain(tt(t_val, t_msk, t_iot, ALU.mult))
            chain(dve.tensor_reduce(blk[:, 1:2], t_val, AX.X, ALU.max))
            chain(ts(t_msk, t_msk, -10000.0, 10000.0, ALU.mult, ALU.add))
            chain(tt(t_val, t_val, t_msk, ALU.add))
            chain(dve.tensor_reduce(blk[:, 0:1], t_val, AX.X, ALU.min))
            chain(ts(blk[:, 2:3], blk[:, 0:1], 9000.0, None, ALU.is_lt))
            chain(tt(blk[:, 0:1], blk[:, 0:1], blk[:, 2:3], ALU.mult))
            chain(tt(blk[:, 1:2], blk[:, 1:2], blk[:, 0:1], ALU.subtract))
            chain(ts(t_msk[:, 0:MAXCH], t_iot[:, 0:MAXCH], float(CH), float(CH), ALU.mult, ALU.add))
            chain(ts(t_msk[:, 0:MAXCH], t_msk[:, 0:MAXCH], blk[:, 1:2], None, ALU.is_le))
            chain(dve.tensor_reduce(blk[:, 2:3], t_msk[:, 0:MAXCH], AX.X, ALU.add))
            chain(ts(blk[:, 1:2], blk[:, 2:3], 1.0, None, ALU.add))
            chain(dve.tensor_copy(blk_i[:, 0:2], blk[:, 0:2]))
            dve.sem_inc(blk_full, 1)
            chain.restart()
            dve.sem_inc(xg_clear, 1)
            dve.wait_ge(blk_loaded, 32)
            chain(dve.memset(cum_f[:, :], 0.0))
            chain(dve.tensor_copy(n_f[:, :], n_tab[:, :]))
            chain(dve.tensor_tensor_scan(cum_f[:, 1:NB + 1], ones[0:1, 0:NB], n_f[:, :], 0.0, ALU.mult, ALU.add))
            chain(dve.tensor_copy(cum_tab[:, :], cum_f[:, :]))
            dve.sem_inc(cum_full, 1)
            dve.wait_ge(l_w0, 112)
            dve.sem_inc(w_prep, 1)
            wq4 = wqkvs[:, :, 0:512].rearrange("p c (h n) -> p c h n", h=2)
            chain(dve.tensor_reduce(st4, wq4, AX.X, ALU.add))
            chain(ts(st4, st4, 1.0 / D, None, ALU.mult))
            chain(tt(wq4, wq4, st4.unsqueeze(3).to_broadcast([128, KC, 2, D]), ALU.subtract))
            bq2 = bias0[:, 0:512].rearrange("p (h n) -> p h n", h=2)
            chain(dve.tensor_reduce(st[:, 0, 0:2], bq2, AX.X, ALU.add))
            chain(ts(st[:, 0, 0:2], st[:, 0, 0:2], 1.0 / D, None, ALU.mult))
            chain(tt(bq2, bq2, st[:, 0, 0:2].unsqueeze(2).to_broadcast([B, 2, D]), ALU.subtract))
            take(dve, w_prep_ps)
            for c in range(KC):
                ts(bv_rows[:, c, :], ones[:, :], b1_col[:, c:c + 1], None, ALU.mult)
            chain(dve.tensor_copy(t4f, ps_y[0][:, :]))
            dve.sem_inc(w_prep2, 1)
            take(dve, w_prep_ps)
            sv = wqkvs[:, :, 3 * D:4 * D]
            chain(tt(sv, sv, ps_y[1][:, :].rearrange("p (c n) -> p c n", c=KC), ALU.add))
            chain(tt(b_tmp, b_tmp, ps_t[0][0:B, 0:D], ALU.add))
            chain(tt(bias0[:, 3 * D:], bias0[:, 3 * D:], b_tmp, ALU.add))
            chain.restart()
            chain(dve.memset(st2[:, :], 0.0))
            dve.sem_inc(setup_done, 1)
            dve.sem_inc(xa_used, 1)
            chain.restart()

            def onehots(b, weighted):
                n = dve.value_load(n_tab[0:1, ds(b, 1)], min_val=1, max_val=MAXCH)
                lo = dve.value_load(lo_tab[0:1, ds(b, 1)], min_val=0, max_val=NT - 1)
                chain.restart()
                with dve.Fori(0, n) as c:
                    t0 = nc.s_assert_within(dve.snap(lo + c * CH), 0, NT - 1,
                                            skip_runtime_bounds_check_because="a block's chunks start inside its span")
                    take(dve, oh_free)
                    if weighted:
                        dve.tensor_copy(w_cur[:, :], w_f[:, ds(t0, CH)])
                    chain(ts(dst_cur[:, :], dst_f[:, ds(t0, CH)], base[:, ds(b, 1)], None, ALU.subtract))
                    for s in range(CH):
                        if weighted:
                            last = ts(oh[:, s, :], iota[:, :], dst_cur[:, s:s + 1], w_cur[:, s:s + 1],
                                      ALU.is_equal, ALU.mult)
                        else:
                            last = ts(oh[:, s, :], iota[:, :], dst_cur[:, s:s + 1], None, ALU.is_equal)
                    last.then_inc(oh_full, 1)
                    chain.restart()

            def wide(t):
                return t.unsqueeze(2).to_broadcast([B, G, 8])

            def first_max(src, mask):
                chain(dve.tensor_reduce(st[:, 1, :], src, AX.X, ALU.max))
                chain(tt(mask, src, wide(st[:, 1, :]), ALU.is_ge))
                chain(stt(out=mask, in0=mask, scalar=-8.0, in1=iota[:, 0:8].unsqueeze(1).to_broadcast([B, G, 8]),
                          op0=ALU.mult, op1=ALU.add))
                chain(dve.tensor_reduce(st[:, 2, :], mask, AX.X, ALU.min))
                chain(tt(mask, mask, wide(st[:, 2, :]), ALU.is_equal))

            with dve.Fori(0, NS) as s:
                take(dve, xa_in, 32)
                dve.sem_inc(v_full, 1)
                onehots(s * AA, True)
                for i in range(G):
                    take(dve, h_dve[i % 2])
                    tt(row_b[:, i, 0:512], ps_h[i % 2][0:B, :], bias0[:, 0:512], ALU.add).then_inc(h_free[i % 2], 1)
                    take(dve, y_dve[i % 2])
                    if i == 0:
                        take(dve, rowa_free, 16)
                    tt(f_out[:, i, :], ps_y[i % 2][0:B, 0:D], bias0[:, 2 * D:3 * D], ALU.add)
                    last = tt(row_a[:, i, 0:D], ps_y[i % 2][0:B, D:2 * D], bias0[:, 3 * D:4 * D], ALU.add)
                    if i < G - 1:
                        last.then_inc(y_free[i % 2], 1)
                chain(last)
                dve.sem_inc(y_free[0], 1)
                dve.sem_inc(act_in, 1)
                chain(tt(row_a[:, :, 0:D], row_a[:, :, 0:D], x1, ALU.add))
                take(dve, act_out)
                chain(ts(st[:, 4:6, :], st[:, 0:2, :], 1e-7, None, ALU.add))
                chain(dve.reciprocal(st[:, 6:8, :], st[:, 4:6, :]))
                chain(tt(st[:, 8, :], st[:, 6, :], st[:, 3, :], ALU.mult))
                chain(ts(st[:, 9, :], st[:, 8, :], 1e-12, None, ALU.max))
                chain(dve.reciprocal(st[:, 10, :], st[:, 9, :]))
                chain(tt(st[:, 11, :], st[:, 10, :], st[:, 6, :], ALU.mult))
                for i in range(G):
                    last = ts(ek[:, i, 0:D], row_b[:, i, D:2 * D], st[:, 7, i:i + 1], None, ALU.mult)
                chain(last)
                dve.sem_inc(act_in, 1)
                dve.sem_inc(v_full, 1)
                for i in range(G):
                    last = ts(row_a[:, i, D:2 * D], row_b[:, i, 0:D], st[:, 11, i:i + 1], None, ALU.mult)
                chain(last)
                dve.sem_inc(rowa_full, 1)
                take(dve, ps_full)
                chain(tt(st2[:, 0:2], st2[:, 0:2], ps_t[0][:, 0:2], ALU.add))
                dve.sem_inc(t_free[0], 1)
                take(dve, k4_used)
                dve.sem_inc(xa_used, 1)
                onehots(s * AA + 1, True)
            take(dve, sums_full)
            dve.sem_inc(loop_a_done, 1)
            root()
            chain(ts(st2[:, 0:2], st2[:, 0:2], 1e-12, None, ALU.max))
            chain(dve.reciprocal(st2[:, 0:2], st2[:, 0:2]))
            for c in range(KC):
                last = ts(kvf[:, D * c:D * c + D], ps_kv[:, D * c:D * c + D], st2[:, c:c + 1], 1.0 / math.sqrt(N),
                          ALU.mult, ALU.mult)
            chain(last)
            dve.sem_inc(v_full, 1)
            take(dve, y_dve[0])
            chain(dve.tensor_copy(t4f, ps_y[0][:, :]))
            dve.sem_inc(y_free[0], 1)
            dve.sem_inc(v_full, 1)
            take(dve, y_dve[1])
            chain(dve.tensor_copy(kvo[:, :, :], ps_y[1][:, :].rearrange("p (c n) -> p c n", c=KC)))
            dve.sem_inc(y_free[1], 1)
            take(dve, rowa_free, 16)
            dve.sem_inc(rowa_used, 1)
            dve.wait_ge(l_wh, 64)
            dve.wait_ge(l_l1, 16 * 7)
            big = 12582912.0
            chain(dve.tensor_copy(src_lo, src_i[:, 0:NT]))
            chain(ts(src_hi, src_lo, 1.0 / B, 0.004 - 0.5, ALU.mult, ALU.add))
            chain(ts(src_hi, src_hi, big, -big, ALU.add, ALU.add))
            chain(stt(out=src_lo, in0=src_hi, scalar=-float(B), in1=src_lo, op0=ALU.mult, op1=ALU.add))
            for j in range(2):
                dve.sem_inc(deg_free[j], 1)
            chain.restart()

            def degrees(t0):
                for j in range(2):
                    take(dve, deg_free[j])
                    for o, dig, n in ((oh_lo[j], src_lo, B), (oh_hi[j], src_hi, NB)):
                        last = tt(o, iota[:, 0:n].unsqueeze(1).to_broadcast([B, DT, n]),
                                  dig[:, ds(t0 + j * DT, DT)].unsqueeze(2).to_broadcast([B, DT, n]), ALU.is_equal)
                    last.then_inc(deg_full[j], 1)

            def positions(s, masks):
                take(dve, ps_full)
                pr = ps_t[0][0:B, 0:E0 * G].rearrange("p (i e) -> p i e", i=G)
                chain(tt(lg[:, :, :], pr, cnt[:, :].unsqueeze(1).to_broadcast([B, G, E0]), ALU.add))
                chain(tt(cnt[:, :], cnt[:, :], ps_t[0][0:B, E0 * G:E0 * G + E0], ALU.add))
                dve.sem_inc(t_free[0], 1)
                for k, mask in enumerate(masks):
                    chain(tt(mask, mask, lg[:, :, :], ALU.mult))
                    chain(dve.tensor_reduce(st[:, 4 + k, :], mask, AX.X, ALU.add))
                    chain(dve.tensor_copy(pos_cur[:, k, :], st[:, 4 + k, :]))
                n = len(masks)
                chain(dve.tensor_copy(pos_f[:, 0:n, ds(s * G, G)], st[:, 4:4 + n, :]))
                dve.sem_inc(pos_full, 1)

            def routes(n):
                chain(dve.tensor_copy(tail_tab[:, :], cnt[0:1, :]))
                chain(tt(count[:, :], cnt[:, :], region[:, :], ALU.subtract))
                chain(ts(count[:, :], count[:, :], -1.0, None, ALU.add))
                chain(tt(pair_msk[:, :, :], count[:, :].unsqueeze(2).to_broadcast([B, E0, MAXP]),
                         pair_at[:, :].unsqueeze(1).to_broadcast([B, E0, MAXP]), ALU.is_ge))
                chain(dve.tensor_reduce(pairs_f[:, :], pair_msk[:, :, :], AX.X, ALU.add))
                chain(ts(pairs_f[:, :], pairs_f[:, :], 1.0, None, ALU.max))
                chain(dve.tensor_copy(pair_tab[:, :], pairs_f[0:1, :]))
                chain(dve.memset(before_f[:, :], 0.0))
                chain(dve.tensor_tensor_scan(before_f[:, 1:E0 + 1], ones[0:B, 0:E0], pairs_f[:, :], 0.0,
                                             ALU.mult, ALU.add))
                chain(dve.tensor_copy(before_tab[:, :], before_f[0:1, 0:E0]))
                chain(dve.tensor_copy(cnt[:, :], region[:, :]))
                dve.sem_inc(routes_full, 1)
                chain(ts(shift[:, 1:E0], pairs_f[:, 0:E0 - 1], float(PT), -float(CAP), ALU.mult, ALU.add))
                for e in range(1, E0):
                    chain(ts(pos_up[:, 0:n, :], pos_f[:, 0:n, :], region[:, e:e + 1], None, ALU.is_ge))
                    chain(ts(pos_up[:, 0:n, :], pos_up[:, 0:n, :], shift[:, e:e + 1], None, ALU.mult))
                    if e == 1:
                        chain(tt(pos_out[:, 0:n, :], pos_f[:, 0:n, :], pos_up[:, 0:n, :], ALU.add))
                    else:
                        chain(tt(pos_out[:, 0:n, :], pos_out[:, 0:n, :], pos_up[:, 0:n, :], ALU.add))
                chain(dve.tensor_copy(pos_tab[:, 0:n, :], pos_out[:, 0:n, :]))

            def experts(layer):
                for e in range(E0):
                    trips = dve.value_load(pair_tab[0:1, e:e + 1], min_val=1, max_val=MAXP)
                    dve.wait_ge(w_full[e % 2], loads(layer, e))
                    chain.restart()
                    with dve.Fori(0, trips):
                        take(dve, yout_free, 16)
                        for i in range(2):
                            take(dve, y_dve[i])
                            last = tt(y_out[:, i, :], ps_y[i][0:B, 0:D], be[:, e % 2, :], ALU.add)
                            if i == 0:
                                last.then_inc(y_free[0], 1)
                        chain(last)
                        dve.sem_inc(y_free[1], 1)
                        dve.sem_inc(yout_full, 1)
                        chain.restart()
                    dve.sem_inc(w_free[e % 2], 1)
                take(dve, yout_free, 16)
                dve.sem_inc(yout_free, 16)
                dve.sem_inc(sorted_done, 1)
                dve.sem_inc(got_used[0], 1)
                dve.sem_inc(rowx_used, 1)

            def layer0(s, more):
                def hots(i):
                    if 0 < i < more or i == AB == more:
                        onehots(s * AB + AA * NS + i, True)

                def degs(i):
                    if more:
                        degrees(s * (10 * DT) + i * (2 * DT))

                degs(0)
                take(dve, rowa_in, 32)
                dve.sem_inc(v_full, 1)
                take(dve, rowx_free, 16)
                each(lambda i: tt(x1[:, i, :], ps_y[i % 2][0:B, 0:D], row_a[:, i, 0:D], ALU.add), y_dve, y_free)
                dve.sem_inc(rowx_full, 1)
                if not isinstance(s, int) or s < NS - 1:
                    dve.sem_inc(rowa_used, 1)
                hots(1)
                degs(1)
                landed = s * (16 * G) + 16
                dve.wait_ge(scattered, landed if isinstance(s, int) else dve.snap(landed))
                dve.tensor_copy(p_cur[:, 0:1], ones[0:B, 0:1])
                norm(y, x1)
                dve.sem_inc(v_full, 1)
                hots(2)
                degs(2)
                hots(3)
                take(dve, ps_full)
                pg = ps_t[0][0:B, 0:8 * G].rearrange("p (i e) -> p i e", i=G)
                chain(tt(lg[:, :, :], pg, bg_bc[:, :].unsqueeze(1).to_broadcast([B, G, 8]), ALU.add))
                dve.sem_inc(t_free[0], 1)
                chain(dve.tensor_reduce(st[:, 1, :], lg[:, :, :], AX.X, ALU.max))
                chain(tt(lt[:, :, :], lg[:, :, :], wide(st[:, 1, :]), ALU.subtract))
                dve.sem_inc(act_in, 1)
                take(dve, act_out)
                chain(dve.tensor_reduce(st[:, 0, :], lt[:, :, :], AX.X, ALU.add))
                chain(dve.reciprocal(st[:, 3, :], st[:, 0, :]))
                chain(tt(lt[:, :, :], lt[:, :, :], wide(st[:, 3, :]), ALU.mult))
                first_max(lt[:, :, :], gate[:, :, :])
                dve.sem_inc(v_full, 1)
                chain(tt(lu[:, :, :], lt[:, :, :], gate[:, :, :], ALU.mult))
                chain(dve.tensor_reduce(st[:, 0, :], lu[:, :, :], AX.X, ALU.add))
                chain(dve.tensor_copy(p_tab[:, ds(s * G, G)], st[:, 0, :]))
                chain(dve.tensor_copy(lu[:, :, :], gate[:, :, :]))
                degs(3)
                positions(s, (lu[:, :, :],))
                degs(4)
                hots(4)
                chain.restart()

            def result0(s):
                landed = (s + 1) * (16 * G)
                if not isinstance(s, int):
                    landed = dve.snap(landed)
                take(dve, rowx_in, 16)
                take(dve, rowb_free, 16)
                chain(dve.tensor_copy(p_cur[:, :], p_tab[:, ds(s * G, G)]))
                dve.wait_ge(got[0], landed)
                for i in range(G):
                    last = stt(out=row_b[:, i, 0:D], in0=y[:, i, :], scalar=p_cur[:, i:i + 1], in1=x1[:, i, :],
                               op0=ALU.mult, op1=ALU.add)
                chain(last)
                dve.sem_inc(got_used[0], 1)
                dve.sem_inc(rowx_used, 1)
                norm_sums(row_b[:, :, 0:D])

            def norm0():
                norm_rows(row_b[:, :, D:2 * D], row_b[:, :, 0:D])
                dve.sem_inc(v_full, 1)
                dve.sem_inc(rowb_full, 1)

            def messages1(s):
                take(dve, fout_ok)
                iv = inv_out[:, ds(s * G, G)].unsqueeze(2).to_broadcast([B, G, D])
                chain(tt(f_out, row_b[:, :, D:2 * D], iv, ALU.mult))
                dve.sem_inc(fout_full, 1)

            def project1(s, more):
                take(dve, k4_used)
                dve.memset(v1[:, :, :, 128:129], 1.0)
                for i in range(G):
                    take(dve, h_dve[i % 2])
                    tt(row_a[:, i, :], ps_h[i % 2][0:B, :], bias1[:, 0:512], ALU.add).then_inc(h_free[i % 2], 1)
                    take(dve, y_dve[i % 2])
                    last = tt(v1[:, i, :, 0:128], ps_y[i % 2][0:B, 0:D].rearrange("p (c n) -> p c n", c=2),
                              bias1[:, 2 * D:3 * D].rearrange("p (c n) -> p c n", c=2), ALU.add)
                    if i < G - 1:
                        last.then_inc(y_free[i % 2], 1)
                chain(last)
                dve.sem_inc(y_free[0], 1)
                for n in (1, 0):
                    chain(ts(ek[:, :, D * n:D * n + D], row_a[:, :, D * n:D * n + D], 0.0, None, ALU.min))
                    dve.sem_inc(act_in2[n], 1)
                if more:
                    result0(s + 1)
                take(dve, act_out2[1])
                chain(stt(out=ek[:, :, D:2 * D], in0=row_a[:, :, D:2 * D], scalar=0.0, in1=ek[:, :, D:2 * D],
                          op0=ALU.max, op1=ALU.add))
                dve.sem_inc(phi_full, 1)
                if more:
                    norm0()
                take(dve, q_free, 16)
                take(dve, act_out2[0])
                chain(stt(out=row_b[:, :, 2 * D:3 * D], in0=row_a[:, :, 0:D], scalar=0.0, in1=ek[:, :, 0:D],
                          op0=ALU.max, op1=ALU.add))
                dve.sem_inc(q_full, 1)
                if more:
                    messages1(s + 1)
                chain.restart()

            onehots(AA * NS, True)
            with dve.Fori(0, NS - 2) as s:
                layer0(s, AB)
            layer0(NS - 2, AB - 1)
            layer0(NS - 1, 0)
            take(dve, deg_ps_full)
            chain(ts(inv_out[:, :], ps_kv[0:B, 0:NB], 1.0, None, ALU.max))
            root()
            chain(dve.reciprocal(inv_out[:, :], inv_out[:, :]))
            routes(1)
            experts(0)
            dve.sem_inc(k4_used, 1)
            result0(0)
            norm0()
            messages1(0)
            chain.restart()
            with dve.Fori(0, NS - 1) as s:
                project1(s, True)
            project1(NS - 1, False)
            take(dve, k4_used)
            take(dve, q_free, 16)
            take(dve, got_used[0])
            take(dve, rowx_used)
            take(dve, sums_full)
            take(dve, rowb_free, 16)
            take(dve, fout_ok)
            dve.sem_inc(loop_b_done, 1)
            dve.sem_inc(rowb_used, 1)
            dve.sem_inc(fout_free, 16)
            chain(dve.memset(kvd[:, :, :], 0.0))
            for h in range(4):
                p = slice(DH * h, DH * h + DH)
                kv = ps_kv[p, 0:258].rearrange("p (c n) -> p c n", c=KC)
                dve.tensor_copy(kvd[p, :, DH * h:DH * h + DH], kv[:, :, DH * h:DH * h + DH])
                last = dve.tensor_copy(kvd[p, :, 128 + h:129 + h], kv[:, :, 128:129])
            chain(last)
            chain.restart()

            dve.wait_ge(l_c, 16 * 7)
            dve.wait_ge(l_bc, 16 * 7)

            def mixer(b, stages):
                def hots(i):
                    if i in stages[1:]:
                        onehots(b + stages.index(i), False)
                    elif i == stages[-1] + 1:
                        onehots(b + len(stages), False)

                take(dve, rowb_in, 16)
                dve.sem_inc(v_full, 1)
                for i in range(G):
                    take(dve, h_dve[i % 2])
                    num = ps_h[i % 2][0:B, 0:264].rearrange("p (c n) -> p c n", c=KC)
                    chain(ts(lt[:, i, :].rearrange("p (c h) -> p c h", c=KC), num[:, :, 128:132], 1e-6, None, ALU.add))
                    chain(dve.reciprocal(lt[:, i, :], lt[:, i, :]))
                    for c in range(KC):
                        last = tt(y[:, i, 128 * c:128 * c + 128].rearrange("p (h n) -> p h n", h=4),
                                  num[:, c, 0:128].rearrange("p (h n) -> p h n", h=4),
                                  lt[:, i, 4 * c:4 * c + 4].unsqueeze(2).to_broadcast([B, 4, DH]), ALU.mult)
                    if i < G - 1:
                        last.then_inc(h_free[i % 2], 1)
                chain(last)
                dve.sem_inc(h_free[0], 1)
                dve.sem_inc(v_full, 1)
                hots(1)
                take(dve, rowx_free, 16)
                each(lambda i: tt(x1[:, i, :], ps_y[i % 2][0:B, 0:D], row_b[:, i, D:2 * D], ALU.add), y_dve, y_free)
                chain(tt(x1, x1, across(bc[:, 1, :]), ALU.add))
                hots(2)
                norm(x1, x1, bc[:, 3, :], bc[:, 4, :])
                dve.sem_inc(v_full, 1)
                hots(3)
                each(lambda i: tt(y[:, i, :], ps_y[i % 2][0:B, 0:D], x1[:, i, :], ALU.add), y_dve, y_free)
                chain(tt(y, y, across(bc[:, 2, :]), ALU.add))
                hots(4)
                norm(y, y, bc[:, 5, :], bc[:, 6, :])
                chain(tt(x1, y, row_b[:, :, 0:D], ALU.add))
                dve.sem_inc(rowx_full, 1)
                dve.sem_inc(rowb_used, 1)
                hots(5)
                chain.restart()

            def graph(s, b, n):
                take(dve, aggs_in, 32)
                chain(ts(sd[:, :], agg_s[:, :, D], 1.0, None, ALU.max))
                root()
                chain(dve.reciprocal(rs[:, :], sd[:, :]))
                for i in range(G):
                    last = ts(agg_s[:, i, 0:D], agg_s[:, i, 0:D], rs[:, i:i + 1], None, ALU.mult)
                chain(last)
                dve.sem_inc(v_full, 1)
                each(lambda i: tt(row_a[:, i, 0:D], ps_y[i % 2][0:B, 0:D], bc[:, 0, :], ALU.add), y_dve, y_free)
                landed = s * (32 * G) + 16 * (NB + 1)
                dve.wait_ge(scattered, landed if isinstance(s, int) else dve.snap(landed))
                chain(ts(row_a[:, :, D:2 * D], row_a[:, :, 0:D], 0.0, None, ALU.min))
                dve.sem_inc(act_in, 1)
                if n > 1:
                    onehots(b + 1, False)
                take(dve, act_out)
                chain(stt(out=row_a[:, :, 0:D], in0=row_a[:, :, 0:D], scalar=0.0, in1=row_a[:, :, D:2 * D],
                          op0=ALU.max, op1=ALU.add))
                chain(stt(out=f_out, in0=row_a[:, :, 0:D], scalar=-1.0, in1=f_out, op0=ALU.add, op1=ALU.add))
                dve.sem_inc(fout_full, 1)
                norm(row_a[:, :, D:2 * D], f_out)
                dve.sem_inc(v_full, 1)
                dve.sem_inc(rowx_used, 1)
                if n > 2:
                    onehots(b + 2, False)
                take(dve, ps_full)
                pg = ps_t[0][0:B, 0:8 * G].rearrange("p (i e) -> p i e", i=G)
                chain(tt(lg[:, :, :], pg, bg_bc[:, :].unsqueeze(1).to_broadcast([B, G, 8]), ALU.add))
                dve.sem_inc(t_free[0], 1)
                first_max(lg[:, :, :], lt[:, :, :])
                chain(stt(out=lg[:, :, :], in0=lt[:, :, :], scalar=-3.0e38, in1=lg[:, :, :], op0=ALU.mult, op1=ALU.add))
                first_max(lg[:, :, :], lu[:, :, :])
                chain(tt(gate[:, :, :], lt[:, :, :], lu[:, :, :], ALU.add))
                dve.sem_inc(v_full, 1)
                positions(s, (lt[:, :, :], lu[:, :, :]))
                if n and not isinstance(b, int):
                    onehots(b + n, False)
                chain.restart()

            onehots(0, False)
            dve.sem_inc(rowx_used, 1)
            with dve.Fori(0, 2) as s:
                mixer(s * len(FOUR), FOUR)
            with dve.Fori(0, NS - 2) as p:
                mixer(p * AP + AC, TWO)
                graph(p, p * AP + (AC + len(TWO)), AG)
            graph(NS - 2, NB - AR, AR)
            graph(NS - 1, NB, 0)
            take(dve, rowx_used)
            routes(2)
            experts(1)
            dve.sem_inc(got_used[1], 1)

            def sum_step(p, j, first, last):
                resid, one, two, o = sums[j]
                take(dve, sum_in[j], 16)
                if not first:
                    take(dve, sum_free[j], 16)
                landed = (p + 1) * (32 * G) + (16 * NB if j == 0 else 0)
                dve.wait_ge(got[j], landed if isinstance(p, int) else dve.snap(landed))
                chain(tt(o, resid, one, ALU.add))
                chain(tt(o, o, two, ALU.add))
                dve.sem_inc(sum_full[j], 1)
                if not last:
                    dve.sem_inc(got_used[j], 1)
                chain.restart()

            for j in range(2):
                sum_step(0, j, True, False)
            with dve.Fori(1, NS // 2) as p:
                for j in range(2):
                    sum_step(p, j, False, False)
            sum_step(NS // 2, 0, False, True)


_NAMES = """x src dst edge_weight L0_gnn_W_self L0_gnn_W_neighbor L0_gnn_bias L0_mix_W_qkv L0_mix_b_qkv
L0_mix_W_out L0_mix_b_out L0_ffn_W1 L0_ffn_b1 L0_ffn_Wg L0_ffn_bg L0_ffn_Wd L0_ffn_bd L1_gnn_weight
L1_gnn_bias L1_mix_Wq L1_mix_bq L1_mix_Wk L1_mix_bk L1_mix_Wv L1_mix_bv L1_mix_Wo L1_mix_bo L1_mix_W1
L1_mix_b1 L1_mix_W2 L1_mix_b2 L1_mix_ln1_g L1_mix_ln1_b L1_mix_ln2_g L1_mix_ln2_b L1_ffn_Wg L1_ffn_bg
L1_ffn_W1 L1_ffn_b1 L1_ffn_W2 L1_ffn_b2""".split()


def kernel(**inputs):
    import numpy as np
    import concourse.bacc as bacc
    from concourse.bass_utils import run_bass_kernel_spmd

    nc = bacc.Bacc("TRN2", target_bir_lowering=False, num_devices=1)
    arrays, aps = {}, {}
    for name in _NAMES:
        v = np.ascontiguousarray(inputs[name])
        arrays["in_" + name] = v
        aps[name] = nc.dram_tensor("in_" + name, v.shape, mybir.dt.from_np(v.dtype), kind="ExternalInput").ap()
    out = nc.dram_tensor("out_rows", (N, D), F32, kind="ExternalOutput").ap()
    program(nc, aps, out)
    r = run_bass_kernel_spmd(nc, [arrays], core_ids=[0])
    return r.results[0]["out_rows"]
```
